# Optimizing a Trainium2 kernel written in Bass

```python
import numpy as np
import jax
import jax.numpy as jnp

def _softmax(x, axis=-1):
    return jax.nn.softmax(x, axis=axis)

def _gelu(x):
    return jax.nn.gelu(x, approximate=True)

def _silu(x):
    return jax.nn.silu(x)

def _sigmoid(x):
    return jax.nn.sigmoid(x)

def _layernorm(x, axis=-1, eps=1e-05):
    m = jnp.mean(x, axis=axis, keepdims=True)
    v = jnp.var(x, axis=axis, keepdims=True)
    return (x - m) / jnp.sqrt(v + eps)

def _scatter_add(tgt, idx, src, axis=0):
    return tgt.at[idx].add(src)

def _segment_sum(src, seg, n):
    return jax.ops.segment_sum(src, seg, n)
kernel_name = 'mk_xattn_ffn_d1_seqx_r4_2a9f97'

def setup_inputs(seed: int=0):
    np.random.seed(seed)
    _w = jnp.asarray

    def _rec_inputs():
        import jax
        import jax.numpy as jnp
        _rk = jax.random.key(seed)
        x = 0.5 + 0.2887 * jax.random.normal(jax.random.fold_in(_rk, 1), (4, 512, 512), jnp.float32)
        _lenS = 512 - jax.random.randint(jax.random.fold_in(_rk, 7), (4,), 0, max(1, 512 // 4) + 1, jnp.int32)
        _lenS2 = 512 - jax.random.randint(jax.random.fold_in(_rk, 8), (4,), 0, max(1, 512 // 4) + 1, jnp.int32)
        _ctx_512P = jax.random.normal(jax.random.fold_in(_rk, 11), (4, 16, 128), jnp.float32)
        _ctx_512c = jax.random.dirichlet(jax.random.fold_in(_rk, 511), 0.3 * jnp.ones((16,), jnp.float32), (4, 512))
        _ctx_512t = jnp.einsum('bsk,bkd->bsd', _ctx_512c, _ctx_512P)
        _ctx_512t = _ctx_512t * jax.lax.rsqrt(jnp.mean(jnp.square(_ctx_512t)) + 1e-12) * 0.953939
        ctx_512 = -0.000392918 + 0.999932 * (_ctx_512t + 0.3 * jax.random.normal(jax.random.fold_in(_rk, 611), (4, 512, 128), jnp.float32))
        return (x, ctx_512)
    x, ctx_512 = _rec_inputs()

    def _L0_xattn_setup():
        import jax, jax.numpy as jnp
        import numpy as np
        B, N, D = (16, 512, 128)
        H = 4
        TOP_K_RATIO = 0.3
        key = jax.random.key(seed)
        k1, k2, k3, k4 = jax.random.split(key, 4)
        h = jax.random.normal(k1, (B, N, D), dtype=jnp.float32)
        adj_raw = jax.random.uniform(k2, (B, N, N), dtype=jnp.float32)
        lim = 1.0 / np.sqrt(D)
        Wq = jax.random.uniform(k3, (D, D), minval=-lim, maxval=lim, dtype=jnp.float32)
        Wk = jax.random.uniform(k4, (D, D), minval=-lim, maxval=lim, dtype=jnp.float32)
        gamma_raw = jnp.float32(-0.85)
        return {'h': h, 'adj_raw': adj_raw, 'Wq': Wq, 'Wk': Wk, 'gamma_raw': gamma_raw}
    _L0_xattn_all = _L0_xattn_setup()
    _L0_xattn_in = {k: v for k, v in _L0_xattn_all.items() if k in ('Wq', 'Wk', 'gamma_raw')}
    del _L0_xattn_all

    def _L0_ffn_setup():
        import jax, jax.numpy as jnp
        import numpy as np
        B, S, H, I, E, TOP_K, NS = (2, 512, 512, 352, 8, 2, 2)
        SI = I * NS
        INIT = 0.02
        key = jax.random.key(seed)
        ks = jax.random.split(key, 9)
        f32 = jnp.float32
        return {'hidden_states': jax.random.normal(ks[0], (B, S, H), f32), 'router_w': jax.random.normal(ks[1], (E, H), f32) * INIT, 'gate_w': jax.random.normal(ks[2], (E, H, I), f32) * INIT, 'up_w': jax.random.normal(ks[3], (E, H, I), f32) * INIT, 'down_w': jax.random.normal(ks[4], (E, I, H), f32) * INIT, 's_gate_w': jax.random.normal(ks[5], (H, SI), f32) * INIT, 's_gate_b': jnp.zeros((SI,), f32), 's_up_w': jax.random.normal(ks[6], (H, SI), f32) * INIT, 's_up_b': jnp.zeros((SI,), f32), 's_down_w': jax.random.normal(ks[7], (SI, H), f32) * INIT, 's_down_b': jnp.zeros((H,), f32)}
    _L0_ffn_all = _L0_ffn_setup()
    _L0_ffn_in = {k: v for k, v in _L0_ffn_all.items() if k in ('router_w', 'gate_w', 'up_w', 'down_w', 's_gate_w', 's_gate_b', 's_up_w', 's_up_b', 's_down_w', 's_down_b')}
    del _L0_ffn_all
    return {'x': x, 'ctx_512': ctx_512, 'L0_xattn_Wq': _L0_xattn_in['Wq'], 'L0_xattn_Wk': _L0_xattn_in['Wk'], 'L0_xattn_gamma_raw': _L0_xattn_in['gamma_raw'], 'L0_ffn_router_w': _L0_ffn_in['router_w'], 'L0_ffn_gate_w': _L0_ffn_in['gate_w'], 'L0_ffn_up_w': _L0_ffn_in['up_w'], 'L0_ffn_down_w': _L0_ffn_in['down_w'], 'L0_ffn_s_gate_w': _L0_ffn_in['s_gate_w'], 'L0_ffn_s_gate_b': _L0_ffn_in['s_gate_b'], 'L0_ffn_s_up_w': _L0_ffn_in['s_up_w'], 'L0_ffn_s_up_b': _L0_ffn_in['s_up_b'], 'L0_ffn_s_down_w': _L0_ffn_in['s_down_w'], 'L0_ffn_s_down_b': _L0_ffn_in['s_down_b']}

def reference(x, ctx_512, L0_xattn_Wq, L0_xattn_Wk, L0_xattn_gamma_raw, L0_ffn_router_w, L0_ffn_gate_w, L0_ffn_up_w, L0_ffn_down_w, L0_ffn_s_gate_w, L0_ffn_s_gate_b, L0_ffn_s_up_w, L0_ffn_s_up_b, L0_ffn_s_down_w, L0_ffn_s_down_b):
    import jax
    import jax.numpy as jnp

    def _L0_xattn_ref(h, adj_raw, Wq, Wk, gamma_raw):
        import jax, jax.numpy as jnp
        import numpy as np
        B, N, D = (16, 512, 128)
        H = 4
        TOP_K_RATIO = 0.3
        b, n, dm = h.shape
        d = dm // H
        Q = (h @ Wq.T).reshape(b, n, H, d).transpose(0, 2, 1, 3)
        K = (h @ Wk.T).reshape(b, n, H, d).transpose(0, 2, 1, 3)
        sim = jnp.einsum('bhnd,bhmd->bnm', Q, K) / (jnp.sqrt(jnp.float32(d)) * H)
        k = max(1, int(n * TOP_K_RATIO))
        topk_vals = jax.lax.top_k(sim, k)[0]
        threshold = topk_vals[:, :, -1:]
        sparse_mask = (sim >= threshold).astype(sim.dtype)
        A_learned = jax.nn.sigmoid(sim) * sparse_mask
        A_learned = (A_learned + jnp.swapaxes(A_learned, -1, -2)) * 0.5
        gamma = jax.nn.sigmoid(gamma_raw)
        return (1.0 - gamma) * adj_raw + gamma * A_learned

    def _L0_ffn_ref(hidden_states, router_w, gate_w, up_w, down_w, s_gate_w, s_gate_b, s_up_w, s_up_b, s_down_w, s_down_b):
        import jax, jax.numpy as jnp
        import numpy as np
        B, S, H, I, E, TOP_K, NS = (2, 512, 512, 352, 8, 2, 2)
        SI = I * NS
        INIT = 0.02
        b, s, h = hidden_states.shape
        x = hidden_states.reshape(-1, h)
        T = x.shape[0]
        num_experts = router_w.shape[0]
        logits = x @ router_w.T
        probs = jax.nn.softmax(logits.astype(jnp.float32), axis=-1)
        topk_w, topk_idx = jax.lax.top_k(probs, TOP_K)
        topk_w = topk_w / jnp.sum(topk_w, axis=-1, keepdims=True)
        combine = jnp.zeros((T, num_experts), probs.dtype)
        combine = combine.at[jnp.arange(T)[:, None], topk_idx].add(topk_w)

        def expert_step(acc, ws):
            gw, uw, dw, ce = ws
            out = jax.nn.silu(x @ gw) * (x @ uw) @ dw
            return (acc + ce[:, None].astype(out.dtype) * out, None)
        moe_out, _ = jax.lax.scan(expert_step, jnp.zeros_like(x), (gate_w, up_w, down_w, combine.T))
        shared = jax.nn.silu(x @ s_gate_w + s_gate_b) * (x @ s_up_w + s_up_b) @ s_down_w + s_down_b
        return (moe_out + shared).reshape(b, s, h)
    x = x + _L0_xattn_ref(ctx_512, _layernorm(x, axis=-1), L0_xattn_Wq, L0_xattn_Wk, L0_xattn_gamma_raw)
    x = x + _L0_ffn_ref(_layernorm(x, axis=-1), L0_ffn_router_w, L0_ffn_gate_w, L0_ffn_up_w, L0_ffn_down_w, L0_ffn_s_gate_w, L0_ffn_s_gate_b, L0_ffn_s_up_w, L0_ffn_s_up_b, L0_ffn_s_down_w, L0_ffn_s_down_b)
    return x

_drawn_inputs = setup_inputs


def setup_inputs(seed=0):
    import zlib

    import numpy as np

    out = dict(_drawn_inputs(seed))
    spreads = {'L0_ffn_s_gate_b': (0.0, 0.681),
     'L0_ffn_s_up_b': (0.0, 0.681),
     'L0_ffn_s_down_b': (0.0, 0.1)}
    factors = {}
    for name, (base, spread) in spreads.items():
        noise = np.random.default_rng([zlib.crc32(name.encode()), seed]).standard_normal(out[name].shape)
        drawn = base * np.exp(spread * noise) if base else spread * noise
        out[name] = jnp.asarray(drawn.astype(out[name].dtype))
    for name, factor in factors.items():
        out[name] = (out[name] * factor).astype(out[name].dtype)
    return out
```

```python
from contextlib import ExitStack

import concourse.bass as bass
from concourse import mybir

F32 = mybir.dt.float32
F16 = mybir.dt.float16
I32 = mybir.dt.int32
U32 = mybir.dt.uint32
ALU = mybir.AluOpType
ACT = mybir.ActivationFunctionType
AX = mybir.AxisListType

P = 128
NB, S, D = 4, 512, 512
TB = S // P
NT = NB * TB
T = NB * S
C = 128
KD = D // P
E, TOPK = 8, 2
I = 352
SI = 704
HEADS = 4
EPS = 1e-5

KTH = int(S * 0.3)
WIN = 8
PROBES = 5
START_Z, SPAN_Z = 0.507, 2.0

XS, WS, HS = 256.0, 64.0, 4.0
XW = XS * WS
HW = HS * WS

DOWN_ROWS = [0, 128, I - P]
DOWN_ZERO = [0, 0, 2 * P - (I - P)]
SH_ROWS = [0, 128, 256, 384, 512, SI - P]
SH_ZERO = [0, 0, 0, 0, 0, 5 * P - (SI - P)]
DC, SC = len(DOWN_ROWS), len(SH_ROWS)

GU = 2 * I
GU_HI, GU_LO = 0, KD * GU
DN_HI, DN_LO = 2 * KD * GU, 2 * KD * GU + DC * D
EW = DN_LO + DC * D
SH = (E - 2) * EW
SG_HI, SG_LO = SH, SH + KD * 2 * SI
SD_HI, SD_LO = SH + 2 * KD * 2 * SI, SH + 2 * KD * 2 * SI + SC * D

BLOCKS = T * TOPK // P + E - 1
HEAD_BLOCKS = 3
DUMMY = T


def weight_units():
    units = []
    for c in range(KD):
        for n, w in enumerate(("s_gate", "s_up")):
            units.append(([(w, None, c * P, SI)], SG_HI + (2 * c + n) * SI, SG_LO + (2 * c + n) * SI, SI, 0))
    for q in range(SC):
        units.append(([("s_down", None, SH_ROWS[q], D)], SD_HI + q * D, SD_LO + q * D, D, SH_ZERO[q]))
    for e in range(E):
        b = e * EW
        for c in range(KD):
            units.append(([("gate", e, c * P, I), ("up", e, c * P, I)], b + GU_HI + c * GU, b + GU_LO + c * GU, GU, 0))
        for q in range(DC):
            units.append(([("down", e, DOWN_ROWS[q], D)], b + DN_HI + q * D, b + DN_LO + q * D, D, DOWN_ZERO[q]))
    return units


UNITS = weight_units()
SHARED_UNITS = 2 * KD + SC
PER_EXPERT = KD + DC
LATE = SHARED_UNITS + (E - 2) * PER_EXPERT
UNITS_AT = [SHARED_UNITS, 0, 14, 14, 14]


def stage_counts():
    at, out = [0, 0], []
    for n, (src, *_) in enumerate(UNITS):
        at[n % 2] += 16 * len(src)
        out.append(at[n % 2])
    return out


STAGED = stage_counts()


def build(nc, x, ctx_in, wq, wk, gamma, router, gate, up, down, s_gate, s_gate_b, s_up, s_up_b, s_down, s_down_b,
          out, xn_dram):
    es = ExitStack()

    def sb(name, shape, dt=F32):
        return es.enter_context(nc.sbuf_tensor(name, shape, dt))

    def sem(name):
        return es.enter_context(nc.semaphore(name))

    dram = {"gate": gate, "up": up, "down": down, "s_gate": s_gate, "s_up": s_up, "s_down": s_down}

    W = sb("W", [P, E * EW], F16)
    sim = sb("sim", [P, TB, S])
    sigA = sb("sigA", [P, 2, S])
    qT = sb("qT", [P, S])
    kT = sb("kT", [P, S])
    xb = sb("xb", [P, TB, D])
    xn = sb("xn", [P, 2, D])
    ysh = sb("ysh", [P, 2, D])
    xT = sb("xT", [P, 2, KD, S], F16)
    hS = sb("hS", [P, 2, SC, S], F16)
    sgt = sb("sgt", [P, 2, S])
    stage = sb("stage", [P, 2, SI])
    below = sb("below", [P, S])
    sdb = sb("sdb", [P, 2, D], F16)
    ident = sb("ident", [P, P])
    row0 = sb("row0", [P, P], F16)
    wqT = sb("wqT", [P, C])
    wkT = sb("wkT", [P, C])
    rwT = sb("rwT", [P, 2, KD, E], F16)
    bias = sb("bias", [P, 2, SC])
    biasS = sb("biasS", [P, 2, SC])
    gam = sb("gam", [P, 4])
    stats = sb("stats", [P, TB, 6])
    mv = sb("mv", [P, TB, 2])
    rstd = sb("rstd", [P, TB])
    pw = sb("pw", [P, 2, TB])
    aff = sb("aff", [P, 2, TB])
    probe = sb("probe", [P, 2, TB])
    lo_ = sb("lo_", [P, 2, TB])
    hi_ = sb("hi_", [P, 2, TB])
    dif = sb("dif", [P, 2, TB])
    msk = sb("msk", [P, 2, TB])
    bad = sb("bad", [P, 4])
    badi = sb("badi", [P, 1], I32)
    top = sb("top", [P, TB, 8])
    pick = sb("pick", [P, TB, 8])
    thr = sb("thr", [P, TB])
    rank8 = sb("rank8", [P, 8])
    lg = sb("lg", [P, NT, E])
    mx = sb("mx", [P, NT, 8])
    mxi = sb("mxi", [P, NT, 8], U32)

    simf = sim[:, :, :].rearrange("p a b -> p (a b)")
    oneh = simf[:, 0:512].rearrange("p (a b) -> p a b", a=4)
    valh = simf[:, 512:512 + 4 * 2 * BLOCKS].rearrange("p (a k b) -> p a k b", a=4, k=2)
    xg = simf[:, 1024:2048].rearrange("p (a b) -> p a b", a=2)
    y2 = xb[:, 0:2, :]
    h2 = xb[:, 2:4, 0:I]
    sg2 = sgt[:, :, 0:I]
    xT2 = xT[:, :, :, 0:2 * P].rearrange("p s c (a t) -> p s c a t", a=2)
    hT2 = hS[:, :, 0:DC, 0:2 * P].rearrange("p s c (a t) -> p s c a t", a=2)
    rt = sigA[:, :, :].rearrange("p a b -> p (a b)")

    def rv(at, n):
        return rt[:, at:at + n]

    iota = rv(0, P)
    io8 = rv(128, 8)
    tok1 = rv(136, NT)
    ef = rv(152, 2 * NT).rearrange("p (k g) -> p k g", k=2)
    wt = rv(184, 2 * NT).rearrange("p (k g) -> p k g", k=2)
    sel = rv(216, 2 * NT * E).rearrange("p (k g e) -> p k g e", k=2, g=NT)
    slotr = rv(472, NT * E).rearrange("p (g e) -> p g e", g=NT)
    prod = below[:, 0:2 * NT * E].rearrange("p (k g e) -> p k g e", k=2, g=NT)
    pos = rv(600, 2 * NT).rearrange("p (k g) -> p k g", k=2)
    posi = rv(632, 2 * NT).bitcast(I32)
    lowi = rv(664, 2 * NT).bitcast(I32)
    higi = rv(696, 2 * NT).bitcast(I32)
    lowf = rv(728, 2 * NT).rearrange("p (k g) -> p k g", k=2)
    higf = rv(760, 2 * NT).rearrange("p (k g) -> p k g", k=2)
    cnt = rv(792, E)
    nblk = rv(800, E)
    ends = rv(808, E)
    first = rv(816, E)
    one8 = rv(824, E)
    k128 = rv(832, 16)
    dumf = rv(848, 1)
    base_f = rv(849, BLOCKS)
    selsum = ysh[:, 0, 0:64].bitcast(F16)
    upper = ysh[:, 0, 64:128].bitcast(F16)
    ones16 = ysh[:, 0, 128:192].bitcast(F16)
    cmp16 = ysh[:, 0, 192:320].rearrange("p (e k) -> p e k", e=E)
    blkc = ysh[:, 1, 0:BLOCKS * E].rearrange("p (j e) -> p j e", j=BLOCKS)
    tab = ysh[:, 1, 320:320 + 2 * BLOCKS].rearrange("p (k j) -> p k j", k=2)
    zer = ysh[:, 1, 400:400 + BLOCKS]
    wcol = sb("wcol", [P, BLOCKS])
    idx = sb("idx", [P, BLOCKS], I32)
    wbase = sb("wbase", [P, BLOCKS], I32)
    gidx = sb("gidx", [P, 2], I32)
    sidx = sb("sidx", [P, 2], I32)

    above = below[:, :].bitcast(mybir.dt.uint8).rearrange("p (t s) -> p t s", t=TB)

    bank = [es.enter_context(nc.psum_tensor(f"bank{i}", [P, 512], F32)) for i in range(8)]

    d_in = sem("d_in")
    d_ctx = sem("d_ctx")
    d_x = sem("d_x")
    d_x1 = sem("d_x1")
    d_zero = sem("d_zero")
    d_xn = [sem(f"d_xn{i}") for i in range(2)]
    d_y = [sem(f"d_y{i}") for i in range(2)]
    d_stage = [sem(f"d_stage{i}") for i in range(2)]
    d_xg = [sem(f"d_xg{i}") for i in range(2)]
    d_sc = [sem(f"d_sc{i}") for i in range(2)]
    s_const = sem("s_const")
    s_zero = sem("s_zero")
    s_chain = sem("s_chain")
    s_pool = sem("s_pool")
    s_fall = sem("s_fall")
    s_wT = sem("s_wT")
    s_wTc = sem("s_wTc")
    s_rw = sem("s_rw")
    s_gam = sem("s_gam")
    s_cT = sem("s_cT")
    s_cTc = sem("s_cTc")
    s_sim = sem("s_sim")
    s_simc = sem("s_simc")
    s_sigA = sem("s_sigA")
    s_A = sem("s_A")
    s_AT = sem("s_AT")
    s_x1 = sem("s_x1")
    s_var = sem("s_var")
    s_rstd = sem("s_rstd")
    s_bad = sem("s_bad")
    s_badr = sem("s_badr")
    s_xn = sem("s_xn")
    s_xnT = sem("s_xnT")
    s_xhi = sem("s_xhi")
    s_xlo = sem("s_xlo")
    s_lg = sem("s_lg")
    s_lgc = sem("s_lgc")
    s_gu = sem("s_gu")
    s_sg = sem("s_sg")
    s_t2 = sem("s_t2")
    s_hhi = sem("s_hhi")
    s_hlo = sem("s_hlo")
    s_yps = sem("s_yps")
    s_y = sem("s_y")
    s_whi = sem("s_whi")
    s_wlo = sem("s_wlo")
    s_top2 = sem("s_top2")
    s_wt = sem("s_wt")
    s_sel = sem("s_sel")
    s_rank = sem("s_rank")
    s_oneh = sem("s_oneh")
    s_tabp = sem("s_tabp")
    s_route = sem("s_route")
    s_x2ps = sem("s_x2ps")
    s_x2hi = sem("s_x2hi")
    s_x2lo = sem("s_x2lo")
    s_gu2 = sem("s_gu2")
    s_sig2 = sem("s_sig2")
    s_t12 = sem("s_t12")
    s_h2 = sem("s_h2")
    s_h2ps = sem("s_h2ps")
    s_h2hi = sem("s_h2hi")
    s_h2lo = sem("s_h2lo")
    s_y2ps = sem("s_y2ps")
    s_y2 = sem("s_y2")
    s_gi = sem("s_gi")
    s_held = sem("s_held")
    s_si = sem("s_si")

    block = es.enter_context(nc.Block())
    N_CONST = 11

    @block.sync
    def _(sp):
        sp.dma_start(kT[:, :].rearrange("p (t c) -> p t c", t=TB), ctx_in[0].rearrange("(t p) c -> p t c", p=P)).then_inc(d_ctx, 16)
        sp.dma_start(below[:, 0:C], wq).then_inc(d_in, 16)
        sp.dma_start(below[:, C:2 * C], wk).then_inc(d_in, 16)
        sp.dma_start(ysh[0:E, 0, :], router).then_inc(d_in, 16)
        sp.dma_start(gam[:, 0:1], gamma.to_broadcast([P, 1])).then_inc(d_in, 16)
        for n, v in enumerate((s_gate_b, s_up_b)):
            for q in range(SC):
                sp.dma_start(bias[:, n, q:q + 1], v[SH_ROWS[q]:SH_ROWS[q] + P, :]).then_inc(d_in, 16)
        sp.dma_start(ysh[0:1, 1, :], s_down_b).then_inc(d_in, 16)
        sp.dma_start(xb[:, :, :], x[0].rearrange("(t p) d -> p t d", p=P)).then_inc(d_x, 16)
        sp.wait_ge(s_zero, 1)
        for dst in (xn_dram, out):
            sp.dma_start(dst[DUMMY:DUMMY + P, :], xn[:, 0, :]).then_inc(d_zero, 16)
        for b in range(NB):
            if b + 1 < NB:
                sp.wait_ge(s_sim, TB * (b + 1))
                sp.dma_start(kT[:, :].rearrange("p (t c) -> p t c", t=TB), ctx_in[b + 1].rearrange("(t p) c -> p t c", p=P)).then_inc(d_ctx, 16)
            for t in range(TB):
                g = TB * b + t
                sp.wait_ge(s_x1, g + 1)
                sp.dma_start(out[g * P:(g + 1) * P, :], xb[:, t, :]).then_inc(d_x1, 16)
            for t in range(TB):
                g = TB * b + t
                sp.wait_ge(s_xn, g + 1)
                sp.dma_start(xn_dram[g * P:(g + 1) * P, :], xn[:, t % 2, :]).then_inc(d_xn[t % 2], 16)
            if b + 1 < NB:
                sp.wait_ge(d_x1, 16 * TB * (b + 1))
                sp.dma_start(xb[:, :, :], x[b + 1].rearrange("(t p) d -> p t d", p=P)).then_inc(d_x, 16)
        sp.wait_ge(d_x1, 16 * NT)
        for i in range(2):
            sp.wait_ge(d_xn[i], 16 * NT // 2)
        sp.wait_ge(d_zero, 32)

    @block.gpsimd
    def _(pool):
        chain = [0]

        def link(ins):
            chain[0] += 1
            ins.then_inc(s_pool, 1)
            pool.wait_ge(s_pool, chain[0])

        link(pool.memset(ident[:, :], 0.0))
        pool.affine_select(out=ident[:, :], in_=ident[:, :], compare_op=ALU.not_equal, fill=1.0, base=0,
                           pattern=[[-1, P]], channel_multiplier=1).then_inc(s_const, 1)
        link(pool.memset(row0[:, :], 0.0))
        pool.memset(row0[0:1, :], 1.0).then_inc(s_const, 1)
        pool.iota(rank8[:, :], [[1, 8]], base=1, channel_multiplier=0, allow_small_or_imprecise_dtypes=True).then_inc(s_const, 1)
        pool.memset(pw[:, 1, :], -0.5).then_inc(s_const, 1)
        pool.wait_ge(s_const, 4)

        units = iter(range(len(UNITS)))

        def split_lo(n):
            src, hi, lo, cols, zero = UNITS[n]
            st = stage[:, n % 2, 0:cols]
            pool.wait_ge(s_whi, n + 1)
            link(pool.tensor_scalar(st, st, WS, 1.0, ALU.mult, ALU.mult))
            last = pool.tensor_tensor(W[:, lo:lo + cols], st, W[:, hi:hi + cols], ALU.subtract)
            if zero:
                link(last)
                link(pool.memset(W[0:zero, hi:hi + cols], 0.0))
                last = pool.memset(W[0:zero, lo:lo + cols], 0.0)
            last.then_inc(s_wlo, 1)

        def split_some(k):
            for _ in range(k):
                split_lo(next(units))

        def power(n):
            pool.wait_ge(s_var, n + 1)
            pool.tensor_tensor(rstd[:, :], pw[:, 0, :], pw[:, 1, :], ALU.pow).then_inc(s_rstd, 1)

        def add_shared(b, t):
            g = TB * b + t
            pool.wait_ge(s_y, g + 1)
            pool.wait_ge(d_x1, 16 * TB * (b + 1))
            pool.dma_start(out[g * P:(g + 1) * P, :], ysh[:, t % 2, :], accum_op=ALU.add).then_inc(d_y[t % 2], 16)

        for b in range(NB):
            power(3 * b)
            power(3 * b + 1)
            if b == 0:
                split_some(UNITS_AT[0])
            split_some(UNITS_AT[1 + b])
            pool.wait_ge(s_bad, b + 1)
            pool.partition_all_reduce(bad[:, 1:2], bad[:, 0:1], P, bass.bass_isa.ReduceOp.max).then_inc(s_badr, 1)
            if b:
                for t in range(TB):
                    add_shared(b - 1, t)
            power(3 * b + 2)

        pool.wait_ge(s_A, NT)
        pool.iota(iota, [[1, P]], base=0, channel_multiplier=0, allow_small_or_imprecise_dtypes=True).then_inc(s_const, 1)
        pool.iota(io8, [[1, E]], base=0, channel_multiplier=0, allow_small_or_imprecise_dtypes=True).then_inc(s_const, 1)
        pool.iota(tok1, [[P, NT]], base=1, channel_multiplier=1, allow_small_or_imprecise_dtypes=True).then_inc(s_const, 1)
        pool.iota(k128, [[P, 16]], base=0, channel_multiplier=0, allow_small_or_imprecise_dtypes=True).then_inc(s_const, 1)
        pool.iota(dumf, [[0, 1]], base=DUMMY + 1, channel_multiplier=1, allow_small_or_imprecise_dtypes=True).then_inc(s_const, 1)
        pool.memset(one8, 1.0).then_inc(s_const, 1)
        for i in range(2):
            pool.wait_ge(d_y[i], 16 * (NT - TB) // 2)
        link(pool.memset(upper, 1.0))
        pool.memset(ones16, 1.0)
        pool.affine_select(out=upper, in_=upper, compare_op=ALU.is_gt, fill=0.0, base=0, pattern=[[1, P]],
                           channel_multiplier=-1).then_inc(s_const, 1)

        for t in range(TB):
            g = NT - TB + t
            pool.wait_ge(s_y, g + 1)
            pool.dma_start(out[g * P:(g + 1) * P, :], xn[:, t % 2, :], accum_op=ALU.add).then_inc(d_y[t % 2], 16)
        split_some(len(UNITS) - sum(UNITS_AT))

        def gather(j, p):
            link2(pool.tensor_copy(gidx[:, p:p + 1], idx[:, bass.ds(j, 1)]), s_gi, j + 1)
            pool.indirect_dma_start(out=xg[:, p, :], out_offset=None, in_=xn_dram,
                                    in_offset=bass.IndirectOffsetOnAxis(ap=gidx[:, p:p + 1], axis=0)).then_inc(d_xg[p], 16)

        def scatter(j, m, p):
            if isinstance(j, int) and j == 0:
                for i in range(2):
                    pool.wait_ge(d_y[i], 16 * NT // 2)
            pool.wait_ge(s_y2, j + 1)
            if not (isinstance(j, int) and j == 0):
                pool.wait_ge(d_sc[1 - p], 16 * (m + 1) if p else 16 * m)
            link2(pool.tensor_copy(sidx[:, p:p + 1], idx[:, bass.ds(j, 1)]), s_si, j + 1)
            pool.indirect_dma_start(out=out, out_offset=bass.IndirectOffsetOnAxis(ap=sidx[:, p:p + 1], axis=0),
                                    in_=y2[:, p, :], in_offset=None, compute_op=ALU.add).then_inc(d_sc[p], 16)

        def link2(ins, s, v):
            ins.then_inc(s, 1)
            pool.wait_ge(s, v)
            pool.sem_inc(s_held, 1)

        pool.wait_ge(s_route, 1)
        for i in range(2):
            pool.wait_ge(d_xn[i], 16 * NT // 2)
        pool.wait_ge(d_zero, 32)
        gather(0, 0)
        gather(1, 1)

        def step(j, m, p, fetch=True):
            if fetch:
                pool.wait_ge(s_x2ps, j + 1)
                gather(j + 2, p)
            if not (isinstance(j, int) and j == 0):
                scatter(j - 1, m if p else m - 1, 1 - p)

        run_blocks(pool, step)
        scatter(BLOCKS - 1, (BLOCKS - 1) // 2, (BLOCKS - 1) % 2)
        for i in range(2):
            pool.wait_ge(d_sc[i], 16 * (BLOCKS // 2 + (1 - i) * (BLOCKS % 2)))

    @block.scalar
    def _(act):
        loads = iter(range(len(UNITS)))

        def load_unit(n):
            if n >= len(UNITS):
                return
            if n >= 2:
                act.wait_ge(s_wlo, n - 1)
            at = 0
            for name, e, row, cols in UNITS[n][0]:
                src = dram[name] if e is None else dram[name][e]
                act.dma_start(stage[:, n % 2, at:at + cols], src[row:row + P, :]).then_inc(d_stage[n % 2], 16)
                at += cols

        def split_hi(n):
            src, hi, lo, cols, zero = UNITS[n]
            if n == LATE:
                act.wait_ge(s_gu, NB * SC)
            if n == LATE + PER_EXPERT:
                act.wait_ge(s_yps, NT)
            act.wait_ge(d_stage[n % 2], STAGED[n])
            act.activation(W[:, hi:hi + cols], stage[:, n % 2, 0:cols], ACT.Copy, scale=WS).then_inc(s_whi, 1)
            load_unit(n + 1)

        def split_some(k):
            for _ in range(k):
                split_hi(next(loads))

        load_unit(0)
        act.wait_ge(s_wT, 1)
        act.activation(wqT[:, :], bank[0][:, 0:C], ACT.Copy).then_inc(s_wTc, 1)
        act.activation(wkT[:, :], bank[0][:, C:2 * C], ACT.Copy).then_inc(s_wTc, 1)
        act.wait_ge(s_wT, 2)
        act.activation(rwT[:, 0, :, :], bank[1][:, 0:KD * E].rearrange("p (c e) -> p c e", c=KD), ACT.Copy, scale=WS).then_inc(s_wTc, 1)
        act.wait_ge(d_in, 16 * (4 + 2 * SC + 1))
        act.wait_ge(s_zero, 2)
        act.activation(sdb[0:1, 0, :], ysh[0:1, 1, :], ACT.Copy, scale=HW).then_inc(s_wTc, 1)
        act.activation(gam[:, 1:2], gam[:, 0:1], ACT.Sigmoid).then_inc(s_gam, 1)

        def proj(b):
            act.wait_ge(s_cT, 2 * b + 1)
            act.activation(qT[:, :], bank[0][:, :], ACT.Copy).then_inc(s_cTc, 1)
            act.wait_ge(s_cT, 2 * b + 2)
            act.activation(qT[:, :], bank[0][:, :], ACT.Copy).then_inc(s_cTc, 1)
            act.activation(kT[:, :], bank[1][:, :], ACT.Copy).then_inc(s_cTc, 1)

        def scores(b, t):
            g = TB * b + t
            act.wait_ge(s_sim, g + 1)
            if b:
                act.wait_ge(s_AT, TB * b)
                act.wait_ge(s_x1, TB * (b - 1) + t + 1)
            act.activation(sim[:, t, :], bank[t % 2][:, :], ACT.Copy).then_inc(s_simc, 1)

        def sig_scores(b, t):
            g = TB * b + t
            act.wait_ge(s_simc, g + 1)
            if g >= 2:
                act.wait_ge(s_A, g - 1)
            act.activation(sigA[:, t % 2, :], sim[:, t, :], ACT.Sigmoid, scale=1.0 / ((C / HEADS) ** 0.5 * HEADS)).then_inc(s_sigA, 1)

        def sh_sig(b, q):
            n = SC * b + q
            act.wait_ge(s_gu, n + 1)
            if n >= 2:
                act.wait_ge(s_hlo, n - 1)
            act.activation(sgt[:, q % 2, :], bank[4 + 2 * (q % 2)][:, :], ACT.Sigmoid, bias=bias[:, 0, q:q + 1],
                           scale=1.0 / XW).then_inc(s_sg, 1)

        def sh_hi(b, q):
            n = SC * b + q
            act.wait_ge(s_t2, n + 1)
            if b and q == 0:
                act.wait_ge(s_yps, TB * b)
            act.activation(hS[:, 0, q, :], sgt[:, q % 2, :], ACT.Copy, scale=HS / XW / XW).then_inc(s_hhi, 1)

        def x_hi(b, t):
            g = TB * b + t
            act.wait_ge(s_xnT, g + 1)
            if b and t == 0:
                act.wait_ge(s_gu, SC * b)
            act.activation(xT[:, 0, :, t * P:(t + 1) * P], bank[2 + t % 2][:, :].rearrange("p (c t) -> p c t", c=KD),
                           ACT.Copy, scale=XS).then_inc(s_xhi, 1)

        proj(0)
        for t in range(TB):
            scores(0, t)
        for b in range(NB):
            sig_scores(b, 0)
            sig_scores(b, 1)
            k = UNITS_AT[1 + b] + (UNITS_AT[0] if b == 0 else 0)
            if b:
                sh_sig(b - 1, 0)
                for q in range(SC):
                    split_some(k // SC + (q < k % SC))
                    if q + 1 < SC:
                        sh_sig(b - 1, q + 1)
                    sh_hi(b - 1, q)
            else:
                split_some(k)
            if b + 1 < NB:
                proj(b + 1)
            sig_scores(b, 2)
            sig_scores(b, 3)
            if b + 1 < NB:
                for t in range(TB):
                    scores(b + 1, t)
            for t in range(TB):
                x_hi(b, t)
        sh_sig(NB - 1, 0)
        for q in range(SC):
            if q + 1 < SC:
                sh_sig(NB - 1, q + 1)
            if q == 1:
                act.wait_ge(s_top2, 1)
                act.activation(wt[:, 0, :], wt[:, 1, :], ACT.Sigmoid, scale=1.0 / XW).then_inc(s_wt, 1)
                act.wait_ge(s_wt, 1)
                act.activation(wt[:, 1, :], wt[:, 1, :], ACT.Sigmoid, scale=-1.0 / XW).then_inc(s_wt, 1)
            sh_hi(NB - 1, q)
        split_some(len(UNITS) - sum(UNITS_AT))

        def routed_x(j, p):
            act.wait_ge(s_x2ps, j + 1)
            if not (isinstance(j, int) and j < 2):
                act.wait_ge(s_gu2, j - 1)
            act.activation(xT2[:, 0, :, p, :], bank[0][:, :].rearrange("p (c t) -> p c t", c=KD), ACT.Copy, scale=XS).then_inc(s_x2hi, 1)

        def routed_sig(j, p):
            act.wait_ge(s_gu2, j + 1)
            act.activation(sg2[:, p, :], bank[4 + 2 * p][:, 0:I], ACT.Sigmoid, scale=1.0 / XW).then_inc(s_sig2, 1)

        def routed_h(j, p):
            act.wait_ge(s_h2ps, j + 1)
            if not (isinstance(j, int) and j < 2):
                act.wait_ge(s_y2ps, j - 1)
            act.activation(hT2[:, 0, :, p, :], bank[1][:, 0:DC * P].rearrange("p (c t) -> p c t", c=DC), ACT.Copy).then_inc(s_h2hi, 1)

        def routed_y(j, m, p):
            act.wait_ge(s_y2ps, j + 1)
            if not (isinstance(j, int) and j < 2):
                act.wait_ge(d_sc[p], 16 * m)
            act.activation(y2[:, p, :], bank[2 + p][:, :], ACT.Copy, scale=wcol[:, bass.ds(j, 1)]).then_inc(s_y2, 1)

        def step(j, m, p, fetch=True):
            first_block = isinstance(j, int) and j == 0
            if not first_block:
                routed_h(j - 1, 1 - p)
            if first_block or not (isinstance(j, int) and j == BLOCKS - 1):
                routed_x(j + 1, 1 - p)
            routed_sig(j, p)
            if not first_block:
                routed_y(j - 1, m if p else m - 1, 1 - p)

        act.wait_ge(s_route, 1)
        act.wait_ge(d_x1, 16 * NT)
        routed_x(0, 0)
        run_blocks(act, step)
        j = BLOCKS - 1
        routed_h(j, j % 2)
        routed_y(j, j // 2, j % 2)

    @block.tensor
    def _(pe):
        pe.wait_ge(s_const, 1)
        pe.wait_ge(d_in, 16 * (4 + 2 * SC + 1))
        pe.transpose(bank[0][:, 0:C], below[:, 0:C], ident[:, :])
        pe.transpose(bank[0][:, C:2 * C], below[:, C:2 * C], ident[:, :]).then_inc(s_wT, 1)
        for c in range(KD):
            last = pe.transpose(bank[1][:, c * E:(c + 1) * E], ysh[0:E, 0, c * P:(c + 1) * P], ident[0:E, 0:E])
        last.then_inc(s_wT, 1)

        def proj(b):
            pe.wait_ge(d_ctx, 16 * (b + 1))
            if b == 0:
                pe.wait_ge(s_wTc, 3)
                pe.wait_ge(s_rw, 1)
            else:
                pe.wait_ge(s_simc, TB * b)
                pe.wait_ge(s_lgc, b - 1) if b > 1 else None
            for t in range(TB):
                last = pe.transpose(bank[0][:, t * P:(t + 1) * P], kT[:, t * C:(t + 1) * C], ident[:, :])
            last.then_inc(s_cT, 1)
            pe.wait_ge(s_cTc, 3 * b + 1)
            pe.matmul(bank[0][:, :], wqT[:, :], qT[:, :], start=True, stop=True)
            pe.matmul(bank[1][:, :], wkT[:, :], qT[:, :], start=True, stop=True).then_inc(s_cT, 1)

        def scores(b, t):
            g = TB * b + t
            if t < 2:
                pe.wait_ge(s_cTc, 3 * b + 3)
            else:
                pe.wait_ge(s_simc, g - 1)
            pe.matmul(bank[t % 2][:, :], qT[:, t * P:(t + 1) * P], kT[:, :], start=True, stop=True).then_inc(s_sim, 1)

        def transpose_A(b, t):
            g = TB * b + t
            if t == 0:
                pe.wait_ge(s_A, TB * (b + 1))
            if b and t < 2:
                pe.wait_ge(s_xlo, TB * b)
            if t >= 2:
                pe.wait_ge(s_x1, g - 1)
            for m in range(TB):
                last = pe.transpose(bank[2 + t % 2][:, m * P:(m + 1) * P], sim[:, m, t * P:(t + 1) * P], ident[:, :])
            last.then_inc(s_AT, 1)

        def transpose_xn(b, t):
            g = TB * b + t
            pe.wait_ge(s_xn, g + 1)
            if t >= 2:
                pe.wait_ge(s_xlo, g - 1)
            for c in range(KD):
                last = pe.transpose(bank[2 + t % 2][:, c * P:(c + 1) * P], xn[:, t % 2, c * P:(c + 1) * P], ident[:, :])
            last.then_inc(s_xnT, 1)

        def logits(b):
            pe.wait_ge(s_xlo, TB * (b + 1))
            pe.wait_ge(s_rw, 1)
            pe.wait_ge(s_simc, min(TB * (b + 2), NT))
            for t in range(TB):
                o = bank[0][:, t * E:(t + 1) * E]
                for c in range(KD):
                    xh, xl = (xT[:, s, c, t * P:(t + 1) * P] for s in range(2))
                    pe.matmul(o, xh, rwT[:, 0, c, :], start=(c == 0), stop=False)
                    pe.matmul(o, xh, rwT[:, 1, c, :], start=False, stop=False)
                    last = pe.matmul(o, xl, rwT[:, 0, c, :], start=False, stop=(c == KD - 1))
            last.then_inc(s_lg, 1)

        def shared_up(b, q):
            n = SC * b + q
            if n == 0:
                pe.wait_ge(s_wlo, 2 * KD)
            if q == 0:
                pe.wait_ge(s_xlo, TB * (b + 1))
            if q >= 2:
                pe.wait_ge(s_t2, n - 1)
            elif b:
                pe.wait_ge(s_y, TB * b - 2 + 2 * q)
            for w in range(2):
                o = bank[4 + 2 * (q % 2) + w][:, :]
                for c in range(KD):
                    at = (2 * c + w) * SI + SH_ROWS[q]
                    wh, wl = W[:, SG_HI + at:SG_HI + at + P], W[:, SG_LO + at:SG_LO + at + P]
                    pe.matmul(o, wh, xT[:, 0, c, :], start=(c == 0), stop=False)
                    pe.matmul(o, wh, xT[:, 1, c, :], start=False, stop=False)
                    last = pe.matmul(o, wl, xT[:, 0, c, :], start=False, stop=(c == KD - 1))
            last.then_inc(s_gu, 1)

        def shared_down(b, t):
            if b == 0 and t == 0:
                pe.wait_ge(s_wlo, SHARED_UNITS)
            pe.wait_ge(s_hlo, SC * (b + 1))
            o = bank[4 + t][:, :]
            pe.matmul(o, row0[:, :], sdb[:, 0, :], start=True, stop=False)
            pe.matmul(o, row0[:, :], sdb[:, 1, :], start=False, stop=False)
            for q in range(SC):
                hh, hl = (hS[:, s, q, t * P:(t + 1) * P] for s in range(2))
                wh, wl = W[:, SD_HI + q * D:SD_HI + (q + 1) * D], W[:, SD_LO + q * D:SD_LO + (q + 1) * D]
                pe.matmul(o, hh, wh, start=False, stop=False)
                pe.matmul(o, hh, wl, start=False, stop=False)
                last = pe.matmul(o, hl, wh, start=False, stop=(q == SC - 1))
            last.then_inc(s_yps, 1)

        def rank():
            pe.wait_ge(s_sel, 1)
            pe.wait_ge(s_const, N_CONST)
            pe.matmul(bank[2][:, 0:NT * E], upper, selsum, start=True, stop=False)
            for g in range(NT - 1):
                k = NT - 1 - g
                pe.matmul(bank[2][:, (g + 1) * E:NT * E].rearrange("p (g e) -> p g e", g=k), ones16,
                          selsum[:, g * E:(g + 1) * E].rearrange("p (g e) -> p g e", g=1).to_broadcast([P, k, E]),
                          start=False, stop=(g == NT - 2))
            for g in range(NT):
                last = pe.matmul(bank[3][:, 0:E], ones16, selsum[:, g * E:(g + 1) * E], start=(g == 0), stop=(g == NT - 1))
            last.then_inc(s_rank, 1)

        def table():
            for n in range(2 * NT):
                pe.wait_ge(s_oneh, n + 1)
                pe.matmul(bank[0][:, 0:2 * BLOCKS], oneh[:, n % 4, :],
                          valh[:, n % 4, :, :].rearrange("p k b -> p (k b)"),
                          start=(n == 0), stop=(n == 2 * NT - 1)).then_inc(s_tabp, 1)

        proj(0)
        for t in range(TB):
            scores(0, t)
        for b in range(NB):
            if b:
                for q in range(SC):
                    shared_up(b - 1, q)
                for t in range(TB):
                    shared_down(b - 1, t)
            if b + 1 < NB:
                proj(b + 1)
            for t in range(TB):
                transpose_A(b, t)
            if b + 1 < NB:
                for t in range(TB):
                    scores(b + 1, t)
            for t in range(TB):
                transpose_xn(b, t)
            logits(b)
        for q in range(SC):
            shared_up(NB - 1, q)
            if q == 1:
                rank()
        for t in range(TB):
            shared_down(NB - 1, t)
        table()

        def routed_x(j, m, p):
            pe.wait_ge(d_xg[p], 16 * (m + 1))
            if isinstance(j, int) and j == 0:
                pe.wait_ge(s_route, 1)
            else:
                pe.wait_ge(s_x2lo, j)
            for c in range(KD):
                last = pe.transpose(bank[0][:, c * P:(c + 1) * P], xg[:, p, c * P:(c + 1) * P], ident[:, :])
            last.then_inc(s_x2ps, 1)

        def routed_up(j, p, at):
            pe.wait_ge(s_x2lo, j + 1)
            if not (isinstance(j, int) and j < 2):
                pe.wait_ge(s_h2, j - 1)
            elif j == 0:
                pe.wait_ge(s_y, NT)
            og, ou = bank[4 + 2 * p][:, 0:I], bank[5 + 2 * p][:, 0:I]
            for c in range(KD):
                hi, lo = at + (GU_HI + c * GU), at + (GU_LO + c * GU)
                xh, xl = xT2[:, 0, c, p, :], xT2[:, 1, c, p, :]
                f, z = c == 0, c == KD - 1
                pe.matmul(og, xh, W[:, bass.ds(hi, I)], start=f, stop=False)
                pe.matmul(ou, xh, W[:, bass.ds(hi + I, I)], start=f, stop=False)
                pe.matmul(og, xh, W[:, bass.ds(lo, I)], start=False, stop=False)
                pe.matmul(ou, xh, W[:, bass.ds(lo + I, I)], start=False, stop=False)
                pe.matmul(og, xl, W[:, bass.ds(hi, I)], start=False, stop=z)
                last = pe.matmul(ou, xl, W[:, bass.ds(hi + I, I)], start=False, stop=z)
            last.then_inc(s_gu2, 1)

        def routed_hT(j, p):
            pe.wait_ge(s_h2, j + 1)
            if not (isinstance(j, int) and j == 0):
                pe.wait_ge(s_h2lo, j)
            for c in range(DC):
                last = pe.transpose(bank[1][:, c * P:(c + 1) * P], h2[:, p, DOWN_ROWS[c]:DOWN_ROWS[c] + P], ident[:, :])
            last.then_inc(s_h2ps, 1)

        def routed_down(j, p, at):
            pe.wait_ge(s_h2lo, j + 1)
            if not (isinstance(j, int) and j < 2):
                pe.wait_ge(s_y2, j - 1)
            o = bank[2 + p][:, :]
            for c in range(DC):
                hh, hl = hT2[:, 0, c, p, :], hT2[:, 1, c, p, :]
                wh, wl = W[:, bass.ds(at + (DN_HI + c * D), D)], W[:, bass.ds(at + (DN_LO + c * D), D)]
                pe.matmul(o, hh, wh, start=(c == 0), stop=False)
                pe.matmul(o, hh, wl, start=False, stop=False)
                last = pe.matmul(o, hl, wh, start=False, stop=(c == DC - 1))
            last.then_inc(s_y2ps, 1)

        def where(j):
            return pe.value_load(wbase[0:1, bass.ds(j, 1)], min_val=0, max_val=(E - 1) * EW)

        def step(j, m, p, fetch=True):
            first_block = isinstance(j, int) and j == 0
            if not first_block:
                routed_hT(j - 1, 1 - p)
            if first_block or not (isinstance(j, int) and j == BLOCKS - 1):
                routed_x(j + 1, m + (1 if p else 0), 1 - p)
            if first_block:
                pe.wait_ge(s_wlo, len(UNITS))
            routed_up(j, p, where(j))
            if not first_block:
                routed_down(j - 1, 1 - p, where(j - 1))

        routed_x(0, 0, 0)
        run_blocks(pe, step)
        j = BLOCKS - 1
        routed_hT(j, j % 2)
        routed_down(j, j % 2, where(j))

    @block.vector
    def _(dve):
        chain = [0]

        def link(ins):
            chain[0] += 1
            ins.then_inc(s_chain, 1)
            dve.wait_ge(s_chain, chain[0])

        dve.memset(xn[:, 0, :], 0.0).then_inc(s_zero, 1)
        dve.memset(sdb[:, :, :], 0.0).then_inc(s_zero, 1)
        dve.wait_ge(d_in, 16 * (4 + 2 * SC + 1))
        dve.wait_ge(s_wTc, 4)
        dve.scalar_tensor_tensor(rwT[:, 1, :, :], bank[1][:, 0:KD * E].rearrange("p (c e) -> p c e", c=KD), WS,
                                 rwT[:, 0, :, :], ALU.mult, ALU.subtract)
        dve.scalar_tensor_tensor(sdb[0:1, 1, :], ysh[0:1, 1, :], HW, sdb[0:1, 0, :], ALU.mult, ALU.subtract).then_inc(s_rw, 1)
        dve.tensor_scalar(biasS[:, :, :], bias[:, :, :], XW, None, ALU.mult)
        dve.wait_ge(s_gam, 1)
        dve.wait_ge(s_const, 4)
        dve.tensor_scalar(gam[:, 2:3], gam[:, 1:2], -1.0, 1.0, ALU.mult, ALU.add)
        link(dve.tensor_scalar(gam[:, 3:4], gam[:, 1:2], 0.5, None, ALU.mult))

        def variance(src, n, eps):
            for t in range(TB):
                last = dve.bn_stats(stats[:, t, :], src[:, t, :])
            link(last)
            for t in range(TB):
                last = dve.bn_aggr(mv[:, t, :], stats[:, t, :])
            link(last)
            dve.tensor_scalar(pw[:, 0, :], mv[:, :, 1], eps, None, ALU.add).then_inc(s_var, 1)
            dve.wait_ge(s_rstd, n + 1)

        def threshold_start(b):
            dve.wait_ge(s_simc, TB * (b + 1))
            variance(sim, 3 * b, 1e-30)
            link(dve.tensor_tensor(dif[:, 0, :], mv[:, :, 1], rstd[:, :], ALU.mult))
            dve.scalar_tensor_tensor(probe[:, 0, :], dif[:, 0, :], START_Z, mv[:, :, 0], ALU.mult, ALU.add)
            dve.scalar_tensor_tensor(lo_[:, 0, :], dif[:, 0, :], -SPAN_Z, mv[:, :, 0], ALU.mult, ALU.add)
            dve.scalar_tensor_tensor(hi_[:, 0, :], dif[:, 0, :], SPAN_Z, mv[:, :, 0], ALU.mult, ALU.add)
            dve.memset(lo_[:, 1, :], float(S))
            link(dve.memset(hi_[:, 1, :], 0.0))

        def threshold_probe(b, it):
            for t in range(TB):
                last = dve.tensor_scalar(above[:, t, :], sim[:, t, :], probe[:, 0, t:t + 1], None, ALU.is_ge, ALU.add,
                                         accum_out=probe[:, 1, t:t + 1])
            link(last)
            dve.tensor_scalar(msk[:, 0, :], probe[:, 1, :], KTH - WIN / 2, None, ALU.is_ge)
            link(dve.tensor_scalar(msk[:, 1, :], probe[:, 1, :], KTH - WIN / 2, None, ALU.is_lt))
            for k, end in enumerate((lo_, hi_)):
                for w in range(2):
                    last = dve.copy_predicated(end[:, w, :], msk[:, k, :].bitcast(U32), probe[:, w, :])
            link(last)
            if it < PROBES - 1:
                link(dve.tensor_tensor(dif[:, :, :], lo_[:, :, :], hi_[:, :, :], ALU.subtract))
                link(dve.reciprocal(dif[:, 1, :], dif[:, 1, :]))
                link(dve.tensor_tensor(dif[:, 0, :], dif[:, 0, :], dif[:, 1, :], ALU.mult))
                link(dve.scalar_tensor_tensor(dif[:, 0, :], lo_[:, 1, :], KTH - WIN / 2 - 0.5, dif[:, 0, :], ALU.subtract, ALU.mult))
                link(dve.tensor_tensor(probe[:, 0, :], lo_[:, 0, :], dif[:, 0, :], ALU.subtract))

        def threshold_end(b):
            link(dve.tensor_scalar(msk[:, 0, :], lo_[:, 1, :], float(KTH - 1), None, ALU.is_le))
            for w in range(2):
                last = dve.copy_predicated(hi_[:, w, :], msk[:, 0, :].bitcast(U32), lo_[:, w, :])
            link(last)
            dve.tensor_scalar(dif[:, 0, :], hi_[:, 1, :], -1.0, float(KTH), ALU.mult, ALU.add)
            link(dve.tensor_scalar(msk[:, 1, :], hi_[:, 1, :], float(KTH - WIN), None, ALU.is_lt))
            dve.tensor_reduce(bad[:, 0:1], msk[:, 1, :], AX.X, ALU.max).then_inc(s_bad, 1)
            for t in range(TB):
                link(dve.tensor_scalar(below[:, :], sim[:, t, :], hi_[:, 0, t:t + 1], -3e38, ALU.is_ge, ALU.mult))
                link(dve.tensor_tensor(below[:, :], below[:, :], sim[:, t, :], ALU.add))
                link(dve.max(top[:, t, :], below[:, :]))
            for t in range(TB):
                last = dve.scalar_tensor_tensor(pick[:, t, :], rank8[:, :], dif[:, 0, t:t + 1], top[:, t, :], ALU.is_equal, ALU.mult)
            link(last)
            link(dve.tensor_reduce(thr[:, :], pick[:, :, :], AX.X, ALU.add))
            dve.wait_ge(s_badr, b + 1)
            link(dve.tensor_copy(badi[:, :], bad[:, 1:2]))
            missed = dve.value_load(badi[0:1, 0:1], min_val=0, max_val=1)
            rounds = KTH // 8
            per_tile = 1 + 2 * rounds + 1
            with dve.If(missed > 0):
                for t in range(TB):
                    at = (TB * b + t) * per_tile
                    dve.tensor_copy(below[:, :], sim[:, t, :]).then_inc(s_fall, 1)
                    dve.wait_ge(s_fall, at + 1)
                    with dve.Fori(0, rounds) as r:
                        dve.max(top[:, t, :], below[:, :]).then_inc(s_fall, 1)
                        dve.wait_ge(s_fall, 2 * r + (at + 2))
                        dve.sem_inc(s_held, 1)
                        dve.match_replace(below[:, :], top[:, t, :], below[:, :], -3e38).then_inc(s_fall, 1)
                        dve.wait_ge(s_fall, 2 * r + (at + 3))
                    dve.max(top[:, t, :], below[:, :]).then_inc(s_fall, 1)
                    dve.wait_ge(s_fall, at + per_tile)
                    dve.tensor_copy(thr[:, t:t + 1], top[:, t, KTH - 8 * rounds - 1:KTH - 8 * rounds])
            with dve.Else():
                dve.sem_inc(s_fall, TB * per_tile)
            dve.wait_ge(s_fall, (b + 1) * TB * per_tile)

        def layer_norm_x(b):
            dve.wait_ge(d_x, 16 * (b + 1))
            variance(xb, 3 * b + 1, EPS)
            link(dve.tensor_scalar(aff[:, 0, :], rstd[:, :], gam[:, 2:3], None, ALU.mult))
            link(dve.scalar_tensor_tensor(aff[:, 1, :], mv[:, :, 0], -1.0, aff[:, 0, :], ALU.mult, ALU.mult))
            link(dve.tensor_scalar(aff[:, 0, :], aff[:, 0, :], 1.0, None, ALU.add))
            for t in range(TB):
                last = dve.tensor_scalar(xb[:, t, :], xb[:, t, :], aff[:, 0, t:t + 1], aff[:, 1, t:t + 1], ALU.mult, ALU.add)
            link(last)

        def mask(b):
            for t in range(TB):
                g = TB * b + t
                dve.wait_ge(s_sigA, g + 1)
                dve.scalar_tensor_tensor(sim[:, t, :], sim[:, t, :], thr[:, t:t + 1], sigA[:, t % 2, :], ALU.is_ge,
                                         ALU.mult).then_inc(s_A, 1)

        def residual(b):
            dve.wait_ge(s_A, TB * (b + 1))
            for t in range(TB):
                g = TB * b + t
                link(dve.scalar_tensor_tensor(xb[:, t, :], sim[:, t, :], gam[:, 3:4], xb[:, t, :], ALU.mult, ALU.add))
                dve.wait_ge(s_AT, g + 1)
                dve.scalar_tensor_tensor(xb[:, t, :], bank[2 + t % 2][:, :], gam[:, 3:4], xb[:, t, :], ALU.mult,
                                         ALU.add).then_inc(s_x1, 1)
            dve.wait_ge(s_x1, TB * (b + 1))

        def normalise(b):
            variance(xb, 3 * b + 2, EPS)
            link(dve.scalar_tensor_tensor(aff[:, 1, :], mv[:, :, 0], -1.0, rstd[:, :], ALU.mult, ALU.mult))
            for t in range(TB):
                g = TB * b + t
                if t >= 2:
                    xT_lo(b, t - 2)
                if g >= 2:
                    dve.wait_ge(d_xn[t % 2], 16 * (g // 2))
                    dve.wait_ge(s_xnT, g - 1)
                else:
                    dve.wait_ge(d_zero, 32)
                dve.tensor_scalar(xn[:, t % 2, :], xb[:, t, :], rstd[:, t:t + 1], aff[:, 1, t:t + 1], ALU.mult,
                                  ALU.add).then_inc(s_xn, 1)
            for t in range(2, TB):
                xT_lo(b, t)

        def xT_lo(b, t):
            dve.wait_ge(s_xhi, TB * b + t + 1)
            cols = slice(t * P, (t + 1) * P)
            dve.scalar_tensor_tensor(xT[:, 1, :, cols], bank[2 + t % 2][:, :].rearrange("p (c t) -> p c t", c=KD), XS,
                                     xT[:, 0, :, cols], ALU.mult, ALU.subtract).then_inc(s_xlo, 1)

        def largest_logits(b):
            dve.wait_ge(s_lg, b + 1)
            tiles = slice(TB * b, TB * (b + 1))
            dve.tensor_copy(lg[:, tiles, :], bank[0][:, 0:TB * E].rearrange("p (t e) -> p t e", t=TB)).then_inc(s_lgc, 1)
            dve.wait_ge(s_lgc, b + 1)
            for g in range(TB * b, TB * (b + 1)):
                last = dve.max(mx[:, g, :], lg[:, g, :])
            link(last)
            for g in range(TB * b, TB * (b + 1)):
                last = dve.max_index(mxi[:, g, :], mx[:, g, :], lg[:, g, :])
            link(last)

        def shared_lo(b, q):
            n = SC * b + q
            dve.wait_ge(s_hhi, n + 1)
            dve.scalar_tensor_tensor(hS[:, 1, q, :], sgt[:, q % 2, :], HS / XW / XW, hS[:, 0, q, :], ALU.mult,
                                     ALU.subtract).then_inc(s_hlo, 1)

        def shared_hidden(b, q):
            n = SC * b + q
            if q:
                shared_lo(b, q - 1)
            pair = 4 + 2 * (q % 2)
            dve.wait_ge(s_sg, n + 1)
            link(dve.scalar_tensor_tensor(sgt[:, q % 2, :], bank[pair][:, :], biasS[:, 0, q:q + 1], sgt[:, q % 2, :], ALU.add, ALU.mult))
            dve.scalar_tensor_tensor(sgt[:, q % 2, :], bank[pair + 1][:, :], biasS[:, 1, q:q + 1], sgt[:, q % 2, :],
                                     ALU.add, ALU.mult).then_inc(s_t2, 1)
            if q == SC - 1:
                shared_lo(b, q)

        def shared_out(b, dst):
            for t in range(TB):
                g = TB * b + t
                dve.wait_ge(s_yps, g + 1)
                if g >= 2 and dst is ysh or t >= 2:
                    dve.wait_ge(d_y[t % 2], 16 * (g // 2))
                dve.tensor_scalar(dst[:, t % 2, :], bank[4 + t][:, :], 1.0 / HW, None, ALU.mult).then_inc(s_y, 1)

        for b in range(NB):
            threshold_start(b)
            layer_norm_x(b)
            for it in range(PROBES):
                threshold_probe(b, it)
                if b:
                    shared_hidden(b - 1, it)
            if b:
                shared_hidden(b - 1, PROBES)
            threshold_end(b)
            mask(b)
            if b:
                shared_out(b - 1, ysh)
            residual(b)
            normalise(b)
            largest_logits(b)

        last_b = NB - 1
        dve.tensor_copy(ef, mxi[:, :, 0:2].rearrange("p g k -> p k g"))
        dve.tensor_tensor(wt[:, 1, :], mx[:, :, 0], mx[:, :, 1], ALU.subtract).then_inc(s_top2, 1)
        dve.wait_ge(s_top2, 1)
        dve.wait_ge(s_const, N_CONST)
        for k in range(2):
            last = dve.tensor_tensor(sel[:, k, :, :], ef[:, k, :].rearrange("p (g o) -> p g o", o=1).to_broadcast([P, NT, E]),
                                     io8.rearrange("p (o e) -> p o e", o=1).to_broadcast([P, NT, E]), ALU.is_equal)
        link(last)
        dve.tensor_tensor(selsum.rearrange("p (g e) -> p g e", g=NT), sel[:, 0, :, :], sel[:, 1, :, :], ALU.add).then_inc(s_sel, 1)
        shared_hidden(last_b, 0)
        shared_hidden(last_b, 1)
        dve.wait_ge(s_rank, 1)
        link(dve.tensor_copy(cnt, bank[3][:, 0:E]))
        link(dve.tensor_tensor(cmp16, cnt.rearrange("p (e o) -> p e o", o=1).to_broadcast([P, E, 16]),
                               k128.rearrange("p (o k) -> p o k", o=1).to_broadcast([P, E, 16]), ALU.is_gt))
        link(dve.tensor_reduce(nblk, cmp16, AX.X, ALU.add))
        link(dve.tensor_tensor_scan(ends, one8, nblk, 0.0, ALU.mult, ALU.add))
        link(dve.tensor_tensor(first, ends, nblk, ALU.subtract))
        link(dve.scalar_tensor_tensor(slotr, first.rearrange("p (o e) -> p o e", o=1).to_broadcast([P, NT, E]), float(P),
                                      bank[2][:, 0:NT * E].rearrange("p (g e) -> p g e", g=NT), ALU.mult, ALU.add))
        for k in range(2):
            last = dve.tensor_tensor(prod[:, k, :, :], sel[:, k, :, :], slotr, ALU.mult)
        link(last)
        link(dve.tensor_reduce(pos, prod, AX.X, ALU.add))
        link(dve.tensor_copy(posi, pos.rearrange("p k g -> p (k g)")))
        dve.tensor_scalar(lowi, posi, P - 1, None, ALU.bitwise_and)
        link(dve.tensor_scalar(higi, posi, P.bit_length() - 1, None, ALU.logical_shift_right))
        dve.tensor_copy(lowf.rearrange("p k g -> p (k g)"), lowi)
        link(dve.tensor_copy(higf.rearrange("p k g -> p (k g)"), higi))
        link(dve.tensor_tensor(blkc, iota[:, 0:BLOCKS].rearrange("p (j o) -> p j o", o=1).to_broadcast([P, BLOCKS, E]),
                               ends.rearrange("p (o e) -> p o e", o=1).to_broadcast([P, BLOCKS, E]), ALU.is_ge))
        link(dve.tensor_reduce(base_f, blkc, AX.X, ALU.add))
        link(dve.tensor_scalar(base_f, base_f, float(E - 1), float(EW), ALU.min, ALU.mult))
        dve.tensor_copy(wbase[:, :], base_f)
        dve.wait_ge(s_wt, 2)
        for n in range(2 * NT):
            g, k = n // 2, n % 2
            if n >= 4:
                dve.wait_ge(s_tabp, n - 3)
            dve.tensor_scalar(oneh[:, n % 4, :], iota, lowf[:, k, g:g + 1], None, ALU.is_equal)
            dve.tensor_scalar(valh[:, n % 4, 0, :], iota[:, 0:BLOCKS], higf[:, k, g:g + 1], tok1[:, g:g + 1], ALU.is_equal, ALU.mult)
            dve.tensor_scalar(valh[:, n % 4, 1, :], iota[:, 0:BLOCKS], higf[:, k, g:g + 1], wt[:, k, g:g + 1], ALU.is_equal,
                              ALU.mult).then_inc(s_oneh, 1)
            if n == 3:
                for q in range(2, SC):
                    shared_hidden(last_b, q)
                dve.wait_ge(s_xnT, NT)
                for i in range(2):
                    dve.wait_ge(d_xn[i], 16 * NT // 2)
                shared_out(last_b, xn)
        dve.wait_ge(s_tabp, 2 * NT)
        link(dve.tensor_copy(tab, bank[0][:, 0:2 * BLOCKS].rearrange("p (k j) -> p k j", k=2)))
        link(dve.tensor_scalar(zer, tab[:, 0, :], 0.0, dumf, ALU.is_equal, ALU.mult))
        dve.tensor_scalar(wcol[:, :], tab[:, 1, :], 1.0 / HW, None, ALU.mult)
        dve.scalar_tensor_tensor(idx[:, :], tab[:, 0, :], -1.0, zer, ALU.add, ALU.add).then_inc(s_route, 1)

        def routed_x(j, p):
            dve.wait_ge(s_x2hi, j + 1)
            dve.scalar_tensor_tensor(xT2[:, 1, :, p, :], bank[0][:, :].rearrange("p (c t) -> p c t", c=KD), XS,
                                     xT2[:, 0, :, p, :], ALU.mult, ALU.subtract).then_inc(s_x2lo, 1)

        def routed_hidden(j, p):
            dve.wait_ge(s_sig2, j + 1)
            dve.tensor_tensor(sg2[:, p, :], bank[4 + 2 * p][:, 0:I], sg2[:, p, :], ALU.mult).then_inc(s_t12, 1)
            dve.wait_ge(s_t12, j + 1)
            if not (isinstance(j, int) and j < 2):
                dve.wait_ge(s_h2ps, j - 1)
            dve.scalar_tensor_tensor(h2[:, p, :], bank[5 + 2 * p][:, 0:I], HS / XW / XW, sg2[:, p, :], ALU.mult,
                                     ALU.mult).then_inc(s_h2, 1)

        def routed_h(j, p):
            dve.wait_ge(s_h2hi, j + 1)
            dve.tensor_tensor(hT2[:, 1, :, p, :], bank[1][:, 0:DC * P].rearrange("p (c t) -> p c t", c=DC),
                              hT2[:, 0, :, p, :], ALU.subtract).then_inc(s_h2lo, 1)

        def step(j, m, p, fetch=True):
            first_block = isinstance(j, int) and j == 0
            if not first_block:
                routed_h(j - 1, 1 - p)
            if first_block or not (isinstance(j, int) and j == BLOCKS - 1):
                routed_x(j + 1, 1 - p)
            routed_hidden(j, p)

        dve.wait_ge(d_x1, 16 * NT)
        routed_x(0, 0)
        run_blocks(dve, step)
        j = BLOCKS - 1
        routed_h(j, j % 2)

    es.close()


def run_blocks(eng, step):
    for j in range(HEAD_BLOCKS):
        step(j, j // 2, j % 2)
    with eng.Fori(0, (BLOCKS - HEAD_BLOCKS - 2) // 2) as i:
        step(2 * i + HEAD_BLOCKS, i + HEAD_BLOCKS // 2, 1)
        step(2 * i + (HEAD_BLOCKS + 1), i + (HEAD_BLOCKS // 2 + 1), 0)
    for j in (BLOCKS - 2, BLOCKS - 1):
        step(j, j // 2, j % 2, fetch=False)


def kernel(**inputs):
    import numpy as np
    import concourse.bacc as bacc
    from concourse.bass_utils import run_bass_kernel_spmd

    nc = bacc.Bacc("TRN2", target_bir_lowering=False, num_devices=1)
    shapes = {
        "x": (NB, S, D), "ctx_512": (NB, S, C), "L0_xattn_Wq": (C, C), "L0_xattn_Wk": (C, C),
        "L0_xattn_gamma_raw": (1, 1), "L0_ffn_router_w": (E, D), "L0_ffn_gate_w": (E, D, I), "L0_ffn_up_w": (E, D, I),
        "L0_ffn_down_w": (E, I, D), "L0_ffn_s_gate_w": (D, SI), "L0_ffn_s_gate_b": (SI, 1), "L0_ffn_s_up_w": (D, SI),
        "L0_ffn_s_up_b": (SI, 1), "L0_ffn_s_down_w": (SI, D), "L0_ffn_s_down_b": (1, D),
    }
    arrays, args = {}, []
    for name, shape in shapes.items():
        arrays[name + "_in"] = np.ascontiguousarray(inputs[name]).reshape(shape)
        args.append(nc.dram_tensor(name + "_in", shape, F32, kind="ExternalInput").ap())
    out = nc.dram_tensor("out_dram", (T + P, D), F32, kind="ExternalOutput").ap()
    xn_dram = nc.dram_tensor("xn_dram", (T + P, D), F32, kind="Internal").ap()
    build(nc, *args, out, xn_dram)
    r = run_bass_kernel_spmd(nc, [arrays], core_ids=[0])
    return r.results[0]["out_dram"][:T].reshape(NB, S, D)
```

```python
from contextlib import ExitStack

import concourse.bass as bass
from concourse import mybir

F32 = mybir.dt.float32
F16 = mybir.dt.float16
I32 = mybir.dt.int32
U32 = mybir.dt.uint32
ALU = mybir.AluOpType
ACT = mybir.ActivationFunctionType
AX = mybir.AxisListType

P = 128
NB, S, D = 4, 512, 512
TB = S // P
NT = NB * TB
T = NB * S
C = 128
KD = D // P
E, TOPK = 8, 2
I = 352
SI = 704
HEADS = 4
EPS = 1e-5

KTH = int(S * 0.3)
WIN = 8
PROBES = 5
ACT_TILES = 2
START_Z, SPAN_Z = 0.507, 1.5

XS, WS, HS = 16.0, 64.0, 4.0
XW = XS * WS
HW = HS * WS

DOWN_ROWS = [0, 128, I - P]
DOWN_ZERO = [0, 0, 2 * P - (I - P)]
SH_ROWS = [0, 128, 256, 384, 512, SI - P]
SH_ZERO = [0, 0, 0, 0, 0, 5 * P - (SI - P)]
DC, SC = len(DOWN_ROWS), len(SH_ROWS)

GU = 2 * I
GU_HI, GU_LO = 0, KD * GU
DN_HI, DN_LO = 2 * KD * GU, 2 * KD * GU + DC * D
EW = DN_LO + DC * D
SH = (E - 2) * EW
SG_HI, SG_LO = SH, SH + KD * 2 * SI
SD_HI, SD_LO = SH + 2 * KD * 2 * SI, SH + 2 * KD * 2 * SI + SC * D

BLOCKS = T * TOPK // P + E - 1
HEAD_BLOCKS = 3
RING = 8
TABLE_AT = [(0, 10), (10, 21), (21, 2 * NT)]
AT_BANK = [2, 3, 0, 1]
DUMMY = T


def weight_units():
    units = []
    for c in range(KD):
        for n, w in enumerate(("s_gate", "s_up")):
            units.append(([(w, None, c * P, SI)], SG_HI + (2 * c + n) * SI, SG_LO + (2 * c + n) * SI, SI, 0))
    for q in range(SC):
        units.append(([("s_down", None, SH_ROWS[q], D)], SD_HI + q * D, SD_LO + q * D, D, SH_ZERO[q]))
    for e in range(E):
        b = e * EW
        for c in range(KD):
            units.append(([("gate", e, c * P, I), ("up", e, c * P, I)], b + GU_HI + c * GU, b + GU_LO + c * GU, GU, 0))
        for q in range(DC):
            units.append(([("down", e, DOWN_ROWS[q], D)], b + DN_HI + q * D, b + DN_LO + q * D, D, DOWN_ZERO[q]))
    return units


UNITS = weight_units()
EARLY = 2 * KD
PER_EXPERT = KD + DC
LATE = EARLY + SC + (E - 2) * PER_EXPERT
LAST = LATE + PER_EXPERT
UNITS_AT = [([3, 2, 2, 2, 2], [], 2, 3), ([1] * 5, [1, 1, 1, 1, 0], 1, 1), ([1] * 5, [1, 1, 1, 0, 0], 1, 1), ([1] * 5, [1, 1, 1, 1, 0], 1, 1)]
IN_WINDOW = [sum(a) + sum(b) + c + d for a, b, c, d in UNITS_AT]
assert EARLY + sum(IN_WINDOW) == LATE
BY_POOL = LAST - EARLY


def stage_counts():
    at, early, out = [0, 0], [0] * 4, []
    for n, (src, *_) in enumerate(UNITS):
        if n < EARLY:
            early[n % 4] += 16 * len(src)
            out.append(early[n % 4])
        else:
            at[n % 2] += 16 * len(src)
            out.append(at[n % 2])
    return out


STAGED = stage_counts()


def build(nc, x, ctx_in, wq, wk, gamma, router, gate, up, down, s_gate, s_gate_b, s_up, s_up_b, s_down, s_down_b,
          out, xn_dram):
    es = ExitStack()

    def sb(name, shape, dt=F32):
        return es.enter_context(nc.sbuf_tensor(name, shape, dt))

    def sem(name):
        return es.enter_context(nc.semaphore(name))

    dram = {"gate": gate, "up": up, "down": down, "s_gate": s_gate, "s_up": s_up, "s_down": s_down}

    W = sb("W", [P, E * EW], F16)
    sim = sb("sim", [P, TB, S])
    sigA = sb("sigA", [P, 2, S])
    qT = sb("qT", [P, S])
    kT = sb("kT", [P, S])
    xb = sb("xb", [P, TB, D])
    xn = sb("xn", [P, 2, 2 * D], F16)
    ysh = sb("ysh", [P, 2, D])
    xT = sb("xT", [P, 2, KD, S], F16)
    hS = sb("hS", [P, 2, SC, S], F16)
    sgt = sb("sgt", [P, 2, S])
    stage = sb("stage", [P, 2, SI])
    below = sb("below", [P, S])
    sdb = sb("sdb", [P, 2, D], F16)
    ident = sb("ident", [P, P])
    ident16 = sb("ident16", [P, P], F16)
    row0 = sb("row0", [P, P], F16)
    wqT = sb("wqT", [P, C])
    wkT = sb("wkT", [P, C])
    rwT = sb("rwT", [P, 2, KD, E], F16)
    bias = sb("bias", [P, 2, SC])
    biasS = sb("biasS", [P, 2, SC])
    gam = sb("gam", [P, 4])
    stats = sb("stats", [P, TB, 6])
    mv = sb("mv", [P, TB, 2])
    rstd = sb("rstd", [P, TB])
    pw = sb("pw", [P, 2, TB])
    aff = sb("aff", [P, 2, TB])
    probe = sb("probe", [P, 2, TB])
    lo_ = sb("lo_", [P, 2, TB])
    hi_ = sb("hi_", [P, 2, TB])
    dif = sb("dif", [P, 2, TB])
    nprobe = sb("nprobe", [P, TB])
    msk = sb("msk", [P, 2, TB])
    bad = sb("bad", [P, 4])
    badi = sb("badi", [P, 1], I32)
    top = sb("top", [P, TB, 8])
    pick = sb("pick", [P, TB, 8])
    thr = sb("thr", [P, TB])
    rank8 = sb("rank8", [P, 8])
    lg = sb("lg", [P, NT, E])
    mx = sb("mx", [P, NT, 8])
    mxi = sb("mxi", [P, NT, 8], U32)

    simf = sim[:, :, :].rearrange("p a b -> p (a b)")
    oneh = simf[:, 0:RING * P].rearrange("p (a b) -> p a b", a=RING)
    valh = simf[:, RING * P:RING * (P + 2 * BLOCKS)].rearrange("p (a k b) -> p a k b", a=RING, k=2)
    xg = [t[:, :].bitcast(F16) for t in (qT, kT)]
    ylast = xn[:, :, :].bitcast(F32)
    early = hS[:, :, :, :].rearrange("p s c t -> p (s c t)").bitcast(F32)[:, 0:4 * SI].rearrange("p (a n) -> p a n", a=4)
    y2 = xb[:, 0:2, :]
    h2 = xb[:, 2:4, 0:I]
    sg2 = sgt[:, :, 0:I]
    xT2 = xT[:, :, :, :].rearrange("p s c t -> p (s c t)")[:, 0:4 * KD * P].rearrange("p (a s c t) -> p a s c t", a=2, s=2, c=KD)
    hT2 = hS[:, :, 0:DC, 0:2 * P].rearrange("p s c (a t) -> p s c a t", a=2)
    rt = sigA[:, :, :].rearrange("p a b -> p (a b)")

    def rv(at, n):
        return rt[:, at:at + n]

    iota = rv(0, P)
    io8 = rv(128, 8)
    tok1 = rv(136, NT)
    ef = rv(152, 2 * NT).rearrange("p (k g) -> p k g", k=2)
    wt = rv(184, 2 * NT).rearrange("p (k g) -> p k g", k=2)
    sel = rv(216, 2 * NT * E).rearrange("p (k g e) -> p k g e", k=2, g=NT)
    slotr = rv(472, NT * E).rearrange("p (g e) -> p g e", g=NT)
    prod = below[:, 0:2 * NT * E].rearrange("p (k g e) -> p k g e", k=2, g=NT)
    pos = rv(600, 2 * NT).rearrange("p (k g) -> p k g", k=2)
    posi = rv(632, 2 * NT).bitcast(I32)
    lowi = rv(664, 2 * NT).bitcast(I32)
    higi = rv(696, 2 * NT).bitcast(I32)
    lowf = rv(728, 2 * NT).rearrange("p (k g) -> p k g", k=2)
    higf = rv(760, 2 * NT).rearrange("p (k g) -> p k g", k=2)
    cnt = rv(792, E)
    nblk = rv(800, E)
    ends = rv(808, E)
    first = rv(816, E)
    one8 = rv(824, E)
    k128 = rv(832, 16)
    dumf = rv(848, 1)
    base_f = rv(849, BLOCKS)
    selsum = ysh[:, 0, 0:64].bitcast(F16)
    upper = ysh[:, 0, 64:128].bitcast(F16)
    ones16 = ysh[:, 0, 128:192].bitcast(F16)
    cmp16 = ysh[:, 0, 192:320].rearrange("p (e k) -> p e k", e=E)
    blkc = ysh[:, 1, 0:BLOCKS * E].rearrange("p (j e) -> p j e", j=BLOCKS)
    tab = ysh[:, 1, 320:320 + 2 * BLOCKS].rearrange("p (k j) -> p k j", k=2)
    zer = ysh[:, 1, 400:400 + BLOCKS]
    wcol = sb("wcol", [P, BLOCKS])
    idx = sb("idx", [P, BLOCKS], I32)
    wbase = sb("wbase", [P, BLOCKS], I32)
    gidx = sb("gidx", [P, 2], I32)
    sidx = sb("sidx", [P, 2], I32)

    above = below[:, :].bitcast(mybir.dt.uint8).rearrange("p (t s) -> p t s", t=TB)
    signs = sb("signs", [P, ACT_TILES, S // 2], mybir.dt.uint16)[:, :, :].rearrange("p a s -> p (a s)").bitcast(mybir.dt.int8).rearrange("p (a s) -> p a s", a=ACT_TILES)

    bank = [es.enter_context(nc.psum_tensor(f"bank{i}", [P, 512], F32)) for i in range(8)]

    d_w = sem("d_w")
    d_in = sem("d_in")
    d_early = [sem(f"d_early{i}") for i in range(4)]
    d_ctx = sem("d_ctx")
    d_x = sem("d_x")
    d_x1 = sem("d_x1")
    d_zero = sem("d_zero")
    d_xn = [sem(f"d_xn{i}") for i in range(2)]
    d_y = [sem(f"d_y{i}") for i in range(2)]
    d_stage = [sem(f"d_stage{i}") for i in range(2)]
    d_xg = [sem(f"d_xg{i}") for i in range(2)]
    d_sc = [sem(f"d_sc{i}") for i in range(2)]
    s_const = sem("s_const")
    s_zero = sem("s_zero")
    s_chain = sem("s_chain")
    s_pool = sem("s_pool")
    s_fall = sem("s_fall")
    s_wT = sem("s_wT")
    s_wTc = sem("s_wTc")
    s_rw = sem("s_rw")
    s_gam = sem("s_gam")
    s_cT = sem("s_cT")
    s_cTc = sem("s_cTc")
    s_sim = sem("s_sim")
    s_simc = sem("s_simc")
    s_sigA = sem("s_sigA")
    s_A = sem("s_A")
    s_AT = sem("s_AT")
    s_x1 = sem("s_x1")
    s_var = sem("s_var")
    s_rstd = sem("s_rstd")
    s_bad = sem("s_bad")
    s_badr = sem("s_badr")
    s_xn = sem("s_xn")
    s_xnT = sem("s_xnT")
    s_xT = sem("s_xT")
    s_lg = sem("s_lg")
    s_lgc = sem("s_lgc")
    s_gu = sem("s_gu")
    s_sg = sem("s_sg")
    s_t2 = sem("s_t2")
    s_hhi = sem("s_hhi")
    s_hlo = sem("s_hlo")
    s_yps = sem("s_yps")
    s_y = sem("s_y")
    s_ehi = sem("s_ehi")
    s_whi = sem("s_whi")
    s_wlo = sem("s_wlo")
    s_wloD = sem("s_wloD")
    s_cnt = sem("s_cnt")
    s_probe = sem("s_probe")
    s_nhi = sem("s_nhi")
    s_nlo = sem("s_nlo")
    s_top2 = sem("s_top2")
    s_wt = sem("s_wt")
    s_sel = sem("s_sel")
    s_rank = sem("s_rank")
    s_oneh = sem("s_oneh")
    s_tabp = sem("s_tabp")
    s_route = sem("s_route")
    s_x2ps = sem("s_x2ps")
    s_x2 = sem("s_x2")
    s_gu2 = sem("s_gu2")
    s_sig2 = sem("s_sig2")
    s_h2 = sem("s_h2")
    s_h2ps = sem("s_h2ps")
    s_h2hi = sem("s_h2hi")
    s_h2lo = sem("s_h2lo")
    s_y2ps = sem("s_y2ps")
    s_y2 = sem("s_y2")
    s_gi = sem("s_gi")
    s_held = sem("s_held")
    s_si = sem("s_si")

    block = es.enter_context(nc.Block())
    N_CONST = 12

    @block.sync
    def _(sp):
        sp.dma_start(below[:, 0:C], wq).then_inc(d_w, 16)
        sp.dma_start(below[:, C:2 * C], wk).then_inc(d_w, 16)
        sp.dma_start(kT[:, :].rearrange("p (t c) -> p t c", t=TB), ctx_in[0].rearrange("(t p) c -> p t c", p=P)).then_inc(d_ctx, 16)

        def load_early(n):
            if n >= 4:
                sp.wait_ge(s_wloD, n - 3)
            (name, e, row, cols), = UNITS[n][0]
            sp.dma_start(early[:, n % 4, 0:cols], dram[name][row:row + P, :]).then_inc(d_early[n % 4], 16)

        for n in range(4):
            load_early(n)
        sp.dma_start(gam[:, 0:1], gamma.to_broadcast([P, 1])).then_inc(d_in, 16)
        sp.dma_start(ysh[0:E, 0, :], router).then_inc(d_in, 16)
        sp.dma_start(ysh[0:1, 1, :], s_down_b).then_inc(d_in, 16)
        for n, v in enumerate((s_gate_b, s_up_b)):
            for q in range(SC):
                sp.dma_start(bias[:, n, q:q + 1], v[SH_ROWS[q]:SH_ROWS[q] + P, :]).then_inc(d_in, 16)
        sp.dma_start(xb[:, :, :], x[0].rearrange("(t p) d -> p t d", p=P)).then_inc(d_x, 16)
        units = iter(range(EARLY, len(UNITS)))

        def load_units(k):
            for _ in range(k):
                n = next(units)
                if n - 2 >= LAST:
                    sp.wait_ge(s_wloD, EARLY + n - 2 - LAST + 1)
                elif n - 2 >= EARLY:
                    sp.wait_ge(s_wlo, n - 2 - EARLY + 1)
                at = 0
                for name, e, row, cols in UNITS[n][0]:
                    src = dram[name] if e is None else dram[name][e]
                    sp.dma_start(stage[:, n % 2, at:at + cols], src[row:row + P, :]).then_inc(d_stage[n % 2], 16)
                    at += cols

        load_units(2)
        load_early(4)
        load_early(5)
        load_units(2)
        load_early(6)
        load_early(7)
        sp.wait_ge(s_zero, 1)
        sp.dma_start(xn_dram[DUMMY:DUMMY + P, :], xn[:, 0, :]).then_inc(d_zero, 16)
        sp.dma_start(out[DUMMY:DUMMY + P, :], ylast[:, 0, :]).then_inc(d_zero, 16)
        for b in range(NB):
            if b + 1 < NB:
                sp.wait_ge(s_sim, TB * (b + 1))
                sp.dma_start(kT[:, :].rearrange("p (t c) -> p t c", t=TB), ctx_in[b + 1].rearrange("(t p) c -> p t c", p=P)).then_inc(d_ctx, 16)
            after = max(UNITS_AT[b][3] - 2, 0)
            load_units(IN_WINDOW[b] - (4 if b == 0 else 0) - after)
            for t in range(TB):
                g = TB * b + t
                sp.wait_ge(s_x1, g + 1)
                sp.dma_start(out[g * P:(g + 1) * P, :], xb[:, t, :]).then_inc(d_x1, 16)
            for t in range(TB):
                g = TB * b + t
                sp.wait_ge(s_nlo, g + 1)
                sp.dma_start(xn_dram[g * P:(g + 1) * P, :], xn[:, t % 2, :]).then_inc(d_xn[t % 2], 16)
            load_units(after)
            if b + 1 < NB:
                sp.dma_start(xb[:, :, :], x[b + 1].rearrange("(t p) d -> p t d", p=P)).then_inc(d_x, 16)
        load_units(2 * PER_EXPERT)
        sp.wait_ge(d_x1, 16 * NT)
        for i in range(2):
            sp.wait_ge(d_xn[i], 16 * NT // 2)
        sp.wait_ge(d_zero, 32)

    @block.gpsimd
    def _(pool):
        chain = [0]

        def link(ins):
            chain[0] += 1
            ins.then_inc(s_pool, 1)
            pool.wait_ge(s_pool, chain[0])

        link(pool.memset(ident[:, :], 0.0))
        pool.affine_select(out=ident[:, :], in_=ident[:, :], compare_op=ALU.not_equal, fill=1.0, base=0,
                           pattern=[[-1, P]], channel_multiplier=1).then_inc(s_const, 1)
        pool.wait_ge(s_const, 1)
        pool.tensor_copy(ident16[:, :], ident[:, :]).then_inc(s_const, 1)
        link(pool.memset(row0[:, :], 0.0))
        pool.memset(row0[0:1, :], 1.0).then_inc(s_const, 1)
        pool.iota(rank8[:, :], [[1, 8]], base=1, channel_multiplier=0, allow_small_or_imprecise_dtypes=True).then_inc(s_const, 1)
        pool.memset(pw[:, 1, :], -0.5).then_inc(s_const, 1)
        pool.wait_ge(s_const, 5)

        units = iter(range(EARLY, LAST))

        def split_lo(n):
            src, hi, lo, cols, zero = UNITS[n]
            st = stage[:, n % 2, 0:cols]
            pool.wait_ge(s_whi, n - EARLY + 1)
            link(pool.tensor_scalar(st, st, WS, 1.0, ALU.mult, ALU.mult))
            last = pool.tensor_tensor(W[:, lo:lo + cols], st, W[:, hi:hi + cols], ALU.subtract)
            if zero:
                link(last)
                link(pool.memset(W[0:zero, hi:hi + cols], 0.0))
                last = pool.memset(W[0:zero, lo:lo + cols], 0.0)
            last.then_inc(s_wlo, 1)

        def split_some(k):
            for _ in range(k):
                split_lo(next(units))

        def power(n):
            pool.wait_ge(s_var, n + 1)
            pool.tensor_tensor(rstd[:, :], pw[:, 0, :], pw[:, 1, :], ALU.pow).then_inc(s_rstd, 1)

        def add_shared(b, t, src):
            g = TB * b + t
            pool.wait_ge(s_y, g + 1)
            pool.wait_ge(d_x1, 16 * TB * (b + 1))
            pool.dma_start(out[g * P:(g + 1) * P, :], src[:, t % 2, :], accum_op=ALU.add).then_inc(d_y[t % 2], 16)

        def xn_lo(b, t):
            g = TB * b + t
            pool.wait_ge(s_nhi, g + 1)
            pool.tensor_tensor(xn[:, t % 2, D:2 * D], xb[:, t, :], xn[:, t % 2, 0:D], ALU.subtract).then_inc(s_nlo, 1)

        for b in range(NB):
            counted, chunked, masked, ended = UNITS_AT[b]
            power(3 * b)
            split_some(counted[0])
            power(3 * b + 1)
            split_some(sum(counted[1:]) + sum(chunked))
            pool.wait_ge(s_bad, b + 1)
            pool.partition_all_reduce(bad[:, 1:2], bad[:, 0:1], P, bass.bass_isa.ReduceOp.max).then_inc(s_badr, 1)
            split_some(masked)
            if b:
                add_shared(b - 1, 0, ysh)
                add_shared(b - 1, 1, ysh)
            power(3 * b + 2)
            xn_lo(b, 0)
            xn_lo(b, 1)
            if b:
                add_shared(b - 1, 2, ysh)
            xn_lo(b, 2)
            xn_lo(b, 3)
            if b:
                add_shared(b - 1, 3, ysh)
            split_some(ended)

        pool.wait_ge(s_A, NT)
        pool.iota(iota, [[1, P]], base=0, channel_multiplier=0, allow_small_or_imprecise_dtypes=True).then_inc(s_const, 1)
        pool.iota(io8, [[1, E]], base=0, channel_multiplier=0, allow_small_or_imprecise_dtypes=True).then_inc(s_const, 1)
        pool.iota(tok1, [[P, NT]], base=1, channel_multiplier=1, allow_small_or_imprecise_dtypes=True).then_inc(s_const, 1)
        pool.iota(k128, [[P, 16]], base=0, channel_multiplier=0, allow_small_or_imprecise_dtypes=True).then_inc(s_const, 1)
        pool.iota(dumf, [[0, 1]], base=DUMMY + 1, channel_multiplier=1, allow_small_or_imprecise_dtypes=True).then_inc(s_const, 1)
        pool.memset(one8, 1.0).then_inc(s_const, 1)
        for i in range(2):
            pool.wait_ge(d_y[i], 16 * (NT - TB) // 2)
        link(pool.memset(upper, 1.0))
        pool.memset(ones16, 1.0)
        pool.affine_select(out=upper, in_=upper, compare_op=ALU.is_gt, fill=0.0, base=0, pattern=[[1, P]],
                           channel_multiplier=-1).then_inc(s_const, 1)

        split_some(PER_EXPERT)
        for t in range(TB):
            add_shared(NB - 1, t, ylast)

        def gather(j, p):
            link2(pool.tensor_copy(gidx[:, p:p + 1], idx[:, bass.ds(j, 1)]), s_gi, j + 1)
            pool.indirect_dma_start(out=xg[p], out_offset=None, in_=xn_dram,
                                    in_offset=bass.IndirectOffsetOnAxis(ap=gidx[:, p:p + 1], axis=0)).then_inc(d_xg[p], 16)

        def scatter(j, m, p):
            if isinstance(j, int) and j == 0:
                for i in range(2):
                    pool.wait_ge(d_y[i], 16 * NT // 2)
            pool.wait_ge(s_y2, j + 1)
            if not (isinstance(j, int) and j == 0):
                pool.wait_ge(d_sc[1 - p], 16 * (m + 1) if p else 16 * m)
            link2(pool.tensor_copy(sidx[:, p:p + 1], idx[:, bass.ds(j, 1)]), s_si, j + 1)
            pool.indirect_dma_start(out=out, out_offset=bass.IndirectOffsetOnAxis(ap=sidx[:, p:p + 1], axis=0),
                                    in_=y2[:, p, :], in_offset=None, compute_op=ALU.add).then_inc(d_sc[p], 16)

        def link2(ins, s, v):
            ins.then_inc(s, 1)
            pool.wait_ge(s, v)
            pool.sem_inc(s_held, 1)

        pool.wait_ge(s_route, 1)
        for i in range(2):
            pool.wait_ge(d_xn[i], 16 * NT // 2)
        pool.wait_ge(d_zero, 32)
        gather(0, 0)
        gather(1, 1)

        def step(j, m, p, fetch=True):
            if fetch:
                pool.wait_ge(s_x2ps, j + 1)
                gather(j + 2, p)
            if not (isinstance(j, int) and j == 0):
                scatter(j - 1, m if p else m - 1, 1 - p)

        run_blocks(pool, step)
        scatter(BLOCKS - 1, (BLOCKS - 1) // 2, (BLOCKS - 1) % 2)
        for i in range(2):
            pool.wait_ge(d_sc[i], 16 * (BLOCKS // 2 + (1 - i) * (BLOCKS % 2)))

    @block.scalar
    def _(act):
        loads = iter(range(EARLY, len(UNITS)))

        def split_hi(n):
            src, hi, lo, cols, zero = UNITS[n]
            if n == LATE:
                act.wait_ge(s_gu, NB * SC)
            if n == LAST:
                act.wait_ge(s_yps, NT)
            act.wait_ge(d_stage[n % 2], STAGED[n])
            act.activation(W[:, hi:hi + cols], stage[:, n % 2, 0:cols], ACT.Copy, scale=WS).then_inc(s_whi, 1)

        def split_some(k):
            for _ in range(k):
                split_hi(next(loads))

        act.wait_ge(s_wT, 1)
        act.activation(wqT[:, :], bank[0][:, 0:C], ACT.Copy).then_inc(s_wTc, 1)
        act.activation(wkT[:, :], bank[0][:, C:2 * C], ACT.Copy).then_inc(s_wTc, 1)

        def early_hi(n):
            src, hi, lo, cols, zero = UNITS[n]
            act.wait_ge(d_early[n % 4], STAGED[n])
            act.activation(W[:, hi:hi + cols], early[:, n % 4, 0:cols], ACT.Copy, scale=WS).then_inc(s_ehi, 1)

        def small_inputs():
            act.wait_ge(s_wT, 2)
            act.activation(rwT[:, 0, :, :], bank[2][:, 0:KD * E].rearrange("p (c e) -> p c e", c=KD), ACT.Copy, scale=WS).then_inc(s_wTc, 1)
            act.wait_ge(d_in, 16 * (3 + 2 * SC))
            act.wait_ge(s_zero, 2)
            act.activation(sdb[0:1, 0, :], ysh[0:1, 1, :], ACT.Copy, scale=HW).then_inc(s_wTc, 1)
            act.activation(gam[:, 1:2], gam[:, 0:1], ACT.Sigmoid).then_inc(s_gam, 1)

        def context_T(b):
            act.wait_ge(s_cT, 2 * b + 1)
            act.activation(qT[:, :], bank[0][:, :], ACT.Copy).then_inc(s_cTc, 1)

        def proj(b):
            act.wait_ge(s_cT, 2 * b + 2)
            act.activation(qT[:, :], bank[0][:, :], ACT.Copy).then_inc(s_cTc, 1)
            act.activation(kT[:, :], bank[1][:, :], ACT.Copy).then_inc(s_cTc, 1)

        def scores(b, t):
            g = TB * b + t
            act.wait_ge(s_sim, g + 1)
            if b:
                act.wait_ge(s_AT, TB * b)
                act.wait_ge(s_x1, TB * (b - 1) + t + 1)
            act.activation(sim[:, t, :], bank[t % 2][:, :], ACT.Copy).then_inc(s_simc, 1)

        def sig_scores(b, t):
            g = TB * b + t
            act.wait_ge(s_simc, g + 1)
            if g >= 2:
                act.wait_ge(s_A, g - 1)
            act.activation(sigA[:, t % 2, :], sim[:, t, :], ACT.Sigmoid, scale=1.0 / ((C / HEADS) ** 0.5 * HEADS)).then_inc(s_sigA, 1)

        def sh_sig(b, q):
            n = SC * b + q
            act.wait_ge(s_gu, n + 1)
            if n >= 2:
                act.wait_ge(s_hlo, n - 1)
            act.activation(sgt[:, q % 2, :], bank[4 + 2 * (q % 2)][:, :], ACT.Silu, bias=bias[:, 0, q:q + 1],
                           scale=1.0 / XW).then_inc(s_sg, 1)

        def sh_hi(b, q):
            n = SC * b + q
            act.wait_ge(s_t2, n + 1)
            if b and q == 0:
                act.wait_ge(s_yps, TB * b)
            act.activation(hS[:, 0, q, :], sgt[:, q % 2, :], ACT.Copy, scale=HS / XW).then_inc(s_hhi, 1)

        def xn_hi(b, t):
            g = TB * b + t
            act.wait_ge(s_xn, g + 1)
            if g >= 2:
                act.wait_ge(d_xn[t % 2], 16 * (g // 2))
                act.wait_ge(s_xnT, g - 1)
            else:
                act.wait_ge(d_zero, 32)
            act.activation(xn[:, t % 2, 0:D], xb[:, t, :], ACT.Copy).then_inc(s_nhi, 1)

        def x_T(b, t):
            g = TB * b + t
            act.wait_ge(s_xnT, g + 1)
            if b and t == 0:
                act.wait_ge(s_gu, SC * b)
            act.activation(xT[:, :, :, t * P:(t + 1) * P].rearrange("p s c t -> p (s c) t"),
                           bank[2 + t % 2][:, :].bitcast(F16).rearrange("p (c t) -> p c t", c=2 * KD), ACT.Copy).then_inc(s_xT, 1)

        def count(b, it):
            act.wait_ge(s_probe, PROBES * b + it + 1)
            for t in range(TB - ACT_TILES, TB):
                act.activation(signs[:, t - (TB - ACT_TILES), :], sim[:, t, :], ACT.Sign, bias=nprobe[:, t:t + 1],
                               accum_out=probe[:, 1, t:t + 1]).then_inc(s_cnt, 1)

        def shared_out(b, t, dst):
            g = TB * b + t
            act.wait_ge(s_yps, g + 1)
            if dst is ysh and g >= 2 or t >= 2:
                act.wait_ge(d_y[t % 2], 16 * (g // 2))
            act.activation(dst[:, t % 2, :], bank[4 + t][:, :], ACT.Copy, scale=1.0 / HW).then_inc(s_y, 1)

        context_T(0)
        proj(0)
        for t in range(TB):
            scores(0, t)
        small_inputs()
        for n in range(4):
            early_hi(n)
        for b in range(NB):
            counted, chunked, masked, ended = UNITS_AT[b]
            sig_scores(b, 0)
            sig_scores(b, 1)
            for it in range(PROBES):
                count(b, it)
                split_some(counted[it])
                if b == 0 and it in (1, 2):
                    early_hi(2 * it + 2)
                    early_hi(2 * it + 3)
                if b:
                    sh_sig(b - 1, it)
                    if it:
                        sh_hi(b - 1, it - 1)
                    split_some(chunked[it])
                if b + 1 < NB and it == 1:
                    context_T(b + 1)
                if b + 1 < NB and it == 2:
                    proj(b + 1)
            if b:
                sh_sig(b - 1, SC - 1)
                sh_hi(b - 1, SC - 2)
                sh_hi(b - 1, SC - 1)
            sig_scores(b, 2)
            sig_scores(b, 3)
            split_some(masked)
            if b:
                shared_out(b - 1, 0, ysh)
                shared_out(b - 1, 1, ysh)
            if b + 1 < NB:
                for t in range(TB):
                    scores(b + 1, t)
            xn_hi(b, 0)
            xn_hi(b, 1)
            if b:
                shared_out(b - 1, 2, ysh)
            x_T(b, 0)
            x_T(b, 1)
            xn_hi(b, 2)
            xn_hi(b, 3)
            if b:
                shared_out(b - 1, 3, ysh)
            x_T(b, 2)
            x_T(b, 3)
            split_some(ended)
        sh_sig(NB - 1, 0)
        for q in range(SC):
            if q + 1 < SC:
                sh_sig(NB - 1, q + 1)
            if q == 0:
                act.wait_ge(s_top2, 1)
                act.activation(wt[:, 0, :], wt[:, 1, :], ACT.Sigmoid, scale=1.0 / XW).then_inc(s_wt, 1)
                act.wait_ge(s_wt, 1)
                act.activation(wt[:, 1, :], wt[:, 1, :], ACT.Sigmoid, scale=-1.0 / XW).then_inc(s_wt, 1)
            sh_hi(NB - 1, q)
        split_some(PER_EXPERT)
        act.wait_ge(s_xnT, NT)
        for i in range(2):
            act.wait_ge(d_xn[i], 16 * NT // 2)
        for t in range(TB):
            shared_out(NB - 1, t, ylast)
        split_some(PER_EXPERT)

        def routed_sig(j, p):
            act.wait_ge(s_gu2, j + 1)
            act.activation(sg2[:, p, :], bank[4 + 2 * p][:, 0:I], ACT.Silu, scale=1.0 / XW).then_inc(s_sig2, 1)

        def routed_h(j, p):
            act.wait_ge(s_h2ps, j + 1)
            if not (isinstance(j, int) and j < 2):
                act.wait_ge(s_y2ps, j - 1)
            act.activation(hT2[:, 0, :, p, :], bank[1][:, 0:DC * P].rearrange("p (c t) -> p c t", c=DC), ACT.Copy).then_inc(s_h2hi, 1)

        def routed_y(j, m, p):
            act.wait_ge(s_y2ps, j + 1)
            if not (isinstance(j, int) and j < 2):
                act.wait_ge(d_sc[p], 16 * m)
            act.activation(y2[:, p, :], bank[2 + p][:, :], ACT.Copy, scale=wcol[:, bass.ds(j, 1)]).then_inc(s_y2, 1)

        def step(j, m, p, fetch=True):
            first_block = isinstance(j, int) and j == 0
            if not first_block:
                routed_h(j - 1, 1 - p)
            routed_sig(j, p)
            if not first_block:
                routed_y(j - 1, m if p else m - 1, 1 - p)

        act.wait_ge(s_route, 1)
        run_blocks(act, step)
        j = BLOCKS - 1
        routed_h(j, j % 2)
        routed_y(j, j // 2, j % 2)

    @block.tensor
    def _(pe):
        pe.wait_ge(s_const, 1)
        pe.wait_ge(d_w, 32)
        pe.transpose(bank[0][:, 0:C], below[:, 0:C], ident[:, :])
        pe.transpose(bank[0][:, C:2 * C], below[:, C:2 * C], ident[:, :]).then_inc(s_wT, 1)

        def transpose_router():
            pe.wait_ge(d_in, 16 * (3 + 2 * SC))
            for c in range(KD):
                last = pe.transpose(bank[2][:, c * E:(c + 1) * E], ysh[0:E, 0, c * P:(c + 1) * P], ident[0:E, 0:E])
            last.then_inc(s_wT, 1)

        def context_T(b):
            pe.wait_ge(d_ctx, 16 * (b + 1))
            if b == 0:
                pe.wait_ge(s_wTc, 2)
            else:
                pe.wait_ge(s_simc, TB * b)
                if b > 1:
                    pe.wait_ge(s_lgc, b - 1)
            for t in range(TB):
                last = pe.transpose(bank[0][:, t * P:(t + 1) * P], kT[:, t * C:(t + 1) * C], ident[:, :])
            last.then_inc(s_cT, 1)

        def proj(b):
            pe.wait_ge(s_cTc, 3 * b + 1)
            pe.matmul(bank[0][:, :], wqT[:, :], qT[:, :], start=True, stop=True)
            pe.matmul(bank[1][:, :], wkT[:, :], qT[:, :], start=True, stop=True).then_inc(s_cT, 1)

        def scores(b, t):
            g = TB * b + t
            if t == 0:
                pe.wait_ge(s_cTc, 3 * b + 3)
            if t < 2:
                if b:
                    pe.wait_ge(s_x1, TB * (b - 1) + t + 3)
            else:
                pe.wait_ge(s_simc, g - 1)
            pe.matmul(bank[t % 2][:, :], qT[:, t * P:(t + 1) * P], kT[:, :], start=True, stop=True).then_inc(s_sim, 1)

        def transpose_A(b, t):
            g = TB * b + t
            if t == 0:
                pe.wait_ge(s_A, TB * (b + 1))
                if b:
                    pe.wait_ge(s_xT, TB * b)
                else:
                    pe.wait_ge(s_rw, 1)
                pe.wait_ge(s_cTc, 3 * min(b + 2, NB))
                if b:
                    pe.wait_ge(s_lgc, b)
            for m in range(TB):
                last = pe.transpose(bank[AT_BANK[t]][:, m * P:(m + 1) * P], sim[:, m, t * P:(t + 1) * P], ident[:, :])
            last.then_inc(s_AT, 1)

        def transpose_xn(b, t):
            g = TB * b + t
            pe.wait_ge(s_nlo, g + 1)
            if t >= 2:
                pe.wait_ge(s_xT, g - 1)
            o = bank[2 + t % 2][:, :].bitcast(F16)
            for c in range(2 * KD):
                last = pe.transpose(o[:, c * P:(c + 1) * P], xn[:, t % 2, c * P:(c + 1) * P], ident16[:, :])
            last.then_inc(s_xnT, 1)

        def logits(b):
            pe.wait_ge(s_xT, TB * (b + 1))
            pe.wait_ge(s_simc, min(TB * (b + 2), NT))
            for t in range(TB):
                o = bank[0][:, t * E:(t + 1) * E]
                for c in range(KD):
                    xh, xl = (xT[:, s, c, t * P:(t + 1) * P] for s in range(2))
                    pe.matmul(o, xh, rwT[:, 0, c, :], start=(c == 0), stop=False)
                    pe.matmul(o, xh, rwT[:, 1, c, :], start=False, stop=False)
                    last = pe.matmul(o, xl, rwT[:, 0, c, :], start=False, stop=(c == KD - 1))
            last.then_inc(s_lg, 1)

        def shared_up(b, q):
            n = SC * b + q
            if n == 0:
                pe.wait_ge(s_wloD, EARLY)
            if q == 0:
                pe.wait_ge(s_xT, TB * (b + 1))
            if q >= 2:
                pe.wait_ge(s_t2, n - 1)
            elif b:
                pe.wait_ge(s_y, TB * b - 2 + 2 * q)
            for w in range(2):
                o = bank[4 + 2 * (q % 2) + w][:, :]
                for c in range(KD):
                    at = (2 * c + w) * SI + SH_ROWS[q]
                    wh, wl = W[:, SG_HI + at:SG_HI + at + P], W[:, SG_LO + at:SG_LO + at + P]
                    pe.matmul(o, wh, xT[:, 0, c, :], start=(c == 0), stop=False)
                    pe.matmul(o, wh, xT[:, 1, c, :], start=False, stop=False)
                    last = pe.matmul(o, wl, xT[:, 0, c, :], start=False, stop=(c == KD - 1))
            last.then_inc(s_gu, 1)

        def shared_down(b, t):
            if b == 0 and t == 0:
                pe.wait_ge(s_wlo, SC)
            pe.wait_ge(s_hlo, SC * (b + 1))
            o = bank[4 + t][:, :]
            pe.matmul(o, row0[:, :], sdb[:, 0, :], start=True, stop=False)
            pe.matmul(o, row0[:, :], sdb[:, 1, :], start=False, stop=False)
            for q in range(SC):
                hh, hl = (hS[:, s, q, t * P:(t + 1) * P] for s in range(2))
                wh, wl = W[:, SD_HI + q * D:SD_HI + (q + 1) * D], W[:, SD_LO + q * D:SD_LO + (q + 1) * D]
                pe.matmul(o, hh, wh, start=False, stop=False)
                pe.matmul(o, hh, wl, start=False, stop=False)
                last = pe.matmul(o, hl, wh, start=False, stop=(q == SC - 1))
            last.then_inc(s_yps, 1)

        def rank():
            pe.wait_ge(s_sel, 1)
            pe.wait_ge(s_const, N_CONST)
            pe.matmul(bank[2][:, 0:NT * E], upper, selsum, start=True, stop=False)
            for g in range(NT - 1):
                k = NT - 1 - g
                pe.matmul(bank[2][:, (g + 1) * E:NT * E].rearrange("p (g e) -> p g e", g=k), ones16,
                          selsum[:, g * E:(g + 1) * E].rearrange("p (g e) -> p g e", g=1).to_broadcast([P, k, E]),
                          start=False, stop=(g == NT - 2))
            for g in range(NT):
                last = pe.matmul(bank[3][:, 0:E], ones16, selsum[:, g * E:(g + 1) * E], start=(g == 0), stop=(g == NT - 1))
            last.then_inc(s_rank, 1)

        def table(n0, n1):
            for n in range(n0, n1):
                pe.wait_ge(s_oneh, n + 1)
                if n == 0:
                    pe.wait_ge(s_lgc, NB)
                pe.matmul(bank[0][:, 0:2 * BLOCKS], oneh[:, n % RING, :],
                          valh[:, n % RING, :, :].rearrange("p k b -> p (k b)"),
                          start=(n == 0), stop=(n == 2 * NT - 1)).then_inc(s_tabp, 1)

        context_T(0)
        proj(0)
        for t in range(TB):
            scores(0, t)
        transpose_router()
        for b in range(NB):
            if b:
                for q in range(SC):
                    shared_up(b - 1, q)
                    if b + 1 < NB and q == 1:
                        context_T(b + 1)
                    if b + 1 < NB and q == 2:
                        proj(b + 1)
                shared_down(b - 1, 0)
            else:
                context_T(1)
                proj(1)
            for t in range(TB):
                transpose_A(b, t)
            if b:
                shared_down(b - 1, 1)
            if b + 1 < NB:
                for t in range(TB):
                    scores(b + 1, t)
            if b:
                shared_down(b - 1, 2)
            transpose_xn(b, 0)
            transpose_xn(b, 1)
            if b:
                shared_down(b - 1, 3)
            transpose_xn(b, 2)
            transpose_xn(b, 3)
            logits(b)
        for q in range(SC):
            shared_up(NB - 1, q)
            if q == 1:
                rank()
            if q >= 3:
                table(*TABLE_AT[q - 3])
        for t in range(TB):
            shared_down(NB - 1, t)

        def routed_x(j, m, p):
            pe.wait_ge(d_xg[p], 16 * (m + 1))
            if isinstance(j, int) and j == 0:
                pe.wait_ge(s_route, 1)
            else:
                pe.wait_ge(s_x2, j)
            o = bank[0][:, :].bitcast(F16)
            for c in range(2 * KD):
                last = pe.transpose(o[:, c * P:(c + 1) * P], xg[p][:, c * P:(c + 1) * P], ident16[:, :])
            last.then_inc(s_x2ps, 1)

        def routed_up(j, p, at):
            pe.wait_ge(s_x2, j + 1)
            if not (isinstance(j, int) and j < 2):
                pe.wait_ge(s_h2, j - 1)
            elif j == 0:
                pe.wait_ge(s_y, NT)
            og, ou = bank[4 + 2 * p][:, 0:I], bank[5 + 2 * p][:, 0:I]
            for c in range(KD):
                hi, lo = at + (GU_HI + c * GU), at + (GU_LO + c * GU)
                xh, xl = xT2[:, p, 0, c, :], xT2[:, p, 1, c, :]
                f, z = c == 0, c == KD - 1
                pe.matmul(og, xh, W[:, bass.ds(hi, I)], start=f, stop=False)
                pe.matmul(ou, xh, W[:, bass.ds(hi + I, I)], start=f, stop=False)
                pe.matmul(og, xh, W[:, bass.ds(lo, I)], start=False, stop=False)
                pe.matmul(ou, xh, W[:, bass.ds(lo + I, I)], start=False, stop=False)
                pe.matmul(og, xl, W[:, bass.ds(hi, I)], start=False, stop=z)
                last = pe.matmul(ou, xl, W[:, bass.ds(hi + I, I)], start=False, stop=z)
            last.then_inc(s_gu2, 1)

        def routed_hT(j, p):
            pe.wait_ge(s_h2, j + 1)
            if not (isinstance(j, int) and j == 0):
                pe.wait_ge(s_h2lo, j)
            for c in range(DC):
                last = pe.transpose(bank[1][:, c * P:(c + 1) * P], h2[:, p, DOWN_ROWS[c]:DOWN_ROWS[c] + P], ident[:, :])
            last.then_inc(s_h2ps, 1)

        def routed_down(j, p, at):
            pe.wait_ge(s_h2lo, j + 1)
            if not (isinstance(j, int) and j < 2):
                pe.wait_ge(s_y2, j - 1)
            o = bank[2 + p][:, :]
            for c in range(DC):
                hh, hl = hT2[:, 0, c, p, :], hT2[:, 1, c, p, :]
                wh, wl = W[:, bass.ds(at + (DN_HI + c * D), D)], W[:, bass.ds(at + (DN_LO + c * D), D)]
                pe.matmul(o, hh, wh, start=(c == 0), stop=False)
                pe.matmul(o, hh, wl, start=False, stop=False)
                last = pe.matmul(o, hl, wh, start=False, stop=(c == DC - 1))
            last.then_inc(s_y2ps, 1)

        def where(j):
            return pe.value_load(wbase[0:1, bass.ds(j, 1)], min_val=0, max_val=(E - 1) * EW)

        def step(j, m, p, fetch=True):
            first_block = isinstance(j, int) and j == 0
            if not first_block:
                routed_hT(j - 1, 1 - p)
            if first_block or not (isinstance(j, int) and j == BLOCKS - 1):
                routed_x(j + 1, m + (1 if p else 0), 1 - p)
            if first_block:
                pe.wait_ge(s_wlo, BY_POOL)
                pe.wait_ge(s_wloD, EARLY + PER_EXPERT)
            routed_up(j, p, where(j))
            if not first_block:
                routed_down(j - 1, 1 - p, where(j - 1))

        routed_x(0, 0, 0)
        run_blocks(pe, step)
        j = BLOCKS - 1
        routed_hT(j, j % 2)
        routed_down(j, j % 2, where(j))

    @block.vector
    def _(dve):
        chain = [0]

        def link(ins):
            chain[0] += 1
            ins.then_inc(s_chain, 1)
            dve.wait_ge(s_chain, chain[0])

        dve.memset(xn[:, 0, :], 0.0).then_inc(s_zero, 1)
        dve.memset(sdb[:, :, :], 0.0).then_inc(s_zero, 1)

        def weight_lo(n, st):
            src, hi, lo, cols, zero = UNITS[n]
            if n < EARLY:
                dve.wait_ge(s_ehi, n + 1)
            else:
                dve.wait_ge(s_whi, n - EARLY + 1)
            last = dve.scalar_tensor_tensor(W[:, lo:lo + cols], st, WS, W[:, hi:hi + cols], ALU.mult, ALU.subtract)
            if zero:
                link(last)
                link(dve.memset(W[0:zero, hi:hi + cols], 0.0))
                last = dve.memset(W[0:zero, lo:lo + cols], 0.0)
            last.then_inc(s_wloD, 1)

        dve.wait_ge(d_in, 16 * (3 + 2 * SC))
        dve.wait_ge(s_wTc, 4)
        dve.scalar_tensor_tensor(rwT[:, 1, :, :], bank[2][:, 0:KD * E].rearrange("p (c e) -> p c e", c=KD), WS,
                                 rwT[:, 0, :, :], ALU.mult, ALU.subtract)
        dve.scalar_tensor_tensor(sdb[0:1, 1, :], ysh[0:1, 1, :], HW, sdb[0:1, 0, :], ALU.mult, ALU.subtract).then_inc(s_rw, 1)
        dve.tensor_scalar(biasS[:, :, :], bias[:, :, :], XW, None, ALU.mult)
        dve.wait_ge(s_gam, 1)
        dve.wait_ge(s_const, 5)
        dve.tensor_scalar(gam[:, 2:3], gam[:, 1:2], -1.0, 1.0, ALU.mult, ALU.add)
        link(dve.tensor_scalar(gam[:, 3:4], gam[:, 1:2], 0.5, None, ALU.mult))

        def variance(src, n, eps):
            for t in range(TB):
                last = dve.bn_stats(stats[:, t, :], src[:, t, :])
            link(last)
            for t in range(TB):
                last = dve.bn_aggr(mv[:, t, :], stats[:, t, :])
            link(last)
            dve.tensor_scalar(pw[:, 0, :], mv[:, :, 1], eps, None, ALU.add).then_inc(s_var, 1)
            dve.wait_ge(s_rstd, n + 1)

        def threshold_start(b):
            dve.wait_ge(s_simc, TB * (b + 1))
            variance(sim, 3 * b, 1e-30)
            link(dve.tensor_tensor(dif[:, 0, :], mv[:, :, 1], rstd[:, :], ALU.mult))
            dve.scalar_tensor_tensor(probe[:, 0, :], dif[:, 0, :], START_Z, mv[:, :, 0], ALU.mult, ALU.add)
            dve.scalar_tensor_tensor(lo_[:, 0, :], dif[:, 0, :], -SPAN_Z, mv[:, :, 0], ALU.mult, ALU.add)
            dve.scalar_tensor_tensor(hi_[:, 0, :], dif[:, 0, :], SPAN_Z, mv[:, :, 0], ALU.mult, ALU.add)
            dve.memset(lo_[:, 1, :], float(S))
            link(dve.memset(hi_[:, 1, :], 0.0))
            dve.tensor_scalar(nprobe[:, :], probe[:, 0, :], -1.0, None, ALU.mult).then_inc(s_probe, 1)

        def threshold_probe(b, it):
            for t in range(TB - ACT_TILES):
                last = dve.tensor_scalar(above[:, t, :], sim[:, t, :], probe[:, 0, t:t + 1], None, ALU.is_ge, ALU.add,
                                         accum_out=probe[:, 1, t:t + 1])
            link(last)
            dve.wait_ge(s_cnt, ACT_TILES * (PROBES * b + it + 1))
            acts = probe[:, 1, TB - ACT_TILES:TB]
            link(dve.tensor_scalar(acts, acts, 0.5, S / 2, ALU.mult, ALU.add))
            dve.tensor_scalar(msk[:, 0, :], probe[:, 1, :], KTH - WIN / 2, None, ALU.is_ge)
            link(dve.tensor_scalar(msk[:, 1, :], probe[:, 1, :], KTH - WIN / 2, None, ALU.is_lt))
            for k, end in enumerate((lo_, hi_)):
                for w in range(2):
                    last = dve.copy_predicated(end[:, w, :], msk[:, k, :].bitcast(U32), probe[:, w, :])
            link(last)
            if it < PROBES - 1:
                link(dve.tensor_tensor(dif[:, :, :], lo_[:, :, :], hi_[:, :, :], ALU.subtract))
                link(dve.reciprocal(dif[:, 1, :], dif[:, 1, :]))
                link(dve.tensor_tensor(dif[:, 0, :], dif[:, 0, :], dif[:, 1, :], ALU.mult))
                link(dve.scalar_tensor_tensor(dif[:, 0, :], lo_[:, 1, :], KTH - WIN / 2 - 0.5, dif[:, 0, :], ALU.subtract, ALU.mult))
                dve.tensor_tensor(nprobe[:, :], dif[:, 0, :], lo_[:, 0, :], ALU.subtract)
                dve.tensor_tensor(probe[:, 0, :], lo_[:, 0, :], dif[:, 0, :], ALU.subtract).then_inc(s_probe, 1)
                dve.wait_ge(s_probe, PROBES * b + it + 2)

        def threshold_end(b):
            link(dve.tensor_scalar(msk[:, 0, :], lo_[:, 1, :], float(KTH - 1), None, ALU.is_le))
            for w in range(2):
                last = dve.copy_predicated(hi_[:, w, :], msk[:, 0, :].bitcast(U32), lo_[:, w, :])
            link(last)
            for t in range(TB):
                threshold_below(t)
            link(dve.tensor_scalar(dif[:, 0, :], hi_[:, 1, :], -1.0, float(KTH), ALU.mult, ALU.add))
            dve.tensor_scalar(msk[:, 0, :], hi_[:, 1, :], float(KTH - WIN), None, ALU.is_lt)
            link(dve.tensor_scalar(msk[:, 1, :], hi_[:, 1, :], float(KTH - 1), None, ALU.is_gt))
            dve.tensor_reduce(bad[:, 0:1], msk[:, :, :].rearrange("p k t -> p (k t)"), AX.X, ALU.max).then_inc(s_bad, 1)
            for t in range(TB):
                last = dve.scalar_tensor_tensor(pick[:, t, :], rank8[:, :], dif[:, 0, t:t + 1], top[:, t, :], ALU.is_equal, ALU.mult)
            link(last)
            link(dve.tensor_reduce(thr[:, :], pick[:, :, :], AX.X, ALU.add))

        def threshold_below(t):
            if t < TB - ACT_TILES:
                link(dve.tensor_scalar(below[:, :], sim[:, t, :], hi_[:, 0, t:t + 1], -3e38, ALU.is_ge, ALU.mult))
                link(dve.tensor_tensor(below[:, :], below[:, :], sim[:, t, :], ALU.add))
            else:
                link(dve.tensor_scalar(below[:, :], sim[:, t, :], hi_[:, 0, t:t + 1], None, ALU.is_ge, ALU.add,
                                       accum_out=hi_[:, 1, t:t + 1]))
                link(dve.scalar_tensor_tensor(below[:, :], below[:, :], -3e38, sim[:, t, :], ALU.mult, ALU.add))
            link(dve.max(top[:, t, :], below[:, :]))

        def threshold_check(b):
            dve.wait_ge(s_badr, b + 1)
            link(dve.tensor_copy(badi[:, :], bad[:, 1:2]))
            missed = dve.value_load(badi[0:1, 0:1], min_val=0, max_val=1)
            rounds = KTH // 8
            per_tile = 1 + 2 * rounds + 1
            with dve.If(missed > 0):
                for t in range(TB):
                    at = (TB * b + t) * per_tile
                    dve.tensor_copy(below[:, :], sim[:, t, :]).then_inc(s_fall, 1)
                    dve.wait_ge(s_fall, at + 1)
                    with dve.Fori(0, rounds) as r:
                        dve.max(top[:, t, :], below[:, :]).then_inc(s_fall, 1)
                        dve.wait_ge(s_fall, 2 * r + (at + 2))
                        dve.sem_inc(s_held, 1)
                        dve.match_replace(below[:, :], top[:, t, :], below[:, :], -3e38).then_inc(s_fall, 1)
                        dve.wait_ge(s_fall, 2 * r + (at + 3))
                    dve.max(top[:, t, :], below[:, :]).then_inc(s_fall, 1)
                    dve.wait_ge(s_fall, at + per_tile)
                    dve.tensor_copy(thr[:, t:t + 1], top[:, t, KTH - 8 * rounds - 1:KTH - 8 * rounds])
            with dve.Else():
                dve.sem_inc(s_fall, TB * per_tile)
            dve.wait_ge(s_fall, (b + 1) * TB * per_tile)

        def layer_norm_x(b):
            dve.wait_ge(d_x, 16 * (b + 1))
            variance(xb, 3 * b + 1, EPS)
            link(dve.tensor_scalar(aff[:, 0, :], rstd[:, :], gam[:, 2:3], None, ALU.mult))
            link(dve.scalar_tensor_tensor(aff[:, 1, :], mv[:, :, 0], -1.0, aff[:, 0, :], ALU.mult, ALU.mult))
            link(dve.tensor_scalar(aff[:, 0, :], aff[:, 0, :], 1.0, None, ALU.add))
            for t in range(TB):
                last = dve.tensor_scalar(xb[:, t, :], xb[:, t, :], aff[:, 0, t:t + 1], aff[:, 1, t:t + 1], ALU.mult, ALU.add)
            link(last)

        def mask(b):
            for t in range(TB):
                g = TB * b + t
                dve.wait_ge(s_sigA, g + 1)
                dve.scalar_tensor_tensor(sim[:, t, :], sim[:, t, :], thr[:, t:t + 1], sigA[:, t % 2, :], ALU.is_ge,
                                         ALU.mult).then_inc(s_A, 1)

        def residual(b):
            dve.wait_ge(s_A, TB * (b + 1))
            for t in range(TB):
                g = TB * b + t
                link(dve.scalar_tensor_tensor(xb[:, t, :], sim[:, t, :], gam[:, 3:4], xb[:, t, :], ALU.mult, ALU.add))
                dve.wait_ge(s_AT, g + 1)
                dve.scalar_tensor_tensor(xb[:, t, :], bank[AT_BANK[t]][:, :], gam[:, 3:4], xb[:, t, :], ALU.mult,
                                         ALU.add).then_inc(s_x1, 1)
            dve.wait_ge(s_x1, TB * (b + 1))

        def normalise(b):
            variance(xb, 3 * b + 2, EPS)
            link(dve.tensor_scalar(rstd[:, :], rstd[:, :], XS, None, ALU.mult))
            link(dve.scalar_tensor_tensor(aff[:, 1, :], mv[:, :, 0], -1.0, rstd[:, :], ALU.mult, ALU.mult))
            dve.wait_ge(d_x1, 16 * TB * (b + 1))
            for t in range(TB):
                dve.tensor_scalar(xb[:, t, :], xb[:, t, :], rstd[:, t:t + 1], aff[:, 1, t:t + 1], ALU.mult,
                                  ALU.add).then_inc(s_xn, 1)

        def largest_logits(b):
            dve.wait_ge(s_lg, b + 1)
            tiles = slice(TB * b, TB * (b + 1))
            dve.tensor_copy(lg[:, tiles, :], bank[0][:, 0:TB * E].rearrange("p (t e) -> p t e", t=TB)).then_inc(s_lgc, 1)
            dve.wait_ge(s_lgc, b + 1)
            for g in range(TB * b, TB * (b + 1)):
                last = dve.max(mx[:, g, :], lg[:, g, :])
            link(last)
            for g in range(TB * b, TB * (b + 1)):
                last = dve.max_index(mxi[:, g, :], mx[:, g, :], lg[:, g, :])
            link(last)

        def shared_lo(b, q):
            n = SC * b + q
            dve.wait_ge(s_hhi, n + 1)
            dve.scalar_tensor_tensor(hS[:, 1, q, :], sgt[:, q % 2, :], HS / XW, hS[:, 0, q, :], ALU.mult,
                                     ALU.subtract).then_inc(s_hlo, 1)

        def shared_hidden(b, q):
            n = SC * b + q
            if q:
                shared_lo(b, q - 1)
            dve.wait_ge(s_sg, n + 1)
            dve.scalar_tensor_tensor(sgt[:, q % 2, :], bank[5 + 2 * (q % 2)][:, :], biasS[:, 1, q:q + 1], sgt[:, q % 2, :],
                                     ALU.add, ALU.mult).then_inc(s_t2, 1)
            if q == SC - 1:
                shared_lo(b, q)

        for b in range(NB):
            if b:
                largest_logits(b - 1)
            threshold_start(b)
            for it in range(PROBES):
                threshold_probe(b, it)
                if b == 0 and 2 * it < EARLY:
                    for n in (2 * it, 2 * it + 1):
                        weight_lo(n, early[:, n % 4, 0:UNITS[n][3]])
                if b:
                    shared_hidden(b - 1, it)
                if it == 0:
                    layer_norm_x(b)
            threshold_end(b)
            if b:
                shared_hidden(b - 1, SC - 1)
            threshold_check(b)
            mask(b)
            residual(b)
            normalise(b)
        largest_logits(NB - 1)

        last_b = NB - 1
        dve.tensor_copy(ef, mxi[:, :, 0:2].rearrange("p g k -> p k g"))
        dve.tensor_tensor(wt[:, 1, :], mx[:, :, 0], mx[:, :, 1], ALU.subtract).then_inc(s_top2, 1)
        dve.wait_ge(s_top2, 1)
        dve.wait_ge(s_const, N_CONST)
        for k in range(2):
            last = dve.tensor_tensor(sel[:, k, :, :], ef[:, k, :].rearrange("p (g o) -> p g o", o=1).to_broadcast([P, NT, E]),
                                     io8.rearrange("p (o e) -> p o e", o=1).to_broadcast([P, NT, E]), ALU.is_equal)
        link(last)
        dve.tensor_tensor(selsum.rearrange("p (g e) -> p g e", g=NT), sel[:, 0, :, :], sel[:, 1, :, :], ALU.add).then_inc(s_sel, 1)
        shared_hidden(last_b, 0)
        shared_hidden(last_b, 1)
        dve.wait_ge(s_rank, 1)
        shared_hidden(last_b, 2)
        link(dve.tensor_copy(cnt, bank[3][:, 0:E]))
        link(dve.tensor_tensor(cmp16, cnt.rearrange("p (e o) -> p e o", o=1).to_broadcast([P, E, 16]),
                               k128.rearrange("p (o k) -> p o k", o=1).to_broadcast([P, E, 16]), ALU.is_gt))
        link(dve.tensor_reduce(nblk, cmp16, AX.X, ALU.add))
        link(dve.tensor_tensor_scan(ends, one8, nblk, 0.0, ALU.mult, ALU.add))
        link(dve.tensor_tensor(first, ends, nblk, ALU.subtract))
        link(dve.scalar_tensor_tensor(slotr, first.rearrange("p (o e) -> p o e", o=1).to_broadcast([P, NT, E]), float(P),
                                      bank[2][:, 0:NT * E].rearrange("p (g e) -> p g e", g=NT), ALU.mult, ALU.add))
        for k in range(2):
            last = dve.tensor_tensor(prod[:, k, :, :], sel[:, k, :, :], slotr, ALU.mult)
        link(last)
        link(dve.tensor_reduce(pos, prod, AX.X, ALU.add))
        link(dve.tensor_copy(posi, pos.rearrange("p k g -> p (k g)")))
        dve.tensor_scalar(lowi, posi, P - 1, None, ALU.bitwise_and)
        link(dve.tensor_scalar(higi, posi, P.bit_length() - 1, None, ALU.logical_shift_right))
        dve.tensor_copy(lowf.rearrange("p k g -> p (k g)"), lowi)
        link(dve.tensor_copy(higf.rearrange("p k g -> p (k g)"), higi))
        link(dve.tensor_tensor(blkc, iota[:, 0:BLOCKS].rearrange("p (j o) -> p j o", o=1).to_broadcast([P, BLOCKS, E]),
                               ends.rearrange("p (o e) -> p o e", o=1).to_broadcast([P, BLOCKS, E]), ALU.is_ge))
        link(dve.tensor_reduce(base_f, blkc, AX.X, ALU.add))
        link(dve.tensor_scalar(base_f, base_f, float(E - 1), float(EW), ALU.min, ALU.mult))
        dve.tensor_copy(wbase[:, :], base_f)
        shared_hidden(last_b, 3)
        dve.wait_ge(s_wt, 2)
        for n in range(2 * NT):
            g, k = n // 2, n % 2
            if n >= RING:
                dve.wait_ge(s_tabp, n - RING + 1)
            dve.tensor_scalar(oneh[:, n % RING, :], iota, lowf[:, k, g:g + 1], None, ALU.is_equal)
            dve.tensor_scalar(valh[:, n % RING, 0, :], iota[:, 0:BLOCKS], higf[:, k, g:g + 1], tok1[:, g:g + 1], ALU.is_equal, ALU.mult)
            dve.tensor_scalar(valh[:, n % RING, 1, :], iota[:, 0:BLOCKS], higf[:, k, g:g + 1], wt[:, k, g:g + 1], ALU.is_equal,
                              ALU.mult).then_inc(s_oneh, 1)
            if n + 1 in (TABLE_AT[0][1], TABLE_AT[1][1]):
                shared_hidden(last_b, 4 if n + 1 == TABLE_AT[0][1] else 5)
        dve.wait_ge(s_tabp, 2 * NT)
        link(dve.tensor_copy(tab, bank[0][:, 0:2 * BLOCKS].rearrange("p (k j) -> p k j", k=2)))
        link(dve.tensor_scalar(zer, tab[:, 0, :], 0.0, dumf, ALU.is_equal, ALU.mult))
        dve.tensor_scalar(wcol[:, :], tab[:, 1, :], 1.0 / HW, None, ALU.mult)
        dve.scalar_tensor_tensor(idx[:, :], tab[:, 0, :], -1.0, zer, ALU.add, ALU.add).then_inc(s_route, 1)

        def routed_x(j, p):
            dve.wait_ge(s_x2ps, j + 1)
            if not (isinstance(j, int) and j < 2):
                dve.wait_ge(s_gu2, j - 1)
            dve.tensor_copy(xT2[:, p, :, :, :].rearrange("p s c t -> p (s c t)").bitcast(F32), bank[0][:, :]).then_inc(s_x2, 1)

        def routed_hidden(j, p):
            dve.wait_ge(s_sig2, j + 1)
            if not (isinstance(j, int) and j < 2):
                dve.wait_ge(s_h2ps, j - 1)
            dve.scalar_tensor_tensor(h2[:, p, :], bank[5 + 2 * p][:, 0:I], HS / XW, sg2[:, p, :], ALU.mult,
                                     ALU.mult).then_inc(s_h2, 1)

        def routed_h(j, p):
            dve.wait_ge(s_h2hi, j + 1)
            dve.tensor_tensor(hT2[:, 1, :, p, :], bank[1][:, 0:DC * P].rearrange("p (c t) -> p c t", c=DC),
                              hT2[:, 0, :, p, :], ALU.subtract).then_inc(s_h2lo, 1)

        def step(j, m, p, fetch=True):
            first_block = isinstance(j, int) and j == 0
            if not first_block:
                routed_h(j - 1, 1 - p)
            if first_block or not (isinstance(j, int) and j == BLOCKS - 1):
                routed_x(j + 1, 1 - p)
            routed_hidden(j, p)

        for n in range(LAST, len(UNITS)):
            weight_lo(n, stage[:, n % 2, 0:UNITS[n][3]])
        routed_x(0, 0)
        run_blocks(dve, step)
        j = BLOCKS - 1
        routed_h(j, j % 2)

    es.close()


def run_blocks(eng, step):
    for j in range(HEAD_BLOCKS):
        step(j, j // 2, j % 2)
    with eng.Fori(0, (BLOCKS - HEAD_BLOCKS - 2) // 2) as i:
        step(2 * i + HEAD_BLOCKS, i + HEAD_BLOCKS // 2, 1)
        step(2 * i + (HEAD_BLOCKS + 1), i + (HEAD_BLOCKS // 2 + 1), 0)
    for j in (BLOCKS - 2, BLOCKS - 1):
        step(j, j // 2, j % 2, fetch=False)


def kernel(**inputs):
    import numpy as np
    import concourse.bacc as bacc
    from concourse.bass_utils import run_bass_kernel_spmd

    nc = bacc.Bacc("TRN2", target_bir_lowering=False, num_devices=1)
    shapes = {
        "x": (NB, S, D), "ctx_512": (NB, S, C), "L0_xattn_Wq": (C, C), "L0_xattn_Wk": (C, C),
        "L0_xattn_gamma_raw": (1, 1), "L0_ffn_router_w": (E, D), "L0_ffn_gate_w": (E, D, I), "L0_ffn_up_w": (E, D, I),
        "L0_ffn_down_w": (E, I, D), "L0_ffn_s_gate_w": (D, SI), "L0_ffn_s_gate_b": (SI, 1), "L0_ffn_s_up_w": (D, SI),
        "L0_ffn_s_up_b": (SI, 1), "L0_ffn_s_down_w": (SI, D), "L0_ffn_s_down_b": (1, D),
    }
    arrays, args = {}, []
    for name, shape in shapes.items():
        arrays[name + "_in"] = np.ascontiguousarray(inputs[name]).reshape(shape)
        args.append(nc.dram_tensor(name + "_in", shape, F32, kind="ExternalInput").ap())
    out = nc.dram_tensor("out_dram", (T + P, D), F32, kind="ExternalOutput").ap()
    xn_dram = nc.dram_tensor("xn_dram", (T + P, 2 * D), mybir.dt.float16, kind="Internal").ap()
    build(nc, *args, out, xn_dram)
    r = run_bass_kernel_spmd(nc, [arrays], core_ids=[0])
    return r.results[0]["out_dram"][:T].reshape(NB, S, D)
```

```python
from contextlib import ExitStack

import concourse.bass as bass
from concourse import mybir

F32 = mybir.dt.float32
F16 = mybir.dt.float16
I32 = mybir.dt.int32
U32 = mybir.dt.uint32
ALU = mybir.AluOpType
ACT = mybir.ActivationFunctionType
AX = mybir.AxisListType

P = 128
NB, S, D = 4, 512, 512
TB = S // P
NT = NB * TB
T = NB * S
C = 128
KD = D // P
E, TOPK = 8, 2
I = 352
SI = 704
HEADS = 4
EPS = 1e-5

KTH = int(S * 0.3)
WIN = 8
MIDDLE = KTH - WIN / 2 - 0.5
PROBES = 5
ACT_TILES = 2
START_Z, SPAN_Z = 0.507, 1.5

XS, WS, HS = 16.0, 64.0, 4.0
XW = XS * WS
HW = HS * WS

DOWN_ROWS = [0, 128, I - P]
DOWN_ZERO = [0, 0, 2 * P - (I - P)]
SH_ROWS = [0, 128, 256, 384, 512, SI - P]
SH_ZERO = [0, 0, 0, 0, 0, 5 * P - (SI - P)]
DC, SC = len(DOWN_ROWS), len(SH_ROWS)

GU = 2 * I
GU_HI, GU_LO = 0, KD * GU
DN_HI, DN_LO = 2 * KD * GU, 2 * KD * GU + DC * D
EW = DN_LO + DC * D
SH = (E - 2) * EW
SG_HI, SG_LO = SH, SH + KD * 2 * SI
SD_HI, SD_LO = SH + 2 * KD * 2 * SI, SH + 2 * KD * 2 * SI + SC * D

BLOCKS = T * TOPK // P + E - 1
SURE = 33
HEAD_BLOCKS = 3
RING = 8
TABLE_AT = [(0, 5), (5, 13), (13, 20), (20, 28), (28, 2 * NT)]
HIDDEN_AT = {7: 4, 13: 5}
LAST_AT = [0, 4, 3, 0]
AT_BANK = [2, 3, 0, 1]
CONTEXT_AT, PROJ_AT = 3, 4
DUMMY = T


def weight_units():
    units = []
    for c in range(KD):
        for n, w in enumerate(("s_gate", "s_up")):
            units.append(([(w, None, c * P, SI)], SG_HI + (2 * c + n) * SI, SG_LO + (2 * c + n) * SI, SI, 0))
    for q in range(SC):
        units.append(([("s_down", None, SH_ROWS[q], D)], SD_HI + q * D, SD_LO + q * D, D, SH_ZERO[q]))
    for e in range(E):
        b = e * EW
        for c in range(KD):
            units.append(([("gate", e, c * P, I), ("up", e, c * P, I)], b + GU_HI + c * GU, b + GU_LO + c * GU, GU, 0))
        for q in range(DC):
            units.append(([("down", e, DOWN_ROWS[q], D)], b + DN_HI + q * D, b + DN_LO + q * D, D, DOWN_ZERO[q]))
    return units


UNITS = weight_units()
EARLY = 2 * KD
PER_EXPERT = KD + DC
LATE = EARLY + SC + (E - 2) * PER_EXPERT
LAST = LATE + PER_EXPERT
UNITS_AT = [
    ([2, 2, 2, 1, 3], [], 3, 2),
    ([0, 1, 1, 1, 1], [0, 1, 1, 1, 0], 2, 0),
    ([0, 1, 1, 1, 1], [0, 1, 1, 1, 0], 2, 0),
    ([0, 1, 1, 1, 1], [0, 1, 1, 0, 0], 2, 0),
]
UNITS_END = [1, 2, 2, 2, 0, 0]
IN_WINDOW = [sum(a) + sum(b) + c + d for a, b, c, d in UNITS_AT]
assert EARLY + sum(IN_WINDOW) + sum(UNITS_END) == LATE
assert sum(LAST_AT) == PER_EXPERT and len(LAST_AT) == HEAD_BLOCKS + 1
assert SURE > T * TOPK // P and (SURE - HEAD_BLOCKS) % 2 == 0 and (BLOCKS - SURE) % 2 == 0
EXTRA = range(LAST + 2, len(UNITS) - 1)


def stage_counts():
    at, early, out = [0, 0], [0] * 4, []
    for n, (src, *_) in enumerate(UNITS):
        if n < EARLY:
            early[n % 4] += 16 * len(src)
            out.append(early[n % 4])
        elif n in EXTRA:
            out.append(16 * sum(len(UNITS[k][0]) for k in EXTRA))
        else:
            at[n % 2] += 16 * len(src)
            out.append(at[n % 2])
    return out


STAGED = stage_counts()


def build(nc, x, ctx_in, wq, wk, gamma, router, gate, up, down, s_gate, s_gate_b, s_up, s_up_b, s_down, s_down_b,
          out, xn_dram):
    es = ExitStack()

    def sb(name, shape, dt=F32):
        return es.enter_context(nc.sbuf_tensor(name, shape, dt))

    def sem(name):
        return es.enter_context(nc.semaphore(name))

    def staged(n):
        cols = UNITS[n][3]
        if n < EARLY:
            return early[:, n % 4, 0:cols], d_early[n % 4]
        if n not in EXTRA:
            return stage[:, n % 2, 0:cols], d_stage[n % 2]
        if n == EXTRA[-1]:
            return below[:, 0:cols], d_extra
        at = sum(UNITS[k][3] for k in EXTRA if k < n)
        return simf[:, at:at + cols], d_extra

    dram = {"gate": gate, "up": up, "down": down, "s_gate": s_gate, "s_up": s_up, "s_down": s_down}

    W = sb("W", [P, E * EW], F16)
    sim = sb("sim", [P, TB, S])
    sigA = sb("sigA", [P, 2, S])
    qT = sb("qT", [P, S])
    kT = sb("kT", [P, S])
    xb = sb("xb", [P, TB, D])
    xn = sb("xn", [P, 2, 2 * D], F16)
    ysh = sb("ysh", [P, 2, D])
    xT = sb("xT", [P, 2, KD, S], F16)
    hS = sb("hS", [P, 2, SC, S], F16)
    sgt = sb("sgt", [P, 2, S])
    stage = sb("stage", [P, 2, SI])
    below = sb("below", [P, S])
    sdb = sb("sdb", [P, 2, D], F16)
    ident = sb("ident", [P, P])
    ident16 = sb("ident16", [P, P], F16)
    row0 = sb("row0", [P, P], F16)
    wqT = sb("wqT", [P, C])
    wkT = sb("wkT", [P, C])
    rwT = sb("rwT", [P, 2, KD, E], F16)
    bias = sb("bias", [P, 2, SC])
    biasS = sb("biasS", [P, 2, SC])
    gam = sb("gam", [P, 4])
    stats = sb("stats", [P, TB, 6])
    mv = sb("mv", [P, TB, 2])
    rstd = sb("rstd", [P, TB])
    pw = sb("pw", [P, 2, TB])
    aff = sb("aff", [P, 2, TB])
    probe = sb("probe", [P, 2, TB])
    lo_ = sb("lo_", [P, 2, TB])
    hi_ = sb("hi_", [P, 2, TB])
    dif = sb("dif", [P, 2, TB])
    over = sb("over", [P, TB])
    target = sb("target", [P, TB])
    nprobe = sb("nprobe", [P, TB])
    msk = sb("msk", [P, 2, TB])
    bad = sb("bad", [P, 4])
    badi = sb("badi", [P, 1], I32)
    top = sb("top", [P, TB, 8])
    pick = sb("pick", [P, TB, 8])
    thr = sb("thr", [P, TB])
    rank8 = sb("rank8", [P, 8])
    spare = sb("spare", [P, 1])
    lg = sb("lg", [P, NT, E])
    mx = sb("mx", [P, NT, 8])
    mxi = sb("mxi", [P, NT, 8], U32)

    simf = sim[:, :, :].rearrange("p a b -> p (a b)")
    oneh = simf[:, 0:RING * P].rearrange("p (a b) -> p a b", a=RING)
    valh = simf[:, RING * P:RING * (P + 2 * BLOCKS)].rearrange("p (a k b) -> p a k b", a=RING, k=2)
    xg = [t[:, :].bitcast(F16) for t in (qT, kT)]
    ylast = xn[:, :, :].bitcast(F32)
    early = hS[:, :, :, :].rearrange("p s c t -> p (s c t)").bitcast(F32)[:, 0:4 * SI].rearrange("p (a n) -> p a n", a=4)
    y2 = xb[:, 0:2, :]
    h2 = xb[:, 2:4, 0:I]
    sg2 = sgt[:, :, 0:I]
    xT2 = xT[:, :, :, :].rearrange("p s c t -> p (s c t)")[:, 0:4 * KD * P].rearrange("p (a s c t) -> p a s c t", a=2, s=2, c=KD)
    hT2 = hS[:, :, 0:DC, 0:2 * P].rearrange("p s c (a t) -> p s c a t", a=2)
    rt = sigA[:, :, :].rearrange("p a b -> p (a b)")

    def rv(at, n):
        return rt[:, at:at + n]

    iota = rv(0, P)
    io8 = rv(128, 8)
    tok1 = rv(136, NT)
    ef = rv(152, 2 * NT).rearrange("p (k g) -> p k g", k=2)
    wt = rv(184, 2 * NT).rearrange("p (k g) -> p k g", k=2)
    sel = rv(216, 2 * NT * E).rearrange("p (k g e) -> p k g e", k=2, g=NT)
    slotr = rv(472, NT * E).rearrange("p (g e) -> p g e", g=NT)
    prod = below[:, 0:2 * NT * E].rearrange("p (k g e) -> p k g e", k=2, g=NT)
    pos = rv(600, 2 * NT).rearrange("p (k g) -> p k g", k=2)
    posi = rv(632, 2 * NT).bitcast(I32)
    lowi = rv(664, 2 * NT).bitcast(I32)
    higi = rv(696, 2 * NT).bitcast(I32)
    lowf = rv(728, 2 * NT).rearrange("p (k g) -> p k g", k=2)
    higf = rv(760, 2 * NT).rearrange("p (k g) -> p k g", k=2)
    cnt = rv(792, E)
    nblk = rv(800, E)
    ends = rv(808, E)
    first = rv(816, E)
    one8 = rv(824, E)
    k128 = rv(832, 16)
    dumf = rv(848, 1)
    base_f = rv(849, BLOCKS)
    need_f = rv(849 + BLOCKS, HEAD_BLOCKS + 1)
    selsum = ysh[:, 0, 0:64].bitcast(F16)
    upper = ysh[:, 0, 64:128].bitcast(F16)
    ones16 = ysh[:, 0, 128:192].bitcast(F16)
    cmp16 = ysh[:, 0, 192:320].rearrange("p (e k) -> p e k", e=E)
    blkc = ysh[:, 1, 0:BLOCKS * E].rearrange("p (j e) -> p j e", j=BLOCKS)
    tab = ysh[:, 1, 320:320 + 2 * BLOCKS].rearrange("p (k j) -> p k j", k=2)
    zer = ysh[:, 1, 400:400 + BLOCKS]
    wcol = sb("wcol", [P, BLOCKS])
    idx = sb("idx", [P, BLOCKS], I32)
    wbase = sb("wbase", [P, BLOCKS], I32)
    need_used = sb("need_used", [P, HEAD_BLOCKS + 1], I32)
    need = need_used[:, 0:HEAD_BLOCKS]
    used = need_used[0:1, HEAD_BLOCKS:HEAD_BLOCKS + 1]
    gidx = sb("gidx", [P, 2], I32)
    sidx = sb("sidx", [P, 2], I32)

    above = below[:, :].bitcast(mybir.dt.uint8).rearrange("p (t s) -> p t s", t=TB)
    signs = sb("signs", [P, ACT_TILES, S // 2], mybir.dt.uint16)[:, :, :].rearrange("p a s -> p (a s)").bitcast(mybir.dt.int8).rearrange("p (a s) -> p a s", a=ACT_TILES)

    bank = [es.enter_context(nc.psum_tensor(f"bank{i}", [P, 512], F32)) for i in range(8)]

    d_w = sem("d_w")
    d_in = sem("d_in")
    d_early = [sem(f"d_early{i}") for i in range(4)]
    d_ctx = sem("d_ctx")
    d_x = sem("d_x")
    d_x1 = sem("d_x1")
    d_zero = sem("d_zero")
    d_xn = [sem(f"d_xn{i}") for i in range(2)]
    d_y = [sem(f"d_y{i}") for i in range(2)]
    d_stage = [sem(f"d_stage{i}") for i in range(2)]
    d_extra = sem("d_extra")
    d_xg = [sem(f"d_xg{i}") for i in range(2)]
    d_sc = [sem(f"d_sc{i}") for i in range(2)]
    s_const = sem("s_const")
    s_zero = sem("s_zero")
    s_chain = sem("s_chain")
    s_pool = sem("s_pool")
    s_fall = sem("s_fall")
    s_wT = sem("s_wT")
    s_wTc = sem("s_wTc")
    s_rw = sem("s_rw")
    s_gam = sem("s_gam")
    s_cT = sem("s_cT")
    s_cTc = sem("s_cTc")
    s_sim = sem("s_sim")
    s_simc = sem("s_simc")
    s_sigA = sem("s_sigA")
    s_A = sem("s_A")
    s_AT = sem("s_AT")
    s_x1 = sem("s_x1")
    s_var = sem("s_var")
    s_aff = sem("s_aff")
    s_xa = sem("s_xa")
    s_rstd = sem("s_rstd")
    s_bad = sem("s_bad")
    s_badr = sem("s_badr")
    s_xn = sem("s_xn")
    s_xnT = sem("s_xnT")
    s_xT = sem("s_xT")
    s_lg = sem("s_lg")
    s_lgc = sem("s_lgc")
    s_gu = sem("s_gu")
    s_sg = sem("s_sg")
    s_t2 = sem("s_t2")
    s_hhi = sem("s_hhi")
    s_hlo = sem("s_hlo")
    s_yps = sem("s_yps")
    s_y = sem("s_y")
    s_ehi = sem("s_ehi")
    s_ready = sem("s_ready")
    s_whi = sem("s_whi")
    s_wlo = sem("s_wlo")
    s_wloD = sem("s_wloD")
    s_cnt = sem("s_cnt")
    s_probe = sem("s_probe")
    s_nhi = sem("s_nhi")
    s_nlo = sem("s_nlo")
    s_top2 = sem("s_top2")
    s_wt = sem("s_wt")
    s_sel = sem("s_sel")
    s_rank = sem("s_rank")
    s_oneh = sem("s_oneh")
    s_tabp = sem("s_tabp")
    s_route = sem("s_route")
    s_x2ps = sem("s_x2ps")
    s_x2 = sem("s_x2")
    s_gu2 = sem("s_gu2")
    s_sig2 = sem("s_sig2")
    s_h2 = sem("s_h2")
    s_h2ps = sem("s_h2ps")
    s_h2hi = sem("s_h2hi")
    s_h2lo = sem("s_h2lo")
    s_y2ps = sem("s_y2ps")
    s_y2 = sem("s_y2")
    s_gi = sem("s_gi")
    s_held = sem("s_held")
    s_si = sem("s_si")

    block = es.enter_context(nc.Block())
    N_CONST = 12

    @block.sync
    def _(sp):
        sp.dma_start(below[:, 0:C], wq).then_inc(d_w, 16)
        sp.dma_start(below[:, C:2 * C], wk).then_inc(d_w, 16)
        sp.dma_start(kT[:, :].rearrange("p (t c) -> p t c", t=TB), ctx_in[0].rearrange("(t p) c -> p t c", p=P)).then_inc(d_ctx, 16)

        def load(n):
            place, loaded = staged(n)
            at = 0
            for name, e, row, cols in UNITS[n][0]:
                src = dram[name] if e is None else dram[name][e]
                sp.dma_start(place[:, at:at + cols], src[row:row + P, :]).then_inc(loaded, 16)
                at += cols

        def load_early(n):
            if n >= 4:
                sp.wait_ge(s_wloD, n - 3)
            load(n)

        for n in range(4):
            load_early(n)
        sp.dma_start(gam[:, 0:1], gamma.to_broadcast([P, 1])).then_inc(d_in, 16)
        sp.dma_start(ysh[0:E, 0, :], router).then_inc(d_in, 16)
        sp.dma_start(ysh[0:1, 1, :], s_down_b).then_inc(d_in, 16)
        for n, v in enumerate((s_gate_b, s_up_b)):
            for q in range(SC):
                sp.dma_start(bias[:, n, q:q + 1], v[SH_ROWS[q]:SH_ROWS[q] + P, :]).then_inc(d_in, 16)
        sp.dma_start(xb[:, :, :], x[0].rearrange("(t p) d -> p t d", p=P)).then_inc(d_x, 16)
        units = iter(range(EARLY, len(UNITS)))

        def load_units(k):
            for _ in range(k):
                n = next(units)
                if n - 2 >= EARLY:
                    sp.wait_ge(s_wlo, n - 2 - EARLY + 1)
                load(n)

        def load_context(b):
            sp.wait_ge(s_sim, TB * b)
            sp.dma_start(kT[:, :].rearrange("p (t c) -> p t c", t=TB), ctx_in[b].rearrange("(t p) c -> p t c", p=P)).then_inc(d_ctx, 16)

        load_units(2)
        load_context(1)
        load_early(4)
        load_early(5)
        load_units(2)
        load_early(6)
        load_early(7)
        sp.wait_ge(s_zero, 1)
        sp.dma_start(xn_dram[DUMMY:DUMMY + P, :], xn[:, 0, :]).then_inc(d_zero, 16)
        sp.dma_start(out[DUMMY:DUMMY + P, :], ylast[:, 0, :]).then_inc(d_zero, 16)
        for b in range(NB):
            if 0 < b < NB - 1:
                load_context(b + 1)
            after = max(UNITS_AT[b][3] - 2, 0)
            load_units(IN_WINDOW[b] - (4 if b == 0 else 0) - after)
            for t in range(TB):
                g = TB * b + t
                sp.wait_ge(s_x1, g + 1)
                sp.dma_start(out[g * P:(g + 1) * P, :], xb[:, t, :]).then_inc(d_x1, 16)
            for t in range(TB):
                g = TB * b + t
                sp.wait_ge(s_nlo, g + 1)
                sp.dma_start(xn_dram[g * P:(g + 1) * P, :], xn[:, t % 2, :]).then_inc(d_xn[t % 2], 16)
            load_units(after)
            if b + 1 < NB:
                sp.dma_start(xb[:, :, :], x[b + 1].rearrange("(t p) d -> p t d", p=P)).then_inc(d_x, 16)
        load_units(sum(UNITS_END) + PER_EXPERT)
        sp.wait_ge(s_tabp, 2 * NT)
        for n in EXTRA:
            load(n)
        load_units(2)
        sp.wait_ge(s_wloD, EARLY + 1)
        load(len(UNITS) - 1)
        sp.wait_ge(d_x1, 16 * NT)
        for i in range(2):
            sp.wait_ge(d_xn[i], 16 * NT // 2)
        sp.wait_ge(d_zero, 32)

    @block.gpsimd
    def _(pool):
        chain = [0]

        def link(ins):
            chain[0] += 1
            ins.then_inc(s_pool, 1)
            pool.wait_ge(s_pool, chain[0])

        link(pool.memset(ident[:, :], 0.0))
        pool.affine_select(out=ident[:, :], in_=ident[:, :], compare_op=ALU.not_equal, fill=1.0, base=0,
                           pattern=[[-1, P]], channel_multiplier=1).then_inc(s_const, 1)
        pool.wait_ge(s_const, 1)
        pool.tensor_copy(ident16[:, :], ident[:, :]).then_inc(s_const, 1)
        link(pool.memset(row0[:, :], 0.0))
        pool.memset(row0[0:1, :], 1.0).then_inc(s_const, 1)
        pool.iota(rank8[:, :], [[1, 8]], base=1, channel_multiplier=0, allow_small_or_imprecise_dtypes=True).then_inc(s_const, 1)
        pool.memset(pw[:, 1, :], -0.5)
        pool.memset(target[:, 0:TB - ACT_TILES], MIDDLE)
        pool.memset(target[:, TB - ACT_TILES:TB], 2 * MIDDLE - S).then_inc(s_const, 1)
        pool.wait_ge(s_const, 5)

        units = iter(range(EARLY, LAST))

        def split_lo(n):
            src, hi, lo, cols, zero = UNITS[n]
            st = stage[:, n % 2, 0:cols]
            pool.wait_ge(s_whi, n - EARLY + 1)
            link(pool.tensor_scalar(st, st, WS, 1.0, ALU.mult, ALU.mult))
            last = pool.tensor_tensor(W[:, lo:lo + cols], st, W[:, hi:hi + cols], ALU.subtract)
            if zero:
                link(last)
                link(pool.memset(W[0:zero, hi:hi + cols], 0.0))
                last = pool.memset(W[0:zero, lo:lo + cols], 0.0)
            last.then_inc(s_wlo, 1)

        def split_some(k):
            for _ in range(k):
                split_lo(next(units))

        def ready(n):
            pool.wait_ge(s_wlo, n - EARLY)
            pool.sem_inc(s_ready, 1)

        def power(n):
            pool.wait_ge(s_var, n + 1)
            pool.tensor_tensor(rstd[:, :], pw[:, 0, :], pw[:, 1, :], ALU.pow).then_inc(s_rstd, 1)

        def add_shared(b, t, src):
            g = TB * b + t
            pool.wait_ge(s_y, g + 1)
            pool.wait_ge(d_x1, 16 * TB * (b + 1))
            pool.dma_start(out[g * P:(g + 1) * P, :], src[:, t % 2, :], accum_op=ALU.add).then_inc(d_y[t % 2], 16)

        def xn_lo(b, t):
            g = TB * b + t
            pool.wait_ge(s_nhi, g + 1)
            pool.tensor_tensor(xn[:, t % 2, D:2 * D], xb[:, t, :], xn[:, t % 2, 0:D], ALU.subtract).then_inc(s_nlo, 1)

        for b in range(NB):
            counted, chunked, masked, ended = UNITS_AT[b]
            if b == 0:
                power(0)
            split_some(sum(counted[:2]) + sum(chunked[:2]))
            power(3 * b + 1)
            split_some(sum(counted[2:]) + sum(chunked[2:]))
            pool.wait_ge(s_bad, b + 1)
            pool.partition_all_reduce(bad[:, 1:2], bad[:, 0:1], P, bass.bass_isa.ReduceOp.max).then_inc(s_badr, 1)
            split_some(masked)
            power(3 * b + 2)
            if b:
                add_shared(b - 1, 0, ysh)
            xn_lo(b, 0)
            xn_lo(b, 1)
            if b:
                add_shared(b - 1, 1, ysh)
            if b + 1 < NB:
                power(3 * b + 3)
            if b:
                add_shared(b - 1, 2, ysh)
            xn_lo(b, 2)
            xn_lo(b, 3)
            if b:
                add_shared(b - 1, 3, ysh)
            split_some(ended)

        pool.wait_ge(s_A, NT)
        pool.iota(iota, [[1, P]], base=0, channel_multiplier=0, allow_small_or_imprecise_dtypes=True).then_inc(s_const, 1)
        pool.iota(io8, [[1, E]], base=0, channel_multiplier=0, allow_small_or_imprecise_dtypes=True).then_inc(s_const, 1)
        pool.iota(tok1, [[P, NT]], base=1, channel_multiplier=1, allow_small_or_imprecise_dtypes=True).then_inc(s_const, 1)
        pool.iota(k128, [[P, 16]], base=0, channel_multiplier=0, allow_small_or_imprecise_dtypes=True).then_inc(s_const, 1)
        pool.iota(dumf, [[0, 1]], base=DUMMY + 1, channel_multiplier=1, allow_small_or_imprecise_dtypes=True).then_inc(s_const, 1)
        pool.memset(one8, 1.0).then_inc(s_const, 1)
        for i in range(2):
            pool.wait_ge(d_y[i], 16 * (NT - TB) // 2)
        link(pool.memset(upper, 1.0))
        pool.memset(ones16, 1.0)
        pool.affine_select(out=upper, in_=upper, compare_op=ALU.is_gt, fill=0.0, base=0, pattern=[[1, P]],
                           channel_multiplier=-1).then_inc(s_const, 1)

        split_some(sum(UNITS_END))
        ready(LATE)

        def gather(j, p):
            link2(pool.tensor_copy(gidx[:, p:p + 1], idx[:, bass.ds(j, 1)]), s_gi, j + 1)
            pool.indirect_dma_start(out=xg[p], out_offset=None, in_=xn_dram,
                                    in_offset=bass.IndirectOffsetOnAxis(ap=gidx[:, p:p + 1], axis=0)).then_inc(d_xg[p], 16)

        def scatter(j, m, p):
            if isinstance(j, int) and j == 0:
                for i in range(2):
                    pool.wait_ge(d_y[i], 16 * NT // 2)
            pool.wait_ge(s_y2, j + 1)
            if not (isinstance(j, int) and j == 0):
                pool.wait_ge(d_sc[1 - p], 16 * (m + 1) if p else 16 * m)
            link2(pool.tensor_copy(sidx[:, p:p + 1], idx[:, bass.ds(j, 1)]), s_si, j + 1)
            pool.indirect_dma_start(out=out, out_offset=bass.IndirectOffsetOnAxis(ap=sidx[:, p:p + 1], axis=0),
                                    in_=y2[:, p, :], in_offset=None, compute_op=ALU.add).then_inc(d_sc[p], 16)

        def link2(ins, s, v):
            ins.then_inc(s, 1)
            pool.wait_ge(s, v)
            pool.sem_inc(s_held, 1)

        split_some(4)
        add_shared(NB - 1, 0, ylast)
        split_some(1)
        add_shared(NB - 1, 1, ylast)
        pool.wait_ge(s_route, 1)
        for i in range(2):
            pool.wait_ge(d_xn[i], 16 * NT // 2)
        pool.wait_ge(d_zero, 32)
        gather(0, 0)
        gather(1, 1)
        split_some(PER_EXPERT - 5)
        ready(LAST)
        add_shared(NB - 1, 2, ylast)
        add_shared(NB - 1, 3, ylast)

        def step(j, m, p, fetch=True):
            if fetch:
                pool.wait_ge(s_x2ps, j + 1)
                gather(j + 2, p)
            if not (isinstance(j, int) and j == 0):
                scatter(j - 1, m if p else m - 1, 1 - p)

        def finish(j):
            scatter(j, j // 2, j % 2)
            for i in range(2):
                pool.wait_ge(d_sc[i], 16 * ((j + 2 - i) // 2))
                pool.wait_ge(d_xg[i], 16 * ((min(j + 2, BLOCKS - 1) + 2 - i) // 2))

        run_blocks(pool, used, step, finish)

    @block.scalar
    def _(act):
        loads = iter(range(EARLY, len(UNITS)))

        def split_hi(n):
            src, hi, lo, cols, zero = UNITS[n]
            if n == LATE:
                act.wait_ge(s_gu, NB * SC)
            if n == LAST:
                act.wait_ge(s_yps, NT)
            place, loaded = staged(n)
            act.wait_ge(loaded, STAGED[n])
            act.activation(W[:, hi:hi + cols], place, ACT.Copy, scale=WS).then_inc(s_whi, 1)

        def split_some(k):
            for _ in range(k):
                split_hi(next(loads))

        act.wait_ge(s_wT, 1)
        act.activation(wqT[:, :], bank[0][:, 0:C], ACT.Copy).then_inc(s_wTc, 1)
        act.activation(wkT[:, :], bank[0][:, C:2 * C], ACT.Copy).then_inc(s_wTc, 1)

        def early_hi(n):
            src, hi, lo, cols, zero = UNITS[n]
            act.wait_ge(d_early[n % 4], STAGED[n])
            act.activation(W[:, hi:hi + cols], early[:, n % 4, 0:cols], ACT.Copy, scale=WS).then_inc(s_ehi, 1)

        def small_inputs():
            act.wait_ge(s_wT, 2)
            act.activation(rwT[:, 0, :, :], bank[2][:, 0:KD * E].rearrange("p (c e) -> p c e", c=KD), ACT.Copy, scale=WS).then_inc(s_wTc, 1)
            act.wait_ge(d_in, 16 * (3 + 2 * SC))
            act.wait_ge(s_zero, 2)
            act.activation(sdb[0:1, 0, :], ysh[0:1, 1, :], ACT.Copy, scale=HW).then_inc(s_wTc, 1)
            act.activation(gam[:, 1:2], gam[:, 0:1], ACT.Sigmoid).then_inc(s_gam, 1)

        def context_T(b):
            act.wait_ge(s_cT, 2 * b + 1)
            act.activation(qT[:, :], bank[0][:, :], ACT.Copy).then_inc(s_cTc, 1)

        def proj(b):
            act.wait_ge(s_cT, 2 * b + 2)
            act.activation(qT[:, :], bank[0][:, :], ACT.Copy).then_inc(s_cTc, 1)
            act.activation(kT[:, :], bank[1][:, :], ACT.Copy).then_inc(s_cTc, 1)

        def scores(b, t):
            g = TB * b + t
            act.wait_ge(s_sim, g + 1)
            if b:
                act.wait_ge(s_AT, TB * b)
                act.wait_ge(s_x1, TB * (b - 1) + t + 1)
            act.activation(sim[:, t, :], bank[t % 2][:, :], ACT.Copy).then_inc(s_simc, 1)

        def sig_scores(b, t):
            g = TB * b + t
            act.wait_ge(s_simc, g + 1)
            if g >= 2:
                act.wait_ge(s_A, g - 1)
            act.activation(sigA[:, t % 2, :], sim[:, t, :], ACT.Sigmoid, scale=1.0 / ((C / HEADS) ** 0.5 * HEADS)).then_inc(s_sigA, 1)

        def sh_sig(b, q):
            n = SC * b + q
            act.wait_ge(s_gu, n + 1)
            if n >= 2:
                act.wait_ge(s_hlo, n - 1)
            act.activation(sgt[:, q % 2, :], bank[4 + 2 * (q % 2)][:, :], ACT.Silu, bias=bias[:, 0, q:q + 1],
                           scale=1.0 / XW).then_inc(s_sg, 1)

        def sh_hi(b, q):
            n = SC * b + q
            act.wait_ge(s_t2, n + 1)
            if b and q == 0:
                act.wait_ge(s_yps, TB * b)
            act.activation(hS[:, 0, q, :], sgt[:, q % 2, :], ACT.Copy, scale=HS / XW).then_inc(s_hhi, 1)

        def xn_hi(b, t):
            g = TB * b + t
            act.wait_ge(s_xn, g + 1)
            if g >= 2:
                act.wait_ge(d_xn[t % 2], 16 * (g // 2))
                act.wait_ge(s_xnT, g - 1)
            else:
                act.wait_ge(d_zero, 32)
            act.activation(xn[:, t % 2, 0:D], xb[:, t, :], ACT.Copy).then_inc(s_nhi, 1)

        def x_T(b, t):
            g = TB * b + t
            act.wait_ge(s_xnT, g + 1)
            if b and t == 0:
                act.wait_ge(s_gu, SC * b)
            act.activation(xT[:, :, :, t * P:(t + 1) * P].rearrange("p s c t -> p (s c) t"),
                           bank[2 + t % 2][:, :].bitcast(F16).rearrange("p (c t) -> p c t", c=2 * KD), ACT.Copy).then_inc(s_xT, 1)

        def count(b, it):
            act.wait_ge(s_probe, PROBES * b + it + 1)
            for t in range(TB - ACT_TILES, TB):
                act.activation(signs[:, t - (TB - ACT_TILES), :], sim[:, t, :], ACT.Sign, bias=nprobe[:, t:t + 1],
                               accum_out=probe[:, 1, t:t + 1]).then_inc(s_cnt, 1)

        def apply_ln(b):
            act.wait_ge(s_aff, b + 1)
            for t in range(TB):
                act.activation(xb[:, t, :], xb[:, t, :], ACT.Identity, bias=aff[:, 1, t:t + 1],
                               scale=aff[:, 0, t:t + 1]).then_inc(s_xa, 1)

        def shared_out(b, t, dst):
            g = TB * b + t
            act.wait_ge(s_yps, g + 1)
            if dst is ysh and g >= 2 or t >= 2:
                act.wait_ge(d_y[t % 2], 16 * (g // 2))
            act.activation(dst[:, t % 2, :], bank[4 + t][:, :], ACT.Copy, scale=1.0 / HW).then_inc(s_y, 1)

        context_T(0)
        early_hi(0)
        proj(0)
        early_hi(1)
        for t in range(TB):
            scores(0, t)
            if t in (1, 3):
                early_hi(2 + t // 2)
        small_inputs()
        count(0, 0)
        for b in range(NB):
            counted, chunked, masked, ended = UNITS_AT[b]
            sig_scores(b, 0)
            sig_scores(b, 1)
            for it in range(PROBES):
                if it:
                    count(b, it)
                split_some(counted[it])
                if b == 0 and it < 2:
                    early_hi(2 * it + 4)
                    early_hi(2 * it + 5)
                if b and it:
                    sh_sig(b - 1, it - 1)
                    if it > 1:
                        sh_hi(b - 1, it - 2)
                split_some(sum(chunked[it:it + 1]))
                if b + 1 < NB and it == (CONTEXT_AT if b else 1):
                    context_T(b + 1)
                if b + 1 < NB and it == (PROJ_AT if b else 2):
                    proj(b + 1)
            if b:
                sh_sig(b - 1, SC - 2)
                sh_hi(b - 1, SC - 3)
            apply_ln(b)
            if b:
                sh_sig(b - 1, SC - 1)
                sh_hi(b - 1, SC - 2)
                sh_hi(b - 1, SC - 1)
            act.activation(spare[:, :], gam[:, 0:1], ACT.Sigmoid)
            sig_scores(b, 2)
            sig_scores(b, 3)
            split_some(masked)
            if b:
                shared_out(b - 1, 0, ysh)
                shared_out(b - 1, 1, ysh)
            if b + 1 < NB:
                for t in range(TB):
                    scores(b + 1, t)
            xn_hi(b, 0)
            xn_hi(b, 1)
            if b:
                shared_out(b - 1, 2, ysh)
            x_T(b, 0)
            x_T(b, 1)
            xn_hi(b, 2)
            xn_hi(b, 3)
            if b + 1 < NB:
                count(b + 1, 0)
            if b:
                shared_out(b - 1, 3, ysh)
            x_T(b, 2)
            x_T(b, 3)
            split_some(ended)
        sh_sig(NB - 1, 0)
        for q in range(SC):
            if q + 1 < SC:
                sh_sig(NB - 1, q + 1)
            if q == 0:
                act.wait_ge(s_top2, 1)
                act.activation(wt[:, 0, :], wt[:, 1, :], ACT.Sigmoid, scale=1.0 / XW).then_inc(s_wt, 1)
                act.wait_ge(s_wt, 1)
                act.activation(wt[:, 1, :], wt[:, 1, :], ACT.Sigmoid, scale=-1.0 / XW).then_inc(s_wt, 1)
            sh_hi(NB - 1, q)
            split_some(UNITS_END[q])
        act.wait_ge(s_xnT, NT)
        for i in range(2):
            act.wait_ge(d_xn[i], 16 * NT // 2)
        for t in range(TB):
            split_some([2, 2, 1, 0][t])
            shared_out(NB - 1, t, ylast)
        split_some(PER_EXPERT - 5)
        split_some(LAST_AT[0])

        def routed_sig(j, p):
            act.wait_ge(s_gu2, j + 1)
            act.activation(sg2[:, p, :], bank[4 + 2 * p][:, 0:I], ACT.Silu, scale=1.0 / XW).then_inc(s_sig2, 1)

        def routed_h(j, p):
            act.wait_ge(s_h2ps, j + 1)
            if not (isinstance(j, int) and j < 2):
                act.wait_ge(s_y2ps, j - 1)
            act.activation(hT2[:, 0, :, p, :], bank[1][:, 0:DC * P].rearrange("p (c t) -> p c t", c=DC), ACT.Copy).then_inc(s_h2hi, 1)

        def routed_y(j, m, p):
            act.wait_ge(s_y2ps, j + 1)
            if not (isinstance(j, int) and j < 2):
                act.wait_ge(d_sc[p], 16 * m)
            act.activation(y2[:, p, :], bank[2 + p][:, :], ACT.Copy, scale=wcol[:, bass.ds(j, 1)]).then_inc(s_y2, 1)

        def step(j, m, p, fetch=True):
            first_block = isinstance(j, int) and j == 0
            if not first_block:
                routed_h(j - 1, 1 - p)
            routed_sig(j, p)
            if not first_block:
                routed_y(j - 1, m if p else m - 1, 1 - p)
            if isinstance(j, int) and j < HEAD_BLOCKS:
                split_some(LAST_AT[j + 1])

        act.wait_ge(s_route, 1)

        def finish(j):
            routed_h(j, j % 2)
            routed_y(j, j // 2, j % 2)

        run_blocks(act, used, step, finish)

    @block.tensor
    def _(pe):
        pe.wait_ge(s_const, 1)
        pe.wait_ge(d_w, 32)
        pe.transpose(bank[0][:, 0:C], below[:, 0:C], ident[:, :])
        pe.transpose(bank[0][:, C:2 * C], below[:, C:2 * C], ident[:, :]).then_inc(s_wT, 1)

        def transpose_router():
            pe.wait_ge(d_in, 16 * (3 + 2 * SC))
            for c in range(KD):
                last = pe.transpose(bank[2][:, c * E:(c + 1) * E], ysh[0:E, 0, c * P:(c + 1) * P], ident[0:E, 0:E])
            last.then_inc(s_wT, 1)

        def context_T(b):
            pe.wait_ge(d_ctx, 16 * (b + 1))
            if b == 0:
                pe.wait_ge(s_wTc, 2)
            else:
                pe.wait_ge(s_simc, TB * b)
                if b > 1:
                    pe.wait_ge(s_lgc, b - 1)
            for t in range(TB):
                last = pe.transpose(bank[0][:, t * P:(t + 1) * P], kT[:, t * C:(t + 1) * C], ident[:, :])
            last.then_inc(s_cT, 1)

        def proj(b):
            pe.wait_ge(s_cTc, 3 * b + 1)
            pe.matmul(bank[0][:, :], wqT[:, :], qT[:, :], start=True, stop=True)
            pe.matmul(bank[1][:, :], wkT[:, :], qT[:, :], start=True, stop=True).then_inc(s_cT, 1)

        def scores(b, t):
            g = TB * b + t
            if t == 0:
                pe.wait_ge(s_cTc, 3 * b + 3)
            if t < 2:
                if b:
                    pe.wait_ge(s_x1, TB * (b - 1) + t + 3)
            else:
                pe.wait_ge(s_simc, g - 1)
            pe.matmul(bank[t % 2][:, :], qT[:, t * P:(t + 1) * P], kT[:, :], start=True, stop=True).then_inc(s_sim, 1)

        def transpose_A(b, t):
            g = TB * b + t
            if t == 0:
                pe.wait_ge(s_A, TB * (b + 1))
                if b:
                    pe.wait_ge(s_xT, TB * b)
                else:
                    pe.wait_ge(s_rw, 1)
                pe.wait_ge(s_cTc, 3 * min(b + 2, NB))
                if b:
                    pe.wait_ge(s_lgc, b)
            for m in range(TB):
                last = pe.transpose(bank[AT_BANK[t]][:, m * P:(m + 1) * P], sim[:, m, t * P:(t + 1) * P], ident[:, :])
            last.then_inc(s_AT, 1)

        def transpose_xn(b, t):
            g = TB * b + t
            pe.wait_ge(s_nlo, g + 1)
            if t >= 2:
                pe.wait_ge(s_xT, g - 1)
            o = bank[2 + t % 2][:, :].bitcast(F16)
            for c in range(2 * KD):
                last = pe.transpose(o[:, c * P:(c + 1) * P], xn[:, t % 2, c * P:(c + 1) * P], ident16[:, :])
            last.then_inc(s_xnT, 1)

        def logits(b):
            pe.wait_ge(s_xT, TB * (b + 1))
            pe.wait_ge(s_simc, min(TB * (b + 2), NT))
            for t in range(TB):
                o = bank[0][:, t * E:(t + 1) * E]
                for c in range(KD):
                    xh, xl = (xT[:, s, c, t * P:(t + 1) * P] for s in range(2))
                    pe.matmul(o, xh, rwT[:, 0, c, :], start=(c == 0), stop=False)
                    pe.matmul(o, xh, rwT[:, 1, c, :], start=False, stop=False)
                    last = pe.matmul(o, xl, rwT[:, 0, c, :], start=False, stop=(c == KD - 1))
            last.then_inc(s_lg, 1)

        def shared_up(b, q):
            n = SC * b + q
            if n == 0:
                pe.wait_ge(s_wloD, EARLY)
            if q == 0:
                pe.wait_ge(s_xT, TB * (b + 1))
            if q >= 2:
                pe.wait_ge(s_t2, n - 1)
            elif b:
                pe.wait_ge(s_y, TB * b - 2 + 2 * q)
            for w in range(2):
                o = bank[4 + 2 * (q % 2) + w][:, :]
                for c in range(KD):
                    at = (2 * c + w) * SI + SH_ROWS[q]
                    wh, wl = W[:, SG_HI + at:SG_HI + at + P], W[:, SG_LO + at:SG_LO + at + P]
                    pe.matmul(o, wh, xT[:, 0, c, :], start=(c == 0), stop=False)
                    pe.matmul(o, wh, xT[:, 1, c, :], start=False, stop=False)
                    last = pe.matmul(o, wl, xT[:, 0, c, :], start=False, stop=(c == KD - 1))
            last.then_inc(s_gu, 1)

        def shared_down(b, t):
            if b == 0 and t == 0:
                pe.wait_ge(s_wlo, SC)
            pe.wait_ge(s_hlo, SC * (b + 1))
            o = bank[4 + t][:, :]
            pe.matmul(o, row0[:, :], sdb[:, 0, :], start=True, stop=False)
            pe.matmul(o, row0[:, :], sdb[:, 1, :], start=False, stop=False)
            for q in range(SC):
                hh, hl = (hS[:, s, q, t * P:(t + 1) * P] for s in range(2))
                wh, wl = W[:, SD_HI + q * D:SD_HI + (q + 1) * D], W[:, SD_LO + q * D:SD_LO + (q + 1) * D]
                pe.matmul(o, hh, wh, start=False, stop=False)
                pe.matmul(o, hh, wl, start=False, stop=False)
                last = pe.matmul(o, hl, wh, start=False, stop=(q == SC - 1))
            last.then_inc(s_yps, 1)

        def rank():
            pe.wait_ge(s_sel, 1)
            pe.wait_ge(s_const, N_CONST)
            pe.matmul(bank[2][:, 0:NT * E], upper, selsum, start=True, stop=False)
            for g in range(NT - 1):
                k = NT - 1 - g
                pe.matmul(bank[2][:, (g + 1) * E:NT * E].rearrange("p (g e) -> p g e", g=k), ones16,
                          selsum[:, g * E:(g + 1) * E].rearrange("p (g e) -> p g e", g=1).to_broadcast([P, k, E]),
                          start=False, stop=(g == NT - 2))
            for g in range(NT):
                last = pe.matmul(bank[3][:, 0:E], ones16, selsum[:, g * E:(g + 1) * E], start=(g == 0), stop=(g == NT - 1))
            last.then_inc(s_rank, 1)

        def table(n0, n1):
            for n in range(n0, n1):
                pe.wait_ge(s_oneh, n + 1)
                if n == 0:
                    pe.wait_ge(s_lgc, NB)
                pe.matmul(bank[0][:, 0:2 * BLOCKS], oneh[:, n % RING, :],
                          valh[:, n % RING, :, :].rearrange("p k b -> p (k b)"),
                          start=(n == 0), stop=(n == 2 * NT - 1)).then_inc(s_tabp, 1)

        context_T(0)
        proj(0)
        for t in range(TB):
            scores(0, t)
        transpose_router()
        for b in range(NB):
            if b:
                for q in range(SC):
                    shared_up(b - 1, q)
                    if b + 1 < NB and q == CONTEXT_AT - 1:
                        context_T(b + 1)
                    if b + 1 < NB and q == PROJ_AT - 1:
                        proj(b + 1)
            else:
                context_T(1)
                proj(1)
            if b:
                shared_down(b - 1, 0)
            for t in range(TB):
                transpose_A(b, t)
            if b:
                shared_down(b - 1, 1)
            if b + 1 < NB:
                for t in range(TB):
                    scores(b + 1, t)
            if b:
                shared_down(b - 1, 2)
            transpose_xn(b, 0)
            transpose_xn(b, 1)
            if b:
                shared_down(b - 1, 3)
            transpose_xn(b, 2)
            transpose_xn(b, 3)
            logits(b)
        for q in range(SC):
            shared_up(NB - 1, q)
            if q == 0:
                rank()
            if q >= SC - 2:
                table(*TABLE_AT[q - (SC - 2)])
        for t in range(TB):
            shared_down(NB - 1, t)
            if t < TB - 1:
                table(*TABLE_AT[2 + t])

        def routed_x(j, m, p):
            pe.wait_ge(d_xg[p], 16 * (m + 1))
            if isinstance(j, int) and j == 0:
                pe.wait_ge(s_route, 1)
            else:
                pe.wait_ge(s_x2, j)
            o = bank[0][:, :].bitcast(F16)
            for c in range(2 * KD):
                last = pe.transpose(o[:, c * P:(c + 1) * P], xg[p][:, c * P:(c + 1) * P], ident16[:, :])
            last.then_inc(s_x2ps, 1)

        def routed_up(j, p, at):
            pe.wait_ge(s_x2, j + 1)
            if not (isinstance(j, int) and j < 2):
                pe.wait_ge(s_h2, j - 1)
            elif j == 0:
                pe.wait_ge(s_y, NT)
            og, ou = bank[4 + 2 * p][:, 0:I], bank[5 + 2 * p][:, 0:I]
            for c in range(KD):
                hi, lo = at + (GU_HI + c * GU), at + (GU_LO + c * GU)
                xh, xl = xT2[:, p, 0, c, :], xT2[:, p, 1, c, :]
                f, z = c == 0, c == KD - 1
                pe.matmul(og, xh, W[:, bass.ds(hi, I)], start=f, stop=False)
                pe.matmul(ou, xh, W[:, bass.ds(hi + I, I)], start=f, stop=False)
                pe.matmul(og, xh, W[:, bass.ds(lo, I)], start=False, stop=False)
                pe.matmul(ou, xh, W[:, bass.ds(lo + I, I)], start=False, stop=False)
                pe.matmul(og, xl, W[:, bass.ds(hi, I)], start=False, stop=z)
                last = pe.matmul(ou, xl, W[:, bass.ds(hi + I, I)], start=False, stop=z)
            last.then_inc(s_gu2, 1)

        def routed_hT(j, p):
            pe.wait_ge(s_h2, j + 1)
            if not (isinstance(j, int) and j == 0):
                pe.wait_ge(s_h2lo, j)
            for c in range(DC):
                last = pe.transpose(bank[1][:, c * P:(c + 1) * P], h2[:, p, DOWN_ROWS[c]:DOWN_ROWS[c] + P], ident[:, :])
            last.then_inc(s_h2ps, 1)

        def routed_down(j, p, at):
            pe.wait_ge(s_h2lo, j + 1)
            if not (isinstance(j, int) and j < 2):
                pe.wait_ge(s_y2, j - 1)
            o = bank[2 + p][:, :]
            for c in range(DC):
                hh, hl = hT2[:, 0, c, p, :], hT2[:, 1, c, p, :]
                wh, wl = W[:, bass.ds(at + (DN_HI + c * D), D)], W[:, bass.ds(at + (DN_LO + c * D), D)]
                pe.matmul(o, hh, wh, start=(c == 0), stop=False)
                pe.matmul(o, hh, wl, start=False, stop=False)
                last = pe.matmul(o, hl, wh, start=False, stop=(c == DC - 1))
            last.then_inc(s_y2ps, 1)

        def where(j):
            return pe.value_load(wbase[0:1, bass.ds(j, 1)], min_val=0, max_val=(E - 1) * EW)

        def step(j, m, p, fetch=True):
            first_block = isinstance(j, int) and j == 0
            if not first_block:
                routed_hT(j - 1, 1 - p)
            if first_block or not (isinstance(j, int) and j == BLOCKS - 1):
                routed_x(j + 1, m + (1 if p else 0), 1 - p)
            at = where(j)
            if isinstance(j, int) and j < HEAD_BLOCKS:
                pe.wait_ge(s_ready, pe.value_load(need[0:1, j:j + 1], min_val=1, max_val=2))
            routed_up(j, p, at)
            if not first_block:
                routed_down(j - 1, 1 - p, where(j - 1))
            if isinstance(j, int) and j == HEAD_BLOCKS - 1:
                pe.wait_ge(s_ready, 3)

        routed_x(0, 0, 0)

        def finish(j):
            routed_hT(j, j % 2)
            routed_down(j, j % 2, where(j))

        run_blocks(pe, used, step, finish)

    @block.vector
    def _(dve):
        chain = [0]

        def link(ins):
            chain[0] += 1
            ins.then_inc(s_chain, 1)
            dve.wait_ge(s_chain, chain[0])

        dve.memset(xn[:, 0, :], 0.0).then_inc(s_zero, 1)
        dve.memset(sdb[:, :, :], 0.0).then_inc(s_zero, 1)

        def weight_lo(n):
            src, hi, lo, cols, zero = UNITS[n]
            if n < EARLY:
                dve.wait_ge(s_ehi, n + 1)
            else:
                dve.wait_ge(s_whi, n - EARLY + 1)
            last = dve.scalar_tensor_tensor(W[:, lo:lo + cols], staged(n)[0], WS, W[:, hi:hi + cols], ALU.mult, ALU.subtract)
            if zero:
                link(last)
                link(dve.memset(W[0:zero, hi:hi + cols], 0.0))
                last = dve.memset(W[0:zero, lo:lo + cols], 0.0)
            last.then_inc(s_wloD, 1)

        for n in range(4):
            weight_lo(n)
        dve.wait_ge(d_in, 16 * (3 + 2 * SC))
        dve.wait_ge(s_wTc, 4)
        dve.scalar_tensor_tensor(rwT[:, 1, :, :], bank[2][:, 0:KD * E].rearrange("p (c e) -> p c e", c=KD), WS,
                                 rwT[:, 0, :, :], ALU.mult, ALU.subtract)
        dve.scalar_tensor_tensor(sdb[0:1, 1, :], ysh[0:1, 1, :], HW, sdb[0:1, 0, :], ALU.mult, ALU.subtract).then_inc(s_rw, 1)
        dve.tensor_scalar(biasS[:, :, :], bias[:, :, :], XW, None, ALU.mult)
        dve.wait_ge(s_gam, 1)
        dve.wait_ge(s_const, 5)
        dve.tensor_scalar(gam[:, 2:3], gam[:, 1:2], -1.0, 1.0, ALU.mult, ALU.add)
        link(dve.tensor_scalar(gam[:, 3:4], gam[:, 1:2], 0.5, None, ALU.mult))

        def variance(src, n, eps, wait=True):
            for t in range(TB):
                last = dve.bn_stats(stats[:, t, :], src[:, t, :])
            link(last)
            for t in range(TB):
                last = dve.bn_aggr(mv[:, t, :], stats[:, t, :])
            link(last)
            dve.tensor_scalar(pw[:, 0, :], mv[:, :, 1], eps, None, ALU.add).then_inc(s_var, 1)
            if wait:
                dve.wait_ge(s_rstd, n + 1)

        def threshold_start(b):
            dve.wait_ge(s_simc, TB * (b + 1))
            variance(sim, 3 * b, 1e-30)
            link(dve.tensor_tensor(dif[:, 0, :], mv[:, :, 1], rstd[:, :], ALU.mult))
            dve.scalar_tensor_tensor(probe[:, 0, :], dif[:, 0, :], START_Z, mv[:, :, 0], ALU.mult, ALU.add)
            dve.scalar_tensor_tensor(lo_[:, 0, :], dif[:, 0, :], -SPAN_Z, mv[:, :, 0], ALU.mult, ALU.add)
            dve.scalar_tensor_tensor(hi_[:, 0, :], dif[:, 0, :], SPAN_Z, mv[:, :, 0], ALU.mult, ALU.add)
            dve.memset(lo_[:, 1, :], float(S))
            dve.memset(hi_[:, 1, 0:TB - ACT_TILES], 0.0)
            link(dve.memset(hi_[:, 1, TB - ACT_TILES:TB], -float(S)))
            dve.tensor_scalar(nprobe[:, :], probe[:, 0, :], -1.0, None, ALU.mult).then_inc(s_probe, 1)

        def threshold_probe(b, it):
            for t in range(TB - ACT_TILES):
                last = dve.tensor_scalar(above[:, t, :], sim[:, t, :], probe[:, 0, t:t + 1], None, ALU.is_ge, ALU.add,
                                         accum_out=probe[:, 1, t:t + 1])
            link(last)
            dve.wait_ge(s_cnt, ACT_TILES * (PROBES * b + it + 1))
            dve.tensor_tensor(msk[:, 0, :], probe[:, 1, :], target[:, :], ALU.is_ge)
            link(dve.tensor_tensor(msk[:, 1, :], probe[:, 1, :], target[:, :], ALU.is_lt))
            for k, end in enumerate((lo_, hi_)):
                for w in range(2):
                    last = dve.copy_predicated(end[:, w, :], msk[:, k, :].bitcast(U32), probe[:, w, :])
            link(last)
            if it < PROBES - 1:
                dve.tensor_tensor(over[:, :], lo_[:, 1, :], target[:, :], ALU.subtract)
                link(dve.tensor_tensor(dif[:, :, :], lo_[:, :, :], hi_[:, :, :], ALU.subtract))
                dve.reciprocal(dif[:, 1, :], dif[:, 1, :])
                link(dve.tensor_tensor(dif[:, 0, :], dif[:, 0, :], over[:, :], ALU.mult))
                link(dve.tensor_tensor(dif[:, 0, :], dif[:, 0, :], dif[:, 1, :], ALU.mult))
                dve.tensor_tensor(nprobe[:, :], dif[:, 0, :], lo_[:, 0, :], ALU.subtract)
                dve.tensor_tensor(probe[:, 0, :], lo_[:, 0, :], dif[:, 0, :], ALU.subtract).then_inc(s_probe, 1)
                dve.wait_ge(s_probe, PROBES * b + it + 2)

        def threshold_end(b):
            for end in (lo_, hi_):
                acts = end[:, 1, TB - ACT_TILES:TB]
                last = dve.tensor_scalar(acts, acts, 0.5, S / 2, ALU.mult, ALU.add)
            link(last)
            link(dve.tensor_scalar(msk[:, 0, :], lo_[:, 1, :], float(KTH - 1), None, ALU.is_le))
            for w in range(2):
                last = dve.copy_predicated(hi_[:, w, :], msk[:, 0, :].bitcast(U32), lo_[:, w, :])
            link(last)
            for t in range(TB):
                threshold_below(t)
                if b and t in (0, 2):
                    shared_hidden(b - 1, SC - 2 + t // 2, False)
            link(dve.tensor_scalar(dif[:, 0, :], hi_[:, 1, :], -1.0, float(KTH), ALU.mult, ALU.add))
            dve.tensor_scalar(msk[:, 0, :], hi_[:, 1, :], float(KTH - WIN), None, ALU.is_lt)
            link(dve.tensor_scalar(msk[:, 1, :], hi_[:, 1, :], float(KTH - 1), None, ALU.is_gt))
            dve.tensor_reduce(bad[:, 0:1], msk[:, :, :].rearrange("p k t -> p (k t)"), AX.X, ALU.max).then_inc(s_bad, 1)
            for t in range(TB):
                last = dve.scalar_tensor_tensor(pick[:, t, :], rank8[:, :], dif[:, 0, t:t + 1], top[:, t, :], ALU.is_equal, ALU.mult)
            link(last)
            link(dve.tensor_reduce(thr[:, :], pick[:, :, :], AX.X, ALU.add))

        def threshold_below(t):
            if t < TB - ACT_TILES:
                link(dve.tensor_scalar(below[:, :], sim[:, t, :], hi_[:, 0, t:t + 1], -3e38, ALU.is_ge, ALU.mult))
                link(dve.tensor_tensor(below[:, :], below[:, :], sim[:, t, :], ALU.add))
            else:
                link(dve.tensor_scalar(below[:, :], sim[:, t, :], hi_[:, 0, t:t + 1], None, ALU.is_ge, ALU.add,
                                       accum_out=hi_[:, 1, t:t + 1]))
                link(dve.scalar_tensor_tensor(below[:, :], below[:, :], -3e38, sim[:, t, :], ALU.mult, ALU.add))
            link(dve.max(top[:, t, :], below[:, :]))

        def threshold_check(b):
            dve.wait_ge(s_badr, b + 1)
            link(dve.tensor_copy(badi[:, :], bad[:, 1:2]))
            missed = dve.value_load(badi[0:1, 0:1], min_val=0, max_val=1)
            rounds = KTH // 8
            per_tile = 1 + 2 * rounds + 1
            with dve.If(missed > 0):
                for t in range(TB):
                    at = (TB * b + t) * per_tile
                    dve.tensor_copy(below[:, :], sim[:, t, :]).then_inc(s_fall, 1)
                    dve.wait_ge(s_fall, at + 1)
                    with dve.Fori(0, rounds) as r:
                        dve.max(top[:, t, :], below[:, :]).then_inc(s_fall, 1)
                        dve.wait_ge(s_fall, 2 * r + (at + 2))
                        dve.sem_inc(s_held, 1)
                        dve.match_replace(below[:, :], top[:, t, :], below[:, :], -3e38).then_inc(s_fall, 1)
                        dve.wait_ge(s_fall, 2 * r + (at + 3))
                    dve.max(top[:, t, :], below[:, :]).then_inc(s_fall, 1)
                    dve.wait_ge(s_fall, at + per_tile)
                    dve.tensor_copy(thr[:, t:t + 1], top[:, t, KTH - 8 * rounds - 1:KTH - 8 * rounds])
            with dve.Else():
                dve.sem_inc(s_fall, TB * per_tile)
            dve.wait_ge(s_fall, (b + 1) * TB * per_tile)

        def layer_norm_x(b):
            dve.wait_ge(s_rstd, 3 * b + 2)
            link(dve.tensor_scalar(aff[:, 0, :], rstd[:, :], gam[:, 2:3], None, ALU.mult))
            link(dve.scalar_tensor_tensor(aff[:, 1, :], mv[:, :, 0], -1.0, aff[:, 0, :], ALU.mult, ALU.mult))
            dve.tensor_scalar(aff[:, 0, :], aff[:, 0, :], 1.0, None, ALU.add).then_inc(s_aff, 1)

        def mask(b):
            for t in range(TB):
                g = TB * b + t
                dve.wait_ge(s_sigA, g + 1)
                dve.scalar_tensor_tensor(sim[:, t, :], sim[:, t, :], thr[:, t:t + 1], sigA[:, t % 2, :], ALU.is_ge,
                                         ALU.mult).then_inc(s_A, 1)

        def residual(b):
            dve.wait_ge(s_A, TB * (b + 1))
            dve.wait_ge(s_xa, TB * (b + 1))
            for t in range(TB):
                last = dve.scalar_tensor_tensor(xb[:, t, :], sim[:, t, :], gam[:, 3:4], xb[:, t, :], ALU.mult, ALU.add)
            link(last)
            for t in range(TB):
                g = TB * b + t
                dve.wait_ge(s_AT, g + 1)
                dve.scalar_tensor_tensor(xb[:, t, :], bank[AT_BANK[t]][:, :], gam[:, 3:4], xb[:, t, :], ALU.mult,
                                         ALU.add).then_inc(s_x1, 1)
            dve.wait_ge(s_x1, TB * (b + 1))

        def normalise(b):
            variance(xb, 3 * b + 2, EPS)
            link(dve.tensor_scalar(rstd[:, :], rstd[:, :], XS, None, ALU.mult))
            link(dve.scalar_tensor_tensor(aff[:, 1, :], mv[:, :, 0], -1.0, rstd[:, :], ALU.mult, ALU.mult))
            dve.wait_ge(d_x1, 16 * TB * (b + 1))
            for t in range(TB):
                dve.tensor_scalar(xb[:, t, :], xb[:, t, :], rstd[:, t:t + 1], aff[:, 1, t:t + 1], ALU.mult,
                                  ALU.add).then_inc(s_xn, 1)

        def largest_logits(b):
            dve.wait_ge(s_lg, b + 1)
            tiles = slice(TB * b, TB * (b + 1))
            dve.tensor_copy(lg[:, tiles, :], bank[0][:, 0:TB * E].rearrange("p (t e) -> p t e", t=TB)).then_inc(s_lgc, 1)
            dve.wait_ge(s_lgc, b + 1)
            for g in range(TB * b, TB * (b + 1)):
                last = dve.max(mx[:, g, :], lg[:, g, :])
            link(last)
            for g in range(TB * b, TB * (b + 1)):
                last = dve.max_index(mxi[:, g, :], mx[:, g, :], lg[:, g, :])
            link(last)

        def shared_lo(b, q):
            n = SC * b + q
            dve.wait_ge(s_hhi, n + 1)
            dve.scalar_tensor_tensor(hS[:, 1, q, :], sgt[:, q % 2, :], HS / XW, hS[:, 0, q, :], ALU.mult,
                                     ALU.subtract).then_inc(s_hlo, 1)

        def shared_hidden(b, q, last_lo=True):
            n = SC * b + q
            if q:
                shared_lo(b, q - 1)
            dve.wait_ge(s_sg, n + 1)
            dve.scalar_tensor_tensor(sgt[:, q % 2, :], bank[5 + 2 * (q % 2)][:, :], biasS[:, 1, q:q + 1], sgt[:, q % 2, :],
                                     ALU.add, ALU.mult).then_inc(s_t2, 1)
            if q == SC - 1 and last_lo:
                shared_lo(b, q)

        for b in range(NB):
            threshold_start(b)
            for it in range(PROBES):
                threshold_probe(b, it)
                if b == 0 and it < 2:
                    for n in (2 * it + 4, 2 * it + 5):
                        weight_lo(n)
                if it == 1:
                    dve.wait_ge(d_x, 16 * (b + 1))
                    variance(xb, 3 * b + 1, EPS, False)
                if b and it:
                    shared_hidden(b - 1, it - 1)
                if b and it == 1:
                    largest_logits(b - 1)
                if it == 2:
                    layer_norm_x(b)
            threshold_end(b)
            if b:
                shared_lo(b - 1, SC - 1)
            threshold_check(b)
            mask(b)
            residual(b)
            normalise(b)
        largest_logits(NB - 1)

        last_b = NB - 1
        dve.tensor_copy(ef, mxi[:, :, 0:2].rearrange("p g k -> p k g"))
        dve.tensor_tensor(wt[:, 1, :], mx[:, :, 0], mx[:, :, 1], ALU.subtract).then_inc(s_top2, 1)
        dve.wait_ge(s_top2, 1)
        dve.wait_ge(s_const, N_CONST)
        for k in range(2):
            last = dve.tensor_tensor(sel[:, k, :, :], ef[:, k, :].rearrange("p (g o) -> p g o", o=1).to_broadcast([P, NT, E]),
                                     io8.rearrange("p (o e) -> p o e", o=1).to_broadcast([P, NT, E]), ALU.is_equal)
        link(last)
        dve.tensor_tensor(selsum.rearrange("p (g e) -> p g e", g=NT), sel[:, 0, :, :], sel[:, 1, :, :], ALU.add).then_inc(s_sel, 1)
        shared_hidden(last_b, 0)
        dve.wait_ge(s_rank, 1)
        link(dve.tensor_copy(cnt, bank[3][:, 0:E]))
        link(dve.tensor_tensor(cmp16, cnt.rearrange("p (e o) -> p e o", o=1).to_broadcast([P, E, 16]),
                               k128.rearrange("p (o k) -> p o k", o=1).to_broadcast([P, E, 16]), ALU.is_gt))
        link(dve.tensor_reduce(nblk, cmp16, AX.X, ALU.add))
        link(dve.tensor_tensor_scan(ends, one8, nblk, 0.0, ALU.mult, ALU.add))
        link(dve.tensor_tensor(first, ends, nblk, ALU.subtract))
        link(dve.scalar_tensor_tensor(slotr, first.rearrange("p (o e) -> p o e", o=1).to_broadcast([P, NT, E]), float(P),
                                      bank[2][:, 0:NT * E].rearrange("p (g e) -> p g e", g=NT), ALU.mult, ALU.add))
        shared_hidden(last_b, 1)
        for k in range(2):
            last = dve.tensor_tensor(prod[:, k, :, :], sel[:, k, :, :], slotr, ALU.mult)
        link(last)
        link(dve.tensor_reduce(pos, prod, AX.X, ALU.add))
        link(dve.tensor_copy(posi, pos.rearrange("p k g -> p (k g)")))
        dve.tensor_scalar(lowi, posi, P - 1, None, ALU.bitwise_and)
        link(dve.tensor_scalar(higi, posi, P.bit_length() - 1, None, ALU.logical_shift_right))
        dve.tensor_copy(lowf.rearrange("p k g -> p (k g)"), lowi)
        link(dve.tensor_copy(higf.rearrange("p k g -> p (k g)"), higi))
        shared_hidden(last_b, 2)
        link(dve.tensor_tensor(blkc, iota[:, 0:BLOCKS].rearrange("p (j o) -> p j o", o=1).to_broadcast([P, BLOCKS, E]),
                               ends.rearrange("p (o e) -> p o e", o=1).to_broadcast([P, BLOCKS, E]), ALU.is_ge))
        link(dve.tensor_reduce(base_f, blkc, AX.X, ALU.add))
        dve.tensor_copy(need_f[:, HEAD_BLOCKS:HEAD_BLOCKS + 1], ends[:, E - 1:E])
        link(dve.tensor_scalar(need_f[:, 0:HEAD_BLOCKS], base_f[:, 0:HEAD_BLOCKS], float(E - 1), None, ALU.min))
        link(dve.tensor_scalar(base_f, base_f, float(E - 1), float(EW), ALU.min, ALU.mult))
        link(dve.tensor_scalar(need_f[:, 0:HEAD_BLOCKS], need_f[:, 0:HEAD_BLOCKS], -float(E - 4), 1.0, ALU.add, ALU.max))
        dve.tensor_copy(need_used[:, :], need_f)
        dve.tensor_copy(wbase[:, :], base_f)
        shared_hidden(last_b, 3)
        dve.wait_ge(s_wt, 2)
        for n in range(2 * NT):
            g, k = n // 2, n % 2
            if n >= RING:
                dve.wait_ge(s_tabp, n - RING + 1)
            dve.tensor_scalar(oneh[:, n % RING, :], iota, lowf[:, k, g:g + 1], None, ALU.is_equal)
            dve.tensor_scalar(valh[:, n % RING, 0, :], iota[:, 0:BLOCKS], higf[:, k, g:g + 1], tok1[:, g:g + 1], ALU.is_equal, ALU.mult)
            dve.tensor_scalar(valh[:, n % RING, 1, :], iota[:, 0:BLOCKS], higf[:, k, g:g + 1], wt[:, k, g:g + 1], ALU.is_equal,
                              ALU.mult).then_inc(s_oneh, 1)
            if n + 1 in HIDDEN_AT:
                shared_hidden(last_b, HIDDEN_AT[n + 1])
        dve.wait_ge(s_tabp, 2 * NT)
        link(dve.tensor_copy(tab, bank[0][:, 0:2 * BLOCKS].rearrange("p (k j) -> p k j", k=2)))
        link(dve.tensor_scalar(zer, tab[:, 0, :], 0.0, dumf, ALU.is_equal, ALU.mult))
        dve.tensor_scalar(wcol[:, :], tab[:, 1, :], 1.0 / HW, None, ALU.mult)
        dve.scalar_tensor_tensor(idx[:, :], tab[:, 0, :], -1.0, zer, ALU.add, ALU.add).then_inc(s_route, 1)

        def routed_x(j, p):
            dve.wait_ge(s_x2ps, j + 1)
            if not (isinstance(j, int) and j < 2):
                dve.wait_ge(s_gu2, j - 1)
            dve.tensor_copy(xT2[:, p, :, :, :].rearrange("p s c t -> p (s c t)").bitcast(F32), bank[0][:, :]).then_inc(s_x2, 1)

        def routed_hidden(j, p):
            dve.wait_ge(s_sig2, j + 1)
            if not (isinstance(j, int) and j < 2):
                dve.wait_ge(s_h2ps, j - 1)
            dve.scalar_tensor_tensor(h2[:, p, :], bank[5 + 2 * p][:, 0:I], HS / XW, sg2[:, p, :], ALU.mult,
                                     ALU.mult).then_inc(s_h2, 1)

        def routed_h(j, p):
            dve.wait_ge(s_h2hi, j + 1)
            dve.tensor_tensor(hT2[:, 1, :, p, :], bank[1][:, 0:DC * P].rearrange("p (c t) -> p c t", c=DC),
                              hT2[:, 0, :, p, :], ALU.subtract).then_inc(s_h2lo, 1)

        def step(j, m, p, fetch=True):
            first_block = isinstance(j, int) and j == 0
            if not first_block:
                routed_h(j - 1, 1 - p)
            if first_block or not (isinstance(j, int) and j == BLOCKS - 1):
                routed_x(j + 1, 1 - p)
            routed_hidden(j, p)
            if isinstance(j, int) and j < HEAD_BLOCKS:
                last_expert(LAST_AT[j + 1])

        last_units = iter(range(LAST, len(UNITS)))

        def last_expert(k):
            for _ in range(k):
                n = next(last_units)
                weight_lo(n)
                if n == len(UNITS) - 1:
                    dve.wait_ge(s_wloD, EARLY + PER_EXPERT)
                    dve.sem_inc(s_ready, 1)

        routed_x(0, 0)
        last_expert(LAST_AT[0])

        def finish(j):
            routed_h(j, j % 2)

        run_blocks(dve, used, step, finish)

    es.close()


def run_blocks(eng, used, step, finish):
    for j in range(HEAD_BLOCKS):
        step(j, j // 2, j % 2)
    with eng.Fori(0, (SURE - HEAD_BLOCKS) // 2) as i:
        step(2 * i + HEAD_BLOCKS, i + HEAD_BLOCKS // 2, 1)
        step(2 * i + (HEAD_BLOCKS + 1), i + (HEAD_BLOCKS // 2 + 1), 0)
    rest(eng, eng.value_load(used, min_val=0, max_val=BLOCKS), SURE, step, finish)


def rest(eng, used, j, step, finish):
    if j == BLOCKS:
        finish(j - 1)
        return
    with eng.If(used > j):
        step(j, j // 2, j % 2, fetch=j + 2 < BLOCKS)
        step(j + 1, (j + 1) // 2, (j + 1) % 2, fetch=j + 2 < BLOCKS)
        rest(eng, used, j + 2, step, finish)
    with eng.Else():
        finish(j - 1)


def kernel(**inputs):
    import numpy as np
    import concourse.bacc as bacc
    from concourse.bass_utils import run_bass_kernel_spmd

    nc = bacc.Bacc("TRN2", target_bir_lowering=False, num_devices=1)
    shapes = {
        "x": (NB, S, D), "ctx_512": (NB, S, C), "L0_xattn_Wq": (C, C), "L0_xattn_Wk": (C, C),
        "L0_xattn_gamma_raw": (1, 1), "L0_ffn_router_w": (E, D), "L0_ffn_gate_w": (E, D, I), "L0_ffn_up_w": (E, D, I),
        "L0_ffn_down_w": (E, I, D), "L0_ffn_s_gate_w": (D, SI), "L0_ffn_s_gate_b": (SI, 1), "L0_ffn_s_up_w": (D, SI),
        "L0_ffn_s_up_b": (SI, 1), "L0_ffn_s_down_w": (SI, D), "L0_ffn_s_down_b": (1, D),
    }
    arrays, args = {}, []
    for name, shape in shapes.items():
        arrays[name + "_in"] = np.ascontiguousarray(inputs[name]).reshape(shape)
        args.append(nc.dram_tensor(name + "_in", shape, F32, kind="ExternalInput").ap())
    out = nc.dram_tensor("out_dram", (T + P, D), F32, kind="ExternalOutput").ap()
    xn_dram = nc.dram_tensor("xn_dram", (T + P, 2 * D), mybir.dt.float16, kind="Internal").ap()
    build(nc, *args, out, xn_dram)
    r = run_bass_kernel_spmd(nc, [arrays], core_ids=[0])
    return r.results[0]["out_dram"][:T].reshape(NB, S, D)
```
